# Optimizing a Trainium2 kernel written in Bass

```python
import numpy as np
import jax
import jax.numpy as jnp

def _softmax(x, axis=-1):
    return jax.nn.softmax(x, axis=axis)

def _gelu(x):
    return jax.nn.gelu(x, approximate=True)

def _silu(x):
    return jax.nn.silu(x)

def _sigmoid(x):
    return jax.nn.sigmoid(x)

def _layernorm(x, axis=-1, eps=1e-05):
    m = jnp.mean(x, axis=axis, keepdims=True)
    v = jnp.var(x, axis=axis, keepdims=True)
    return (x - m) / jnp.sqrt(v + eps)

def _scatter_add(tgt, idx, src, axis=0):
    return tgt.at[idx].add(src)

def _segment_sum(src, seg, n):
    return jax.ops.segment_sum(src, seg, n)
kernel_name = 'mk_macaron_d2_jaxref_r8_1c71b8'

def setup_inputs(seed: int=0):
    np.random.seed(seed)
    _w = jnp.asarray

    def _L0_attn_setup():
        import jax, jax.numpy as jnp
        import numpy as np
        MODEL_DIM = 128
        NUM_HEADS = 16
        D_K = MODEL_DIM // NUM_HEADS
        MAX_SEQ_LEN = 512

        def _xavier(key, shape):
            fan_in, fan_out = (shape[1], shape[0])
            limit = np.sqrt(6.0 / (fan_in + fan_out)).astype(np.float32)
            return jax.random.uniform(key, shape, jnp.float32, -limit, limit)
        key = jax.random.key(seed)
        ks = jax.random.split(key, 6)
        x = jax.random.normal(ks[0], (2, 256, MODEL_DIM), jnp.float32)
        wq = _xavier(ks[1], (MODEL_DIM, MODEL_DIM))
        wk = _xavier(ks[2], (MODEL_DIM, MODEL_DIM))
        wv = _xavier(ks[3], (MODEL_DIM, MODEL_DIM))
        wo = _xavier(ks[4], (MODEL_DIM, MODEL_DIM))
        bq = jnp.zeros((MODEL_DIM,), jnp.float32)
        bk = jnp.zeros((MODEL_DIM,), jnp.float32)
        bv = jnp.zeros((MODEL_DIM,), jnp.float32)
        bo = jnp.zeros((MODEL_DIM,), jnp.float32)
        half = D_K // 2
        theta = jnp.power(10000.0, jnp.arange(half, dtype=jnp.float32) * (-2.0 / D_K))
        angles = jnp.arange(MAX_SEQ_LEN, dtype=jnp.float32)[:, None] * theta[None, :]
        rot_cos = jnp.cos(angles)
        rot_sin = jnp.sin(angles)
        return {'x': x, 'wq': wq, 'bq': bq, 'wk': wk, 'bk': bk, 'wv': wv, 'bv': bv, 'wo': wo, 'bo': bo, 'rot_cos': rot_cos, 'rot_sin': rot_sin}
    _L0_attn_in = _L0_attn_setup()

    def _L0_ffn_setup():
        import jax, jax.numpy as jnp
        import numpy as np
        import math
        D_IN = 128
        FEATURES = (512, 512, 128)
        BATCH, SEQ = (8, 256)

        def _conn_dense(kernel_bool, x):
            w = jnp.where(kernel_bool, jnp.float32(1.0), jnp.float32(-1.0))
            return x @ w
        key = jax.random.key(seed)
        kx, kk0, kk1, kk2 = jax.random.split(key, 4)
        x = jax.random.normal(kx, (BATCH, SEQ, D_IN), dtype=jnp.float32)
        k0 = jax.random.randint(kk0, (2 * D_IN, FEATURES[0]), 0, 2).astype(jnp.bool_)
        k1 = jax.random.randint(kk1, (FEATURES[0], FEATURES[1]), 0, 2).astype(jnp.bool_)
        k2 = jax.random.randint(kk2, (FEATURES[1], FEATURES[2]), 0, 2).astype(jnp.bool_)
        s0 = jnp.asarray(1.0 / math.sqrt(2 * D_IN), dtype=jnp.float32)
        s1 = jnp.asarray(1.0 / math.sqrt(FEATURES[0]), dtype=jnp.float32)
        s2 = jnp.asarray(1.0 / math.sqrt(FEATURES[1]), dtype=jnp.float32)
        return {'x': x, 'k0': k0, 'k1': k1, 'k2': k2, 's0': s0, 's1': s1, 's2': s2}
    _L0_ffn_in = _L0_ffn_setup()

    def _L1_attn_setup():
        import jax, jax.numpy as jnp
        import numpy as np
        C = 64
        key = jax.random.key(seed)
        k1, k2, k3, k4, k5 = jax.random.split(key, 5)
        B, T, D, H = (4, 512, 128, 8)
        out = jax.random.normal(k1, (B, T, D), jnp.float32)
        W_write = jax.random.normal(k2, (D, D), jnp.float32) * 0.02
        W_read = jax.random.normal(k3, (D, D), jnp.float32) * 0.02
        W_beta = jax.random.normal(k4, (H, D), jnp.float32) * 0.02
        decay = 4.6 + jax.random.normal(k5, (H,), jnp.float32) * 0.1
        return {'out': out, 'W_write': W_write, 'W_read': W_read, 'W_beta': W_beta, 'decay': decay}
    _L1_attn_in = _L1_attn_setup()

    def _L1_ffn_setup():
        import jax, jax.numpy as jnp
        import numpy as np
        DIM = 128
        DEPTH = 6
        HEADS = 16
        DIM_HEAD = 64
        WINDOW = 32
        INNER = HEADS * DIM_HEAD
        DIM_INNER = int(DIM * 4 * 2 / 3)
        QK_SCALE = 8.0

        def shift_tokens(t):
            a, s = jnp.split(t, 2, -1)
            s = jnp.pad(s, ((0, 0), (1, 0), (0, 0)))[:, :-1]
            return jnp.concatenate([a, s], -1)

        def l2norm(t):
            return t / jnp.maximum(jnp.linalg.norm(t, axis=-1, keepdims=True), 1e-12)

        def rotate_half(x):
            x1, x2 = jnp.split(x, 2, -1)
            return jnp.concatenate([-x2, x1], -1)

        def rotary_tables(n):
            half = jnp.arange(0, DIM_HEAD, 2, dtype=jnp.float32)
            inv_freq = 1.0 / 10000.0 ** (half / DIM_HEAD)
            t = jnp.arange(n, dtype=jnp.float32)
            freqs = t[:, None] * inv_freq[None, :]
            freqs = jnp.concatenate([freqs, freqs], -1)
            base_scale = (half + 0.4 * DIM_HEAD) / (1.4 * DIM_HEAD)
            power = (t - n // 2) / (WINDOW // 2)
            scale = base_scale[None, :] ** power[:, None]
            scale = jnp.concatenate([scale, scale], -1)
            return (freqs, scale)

        def local_attention(q, k, v):
            b, h, n, d = q.shape
            w = WINDOW
            nw = n // w
            bq = q.reshape(b, h, nw, w, d)
            bk = k.reshape(b, h, nw, w, d)
            bv = v.reshape(b, h, nw, w, d)

            def look(t):
                p = jnp.pad(t, ((0, 0), (0, 0), (1, 0), (0, 0), (0, 0)))
                return jnp.concatenate([p[:, :, :nw], p[:, :, 1:]], axis=3)
            bk2, bv2 = (look(bk), look(bv))
            seq = jnp.arange(n).reshape(nw, w)
            seq_p = jnp.pad(seq, ((1, 0), (0, 0)), constant_values=-1)
            jt = jnp.concatenate([seq_p[:nw], seq_p[1:]], axis=1)
            it = seq[:, :, None]
            jb = jt[:, None, :]
            mask = (it < jb) | (it > jb + w) | (jb == -1)
            sim = jnp.einsum('bhwie,bhwje->bhwij', bq, bk2) * QK_SCALE
            sim = jnp.where(mask, -jnp.finfo(sim.dtype).max, sim)
            attn = jax.nn.softmax(sim, -1)
            out = jnp.einsum('bhwij,bhwje->bhwie', attn, bv2)
            return out.reshape(b, h, n, d)

        def attn_layer(x, Wqkv, qs, ksc, Wo):
            b, n, _ = x.shape
            qkv = x @ Wqkv
            q, k, v = jnp.split(qkv, 3, -1)
            sh = lambda t: t.reshape(b, n, HEADS, DIM_HEAD).transpose(0, 2, 1, 3)
            q, k, v = (sh(q), sh(k), sh(v))
            q = l2norm(q) * qs
            k = l2norm(k) * ksc
            freqs, scale = rotary_tables(n)
            cos, sin = (jnp.cos(freqs), jnp.sin(freqs))
            q = q * cos * scale + rotate_half(q) * sin * scale
            inv = 1.0 / scale
            k = k * cos * inv + rotate_half(k) * sin * inv
            out = local_attention(q, k, v)
            out = out.transpose(0, 2, 1, 3).reshape(b, n, INNER)
            return out @ Wo

        def ffn_layer(x, g, bln, W1, b1, W2, b2):
            mu = x.mean(-1, keepdims=True)
            var = ((x - mu) ** 2).mean(-1, keepdims=True)
            xn = (x - mu) / jnp.sqrt(var + 1e-05) * g + bln
            hg = xn @ W1 + b1
            a, gate = jnp.split(hg, 2, -1)
            return a * jax.nn.gelu(gate, approximate=False) @ W2 + b2
        key = jax.random.key(seed)
        ks = jax.random.split(key, 8)
        B, N = (2, 256)
        init = lambda k, shape: jax.random.normal(k, shape, jnp.float32) * 0.02
        return {'x': jax.random.normal(ks[0], (B, N, DIM), jnp.float32), 'Wqkv': init(ks[1], (DEPTH, DIM, 3 * INNER)), 'q_scale': jnp.ones((DEPTH, DIM_HEAD), jnp.float32), 'k_scale': jnp.ones((DEPTH, DIM_HEAD), jnp.float32), 'Wo': init(ks[2], (DEPTH, INNER, DIM)), 'ln_g': jnp.ones((DEPTH, DIM), jnp.float32), 'ln_b': jnp.zeros((DEPTH, DIM), jnp.float32), 'W1': init(ks[3], (DEPTH, DIM, 2 * DIM_INNER)), 'b1': jnp.zeros((DEPTH, 2 * DIM_INNER), jnp.float32), 'W2': init(ks[4], (DEPTH, DIM_INNER, DIM)), 'b2': jnp.zeros((DEPTH, DIM), jnp.float32)}
    _L1_ffn_in = _L1_ffn_setup()
    _d = {'L0_attn_x': _L0_attn_in['x'], 'L0_attn_wq': _L0_attn_in['wq'], 'L0_attn_bq': _L0_attn_in['bq'], 'L0_attn_wk': _L0_attn_in['wk'], 'L0_attn_bk': _L0_attn_in['bk'], 'L0_attn_wv': _L0_attn_in['wv'], 'L0_attn_bv': _L0_attn_in['bv'], 'L0_attn_wo': _L0_attn_in['wo'], 'L0_attn_bo': _L0_attn_in['bo'], 'L0_attn_rot_cos': _L0_attn_in['rot_cos'], 'L0_attn_rot_sin': _L0_attn_in['rot_sin'], 'L0_ffn_k0': _L0_ffn_in['k0'], 'L0_ffn_k1': _L0_ffn_in['k1'], 'L0_ffn_k2': _L0_ffn_in['k2'], 'L0_ffn_s0': _L0_ffn_in['s0'], 'L0_ffn_s1': _L0_ffn_in['s1'], 'L0_ffn_s2': _L0_ffn_in['s2'], 'L1_attn_W_write': _L1_attn_in['W_write'], 'L1_attn_W_read': _L1_attn_in['W_read'], 'L1_attn_W_beta': _L1_attn_in['W_beta'], 'L1_attn_decay': _L1_attn_in['decay'], 'L1_ffn_Wqkv': _L1_ffn_in['Wqkv'], 'L1_ffn_q_scale': _L1_ffn_in['q_scale'], 'L1_ffn_k_scale': _L1_ffn_in['k_scale'], 'L1_ffn_Wo': _L1_ffn_in['Wo'], 'L1_ffn_ln_g': _L1_ffn_in['ln_g'], 'L1_ffn_ln_b': _L1_ffn_in['ln_b'], 'L1_ffn_W1': _L1_ffn_in['W1'], 'L1_ffn_b1': _L1_ffn_in['b1'], 'L1_ffn_W2': _L1_ffn_in['W2'], 'L1_ffn_b2': _L1_ffn_in['b2']}
    _x0 = _d['L0_attn_x']
    _d['L0_attn_x'] = jax.random.normal(jax.random.fold_in(jax.random.key(seed), 1), (4, 512, 128), dtype=_x0.dtype)
    del _x0
    return _d

def reference(L0_attn_x, L0_attn_wq, L0_attn_bq, L0_attn_wk, L0_attn_bk, L0_attn_wv, L0_attn_bv, L0_attn_wo, L0_attn_bo, L0_attn_rot_cos, L0_attn_rot_sin, L0_ffn_k0, L0_ffn_k1, L0_ffn_k2, L0_ffn_s0, L0_ffn_s1, L0_ffn_s2, L1_attn_W_write, L1_attn_W_read, L1_attn_W_beta, L1_attn_decay, L1_ffn_Wqkv, L1_ffn_q_scale, L1_ffn_k_scale, L1_ffn_Wo, L1_ffn_ln_g, L1_ffn_ln_b, L1_ffn_W1, L1_ffn_b1, L1_ffn_W2, L1_ffn_b2):

    def _L0_attn_ref(x, wq, bq, wk, bk, wv, bv, wo, bo, rot_cos, rot_sin):
        import jax, jax.numpy as jnp
        import numpy as np
        MODEL_DIM = 128
        NUM_HEADS = 16
        D_K = MODEL_DIM // NUM_HEADS
        MAX_SEQ_LEN = 512

        def _xavier(key, shape):
            fan_in, fan_out = (shape[1], shape[0])
            limit = np.sqrt(6.0 / (fan_in + fan_out)).astype(np.float32)
            return jax.random.uniform(key, shape, jnp.float32, -limit, limit)
        b, t, m = x.shape
        h, d = (NUM_HEADS, m // NUM_HEADS)
        q = (x @ wq.T + bq).reshape(b, h, t, d)
        k = (x @ wk.T + bk).reshape(b, h, t, d)
        v = (x @ wv.T + bv).reshape(b, h, t, d)
        c = rot_cos[t]
        s = rot_sin[t]

        def rope(u):
            ur = u.reshape(b, h, t, d // 2, 2)
            re, im = (ur[..., 0], ur[..., 1])
            return jnp.stack([re * c - im * s, re * s + im * c], axis=-1).reshape(b, h, t, d)
        q, k = (rope(q), rope(k))
        scores = jnp.einsum('bhqd,bhkd->bhqk', q, k) / np.float32(np.sqrt(d))
        p = jax.nn.softmax(scores, axis=-1)
        o = jnp.einsum('bhqk,bhkd->bhqd', p, v)
        o = o.transpose(0, 2, 1, 3).reshape(b, t, m)
        return o @ wo.T + bo

    def _L0_ffn_ref(x, k0, k1, k2, s0, s1, s2):
        import jax, jax.numpy as jnp
        import numpy as np
        import math
        D_IN = 128
        FEATURES = (512, 512, 128)
        BATCH, SEQ = (8, 256)

        def _conn_dense(kernel_bool, x):
            w = jnp.where(kernel_bool, jnp.float32(1.0), jnp.float32(-1.0))
            return x @ w
        h = jnp.concatenate([x, -x], axis=-1)
        h = s0 * _conn_dense(k0, h)
        h = jax.nn.relu(h) * 2
        h = s1 * _conn_dense(k1, h)
        h = jax.nn.relu(h) * 2
        h = s2 * _conn_dense(k2, h)
        return h

    def _L1_attn_ref(out, W_write, W_read, W_beta, decay):
        import jax, jax.numpy as jnp
        import numpy as np
        C = 64
        B, T, D = out.shape
        H = decay.shape[0]
        d = D // H
        assert T % C == 0
        N = T // C
        x = out.astype(jnp.float32)
        xh = x.reshape(B, T, H, d)
        rk = xh / jnp.maximum(jnp.linalg.norm(xh, axis=-1, keepdims=True), 1e-12)
        rk = rk.transpose(0, 2, 1, 3)
        wk = jnp.pad(rk[:, :, :-1], ((0, 0), (0, 0), (1, 0), (0, 0)))
        v = (x @ W_write.T).reshape(B, T, H, d).transpose(0, 2, 1, 3)
        beta = jax.nn.sigmoid(x @ W_beta.T).transpose(0, 2, 1)[..., None]
        v = v * beta
        wk_beta = wk * beta
        log_gamma = jnp.log(jax.nn.sigmoid(decay))
        pos = jnp.arange(C, dtype=jnp.float32)
        cum_decay = (pos + 1.0) * log_gamma[:, None]
        tril = jnp.tril(jnp.ones((C, C), jnp.float32))
        L_mask = jnp.exp((cum_decay[:, :, None] - cum_decay[:, None, :]) * tril) * tril
        decay_exp = jnp.exp(cum_decay)[:, :, None]
        chunk_total = jnp.exp(cum_decay[:, -1])[:, None, None]
        dw = jnp.exp(cum_decay[:, -1:] - cum_decay)[:, :, None]
        rk_c = rk.reshape(B, H, N, C, d)
        wk_c = wk.reshape(B, H, N, C, d)
        v_c = v.reshape(B, H, N, C, d)
        wkb_c = wk_beta.reshape(B, H, N, C, d)
        strict_lower = jnp.tril(jnp.ones((C, C), bool), -1)
        A = -(wkb_c @ jnp.swapaxes(wk_c, -1, -2)) * L_mask[None, :, None]
        A = jnp.where(strict_lower, A, 0.0)

        def ut_body(i, A):
            row = A[..., i, :]
            new_row = row + jnp.einsum('bhnj,bhnjk->bhnk', row, A)
            return A.at[..., i, :].set(new_row)
        A = jax.lax.fori_loop(1, C, ut_body, A)
        A = A + jnp.eye(C, dtype=A.dtype)
        v_c = A @ v_c
        wk_cum = A @ (wkb_c * decay_exp[None, :, None])
        causal = jnp.tril(jnp.ones((C, C), bool))
        xs = (jnp.moveaxis(rk_c, 2, 0), jnp.moveaxis(wk_c, 2, 0), jnp.moveaxis(v_c, 2, 0), jnp.moveaxis(wk_cum, 2, 0))
        S0 = jnp.zeros((B, H, d, d), jnp.float32)

        def chunk_step(S, xs_i):
            rk_i, wk_i, v_i, wkc_i = xs_i
            attn = rk_i @ jnp.swapaxes(wk_i, -1, -2) * L_mask[None]
            attn = jnp.where(causal, attn, 0.0)
            v_new = v_i - wkc_i @ S
            o_i = rk_i * decay_exp[None] @ S + attn @ v_new
            S_new = chunk_total[None] * S + jnp.swapaxes(wk_i * dw[None], -1, -2) @ v_new
            return (S_new, o_i)
        _, o = jax.lax.scan(chunk_step, S0, xs)
        o = jnp.moveaxis(o, 0, 2).reshape(B, H, T, d).transpose(0, 2, 1, 3).reshape(B, T, D)
        return out + (o @ W_read.T).astype(out.dtype)

    def _L1_ffn_ref(x, Wqkv, q_scale, k_scale, Wo, ln_g, ln_b, W1, b1, W2, b2):
        import jax, jax.numpy as jnp
        import numpy as np
        DIM = 128
        DEPTH = 6
        HEADS = 16
        DIM_HEAD = 64
        WINDOW = 32
        INNER = HEADS * DIM_HEAD
        DIM_INNER = int(DIM * 4 * 2 / 3)
        QK_SCALE = 8.0

        def shift_tokens(t):
            a, s = jnp.split(t, 2, -1)
            s = jnp.pad(s, ((0, 0), (1, 0), (0, 0)))[:, :-1]
            return jnp.concatenate([a, s], -1)

        def l2norm(t):
            return t / jnp.maximum(jnp.linalg.norm(t, axis=-1, keepdims=True), 1e-12)

        def rotate_half(x):
            x1, x2 = jnp.split(x, 2, -1)
            return jnp.concatenate([-x2, x1], -1)

        def rotary_tables(n):
            half = jnp.arange(0, DIM_HEAD, 2, dtype=jnp.float32)
            inv_freq = 1.0 / 10000.0 ** (half / DIM_HEAD)
            t = jnp.arange(n, dtype=jnp.float32)
            freqs = t[:, None] * inv_freq[None, :]
            freqs = jnp.concatenate([freqs, freqs], -1)
            base_scale = (half + 0.4 * DIM_HEAD) / (1.4 * DIM_HEAD)
            power = (t - n // 2) / (WINDOW // 2)
            scale = base_scale[None, :] ** power[:, None]
            scale = jnp.concatenate([scale, scale], -1)
            return (freqs, scale)

        def local_attention(q, k, v):
            b, h, n, d = q.shape
            w = WINDOW
            nw = n // w
            bq = q.reshape(b, h, nw, w, d)
            bk = k.reshape(b, h, nw, w, d)
            bv = v.reshape(b, h, nw, w, d)

            def look(t):
                p = jnp.pad(t, ((0, 0), (0, 0), (1, 0), (0, 0), (0, 0)))
                return jnp.concatenate([p[:, :, :nw], p[:, :, 1:]], axis=3)
            bk2, bv2 = (look(bk), look(bv))
            seq = jnp.arange(n).reshape(nw, w)
            seq_p = jnp.pad(seq, ((1, 0), (0, 0)), constant_values=-1)
            jt = jnp.concatenate([seq_p[:nw], seq_p[1:]], axis=1)
            it = seq[:, :, None]
            jb = jt[:, None, :]
            mask = (it < jb) | (it > jb + w) | (jb == -1)
            sim = jnp.einsum('bhwie,bhwje->bhwij', bq, bk2) * QK_SCALE
            sim = jnp.where(mask, -jnp.finfo(sim.dtype).max, sim)
            attn = jax.nn.softmax(sim, -1)
            out = jnp.einsum('bhwij,bhwje->bhwie', attn, bv2)
            return out.reshape(b, h, n, d)

        def attn_layer(x, Wqkv, qs, ksc, Wo):
            b, n, _ = x.shape
            qkv = x @ Wqkv
            q, k, v = jnp.split(qkv, 3, -1)
            sh = lambda t: t.reshape(b, n, HEADS, DIM_HEAD).transpose(0, 2, 1, 3)
            q, k, v = (sh(q), sh(k), sh(v))
            q = l2norm(q) * qs
            k = l2norm(k) * ksc
            freqs, scale = rotary_tables(n)
            cos, sin = (jnp.cos(freqs), jnp.sin(freqs))
            q = q * cos * scale + rotate_half(q) * sin * scale
            inv = 1.0 / scale
            k = k * cos * inv + rotate_half(k) * sin * inv
            out = local_attention(q, k, v)
            out = out.transpose(0, 2, 1, 3).reshape(b, n, INNER)
            return out @ Wo

        def ffn_layer(x, g, bln, W1, b1, W2, b2):
            mu = x.mean(-1, keepdims=True)
            var = ((x - mu) ** 2).mean(-1, keepdims=True)
            xn = (x - mu) / jnp.sqrt(var + 1e-05) * g + bln
            hg = xn @ W1 + b1
            a, gate = jnp.split(hg, 2, -1)
            return a * jax.nn.gelu(gate, approximate=False) @ W2 + b2
        for i in range(DEPTH):
            x = attn_layer(shift_tokens(x), Wqkv[i], q_scale[i], k_scale[i], Wo[i]) + x
            x = ffn_layer(shift_tokens(x), ln_g[i], ln_b[i], W1[i], b1[i], W2[i], b2[i]) + x
        return x
    x = L0_attn_x
    x = x + 0.5 * _L0_ffn_ref(_layernorm(x, axis=-1), L0_ffn_k0, L0_ffn_k1, L0_ffn_k2, L0_ffn_s0, L0_ffn_s1, L0_ffn_s2)
    x = x + _L0_attn_ref(_layernorm(x, axis=-1), L0_attn_wq, L0_attn_bq, L0_attn_wk, L0_attn_bk, L0_attn_wv, L0_attn_bv, L0_attn_wo, L0_attn_bo, L0_attn_rot_cos, L0_attn_rot_sin)
    x = x + 0.5 * _L0_ffn_ref(_layernorm(x, axis=-1), L0_ffn_k0, L0_ffn_k1, L0_ffn_k2, L0_ffn_s0, L0_ffn_s1, L0_ffn_s2)
    x = x + 0.5 * _L1_ffn_ref(_layernorm(x, axis=-1), L1_ffn_Wqkv, L1_ffn_q_scale, L1_ffn_k_scale, L1_ffn_Wo, L1_ffn_ln_g, L1_ffn_ln_b, L1_ffn_W1, L1_ffn_b1, L1_ffn_W2, L1_ffn_b2)
    x = x + _L1_attn_ref(_layernorm(x, axis=-1), L1_attn_W_write, L1_attn_W_read, L1_attn_W_beta, L1_attn_decay)
    x = x + 0.5 * _L1_ffn_ref(_layernorm(x, axis=-1), L1_ffn_Wqkv, L1_ffn_q_scale, L1_ffn_k_scale, L1_ffn_Wo, L1_ffn_ln_g, L1_ffn_ln_b, L1_ffn_W1, L1_ffn_b1, L1_ffn_W2, L1_ffn_b2)
    return x

_drawn_inputs = setup_inputs


def setup_inputs(seed=0):
    import zlib

    import numpy as np

    out = dict(_drawn_inputs(seed))
    spreads = {'L0_attn_bq': (0.0, 0.8),
     'L0_attn_bk': (0.0, 0.8),
     'L0_attn_bv': (0.0, 0.528),
     'L0_attn_bo': (0.0, 0.1),
     'L1_ffn_q_scale': (1.0, 0.6),
     'L1_ffn_k_scale': (1.0, 0.6),
     'L1_ffn_ln_g': (1.0, 0.6),
     'L1_ffn_ln_b': (0.0, 0.8),
     'L1_ffn_b1': (0.0, 0.8),
     'L1_ffn_b2': (0.0, 0.308)}
    factors = {'L1_attn_W_write': 4.954,
     'L1_attn_W_read': 5.519,
     'L1_attn_W_beta': 8.0,
     'L1_attn_decay': 8.0,
     'L1_ffn_W1': 6.163,
     'L1_ffn_W2': 6.144}
    for name, (base, spread) in spreads.items():
        noise = np.random.default_rng([zlib.crc32(name.encode()), seed]).standard_normal(out[name].shape)
        drawn = base * np.exp(spread * noise) if base else spread * noise
        out[name] = jnp.asarray(drawn.astype(out[name].dtype))
    for name, factor in factors.items():
        out[name] = (out[name] * factor).astype(out[name].dtype)
    return out
```

```python
from contextlib import ExitStack

import numpy as np
import concourse.bass as bass
from concourse import mybir

P = 128
F32 = mybir.dt.float32
BF16 = mybir.dt.bfloat16
U8 = mybir.dt.uint8
I32 = mybir.dt.int32
ALU = mybir.AluOpType
ACT = mybir.ActivationFunctionType
AXX = mybir.AxisListType.X

BATCH, SEQ, DIM = 4, 512, 128
TOKENS = BATCH * SEQ
TILES = SEQ // P
PER = BATCH * TILES
EPS = 1e-5
DEPTH, HEADS, DH, WIN = 6, 16, 64, 32
INNER = HEADS * DH
PAIRS = HEADS // 2
HALF = DH // 2
WINS = P // WIN
KEYS = 2 * WIN
HALO = WIN
FF = int(DIM * 4 * 2 / 3)
FFB = -(-FF // P)
VEC = 3 + 2 * FFB
MASKED = -3.0e38
ROOT_BITS, NEWTONS = 0x5F3759DF, 3


class Tile:

    def __init__(self, layer, g, i):
        self.n = layer * PER + g * TILES + i
        self.s = layer * (PER + 1) + g * TILES + i
        self.t = i % TILES
        self.col = g * SEQ + i * P


LAGS, TAIL = 5, 2


def tiles(layer, g, j):
    inside = lambda i: not isinstance(g, int) or 0 <= g * TILES + i < PER
    return [Tile(layer, g, j - k) if inside(j - k) else None for k in range(LAGS + 1)]


def attention_layer(eng, layer, step):
    for j in range(LAGS):
        step(*tiles(layer, 0, j))
    head = LAGS - TILES
    with eng.Fori(1, BATCH - 1) as g:
        for j in range(head, head + TILES):
            step(*tiles(layer, g, j))
    for j in range(head, TILES + 2):
        step(*tiles(layer, BATCH - 1, j))


def spread(ap, axis, shape):
    return ap.unsqueeze(axis).broadcast_to(shape)


class Semaphores:

    def __init__(self, nc, ctx, stage):
        self.nc, self.ctx, self.stage, self.held = nc, ctx, stage, {}

    def __call__(self, name):
        if name not in self.held:
            self.held[name] = self.ctx.enter_context(self.nc.semaphore(f"{self.stage}_{name}"))
        return self.held[name]


def windowed_layers(nc, run, sem, ZT, consts, dram):
    first = run * DEPTH
    tag = f"w{run}"
    ident, ident_b, mean_w, mask = consts["ident"], consts["ident_b"], consts["mean_w"], consts["mask"]
    eps = consts["eps"]
    ctx = ExitStack()
    with ctx:
        def sb(name, shape, dt=F32):
            return ctx.enter_context(nc.sbuf_tensor(f"{tag}_{name}", shape, dt))

        def ps(name, shape):
            return ctx.enter_context(nc.psum_tensor(f"{tag}_{name}", shape, F32))

        w_qkv = sb("w_qkv", [P, 3 * INNER])
        w_o = sb("w_o", [P, PAIRS, DIM])
        w_1 = sb("w_1", [P, 2 * FFB, P])
        w_2 = sb("w_2", [P, FFB, DIM])
        vec = sb("vec", [P, VEC])
        qk_scale = sb("qk_scale", [P, 2, DEPTH, DH])
        rot = sb("rot", [P, 2, 2, TILES, DH])
        rot_l = sb("rot_l", [P, 2, 2, TILES, DH])
        shifted = sb("shifted", [P, SEQ])
        raw = sb("raw", [P, 2, INNER])
        squares = sb("squares", [P, 2, INNER])
        turned = sb("turned", [P, 2, 2, INNER])
        sumsq = sb("sumsq", [P, 2, HEADS])
        bits = sb("bits", [P, 2, HEADS], I32)
        newton = sb("newton", [P, 2, HEADS])
        halved = sb("halved", [P, 2, HEADS])
        c_1_5 = sb("c_1_5", [P, 2, HEADS])
        inv_norm = sb("inv_norm", [P, 2, HEADS])
        qk = sb("qk", [P, 2, 2, INNER])
        qT = sb("qT", [P, PAIRS, P])
        kT = sb("kT", [P, PAIRS, 2, HALO + SEQ])
        v = sb("v", [P, TILES, INNER])
        probs = sb("probs", [P, HEADS, KEYS])
        probs_n = sb("probs_n", [P, HEADS, KEYS])
        row_max = sb("row_max", [P, HEADS])
        row_sum = sb("row_sum", [P, HEADS])
        row_inv = sb("row_inv", [P, HEADS])
        pT = sb("pT", [P, 2, HEADS, P])
        pT_prev = sb("pT_prev", [P, 2, HEADS, WIN])
        attT = sb("attT", [P, PAIRS, P])

        w_in, w2_in, tab_in, cleared = sem("w_in"), sem("w2_in"), sem("tab_in"), sem("cleared")
        shift_ready, rot_ready = sem("shift_ready"), sem("rot_ready")
        pe_q, pe_k, pe_v, pe_tq, pe_tk = sem("pe_q"), sem("pe_k"), sem("pe_v"), sem("pe_tq"), sem("pe_tk")
        pe_s, pe_pv, pe_y = sem("pe_s"), sem("pe_pv"), sem("pe_y")
        act_raw, act_sq, act_v, act_tq, act_tk = sem("act_raw"), sem("act_sq"), sem("act_v"), sem("act_tq"), sem("act_tk")
        act_exp, act_o = sem("act_exp"), sem("act_o")
        dve_ss, dve_floor, dve_turn = sem("dve_ss"), sem("dve_floor"), sem("dve_turn")
        dve_shift, dve_guess, pool_newton = sem("dve_shift"), sem("dve_guess"), sem("pool_newton")
        dve_max, dve_sub, dve_sum, dve_inv = sem("dve_max"), sem("dve_sub"), sem("dve_sum"), sem("dve_inv")
        dve_pT, dve_y = sem("dve_pT"), sem("dve_y")
        pool_add, pool_inv, pool_qk, pool_p = sem("pool_add"), sem("pool_inv"), sem("pool_qk"), sem("pool_p")
        f_copy, f_mean, f_cen_s, f_sq_s, f_var = sem("f_copy"), sem("f_mean"), sem("f_cen"), sem("f_sq"), sem("f_var")
        f_std, f_rstd_s, f_nrm, f_ln = sem("f_std"), sem("f_rstd"), sem("f_nrm"), sem("f_ln")
        f_h, f_gelu, f_hid_s, f_out, f_add = sem("f_h"), sem("f_gelu"), sem("f_hid"), sem("f_out"), sem("f_add")

        ring = ps("ring", [P, 2, 2, 512])
        ps_s = ps("ps_s", [P, 2, 512])
        ps_o = ps("ps_o", [P, 2, 512])
        ps_heads = ps_s[:, :, :].rearrange("p a (h k) -> p (a h) k", k=KEYS)
        ps_pairs = ps_o[:, :, :].rearrange("p a (h q) -> p (a h) q", q=P)

        xn = [turned[:, b // 2, 0, b % 2 * SEQ:(b % 2 + 1) * SEQ] for b in range(BATCH)]
        std = [turned[:, b // 2, 1, b % 2 * SEQ:(b % 2 + 1) * SEQ] for b in range(BATCH)]
        sq = squares[:, 1, SEQ:2 * SEQ]
        gate = [raw[:, 0, 0:SEQ], raw[:, 0, SEQ:2 * SEQ]]
        hid = [squares[:, 0, 0:SEQ], squares[:, 0, SEQ:2 * SEQ], squares[:, 1, 0:SEQ]]

        def half(t, use):
            return (5 * t + use) % 2

        block = ctx.enter_context(nc.Block())

        @block.sync
        def _(sp):
            def load_attention(layer):
                sp.dma_start(w_qkv[:], dram["w_qkv"][layer]).then_inc(w_in, 16)
                sp.dma_start(w_o[:].rearrange("p a b -> p (a b)"), dram["w_o"][layer]).then_inc(w_in, 16)

            def load_feed_forward(layer):
                sp.dma_start(w_1[:].rearrange("p a b -> p (a b)"), dram["w_1"][layer]).then_inc(w2_in, 16)
                sp.dma_start(w_2[:].rearrange("p a b -> p (a b)"), dram["w_2"][layer]).then_inc(w2_in, 16)
                sp.dma_start(vec[:], dram["vec"][layer]).then_inc(w2_in, 16)

            sp.dma_start(rot[:].rearrange("p a b t d -> p (a b t d)"), dram["rot"]).then_inc(tab_in, 16)
            sp.dma_start(qk_scale[:].rearrange("p a l d -> p (a l d)"), dram["qk_scale"]).then_inc(tab_in, 16)
            load_attention(0)
            load_feed_forward(0)
            with sp.Fori(1, DEPTH) as layer:
                sp.wait_ge(pe_y, (first + layer) * PER)
                load_attention(layer)
                sp.wait_ge(f_add, (first + layer) * BATCH)
                load_feed_forward(layer)

        @block.tensor
        def _(pe):
            def project(T, at, use, which, done):
                for c in range(2):
                    last = nc.tensor.matmul(ring[:, half(at, use), c, :], shifted[:, T.t * P:(T.t + 1) * P],
                                            w_qkv[:, which * INNER + c * 512:which * INNER + (c + 1) * 512],
                                            start=True, stop=True)
                last.then_inc(done, 1)

            def turn(B, use, which, done):
                at = half(B.t + 2, use)
                for p in range(PAIRS):
                    last = nc.tensor.transpose(ring[:, at, p // 4, (p % 4) * P:(p % 4 + 1) * P],
                                               qk[:, B.t % 2, which, p * P:(p + 1) * P], ident[:])
                last.then_inc(done, 1)

            def values(D, E):
                pe.wait_ge(dve_pT, D.n + 1)
                pe.wait_ge(act_v, D.n + 1)
                if E:
                    pe.wait_ge(dve_y, E.n + 1)
                for p in range(PAIRS):
                    for h in (2 * p, 2 * p + 1):
                        r = DH * (h % 2)
                        last = nc.tensor.matmul(ps_pairs[r:r + DH, p, :], v[:, D.t, h * DH:(h + 1) * DH],
                                                pT[:, D.t % 2, h, :], start=True, stop=D.t == 0)
                    for h in (2 * p, 2 * p + 1) if D.t else ():
                        r = DH * (h % 2)
                        last = nc.tensor.matmul(ps_pairs[r:r + DH, p, 0:WIN],
                                                v[:, D.t - 1, h * DH:(h + 1) * DH],
                                                pT_prev[:, D.t % 2, h, :], start=False, stop=True)
                last.then_inc(pe_pv, 1)

            def output(E):
                pe.wait_ge(act_o, E.n + 1)
                for p in range(PAIRS):
                    last = nc.tensor.matmul(ps_pairs[:, 0, :], w_o[:, p, :], attT[:, p, :],
                                            start=p == 0, stop=p == PAIRS - 1)
                last.then_inc(pe_y, 1)

            def step(T, A, B, C, D, E):
                if B:
                    pe.wait_ge(pool_qk, 2 * B.n + 1)
                    if A:
                        pe.wait_ge(act_sq, 2 * A.n + 2)
                    else:
                        pe.wait_ge(act_v, B.n)
                    turn(B, 0, 0, pe_tq)
                if T:
                    pe.wait_ge(shift_ready, T.s + 1)
                    if B:
                        pe.wait_ge(act_v, B.n + 1)
                    project(T, T.t, 1, 0, pe_q)
                if E:
                    output(E)
                if B:
                    pe.wait_ge(pool_qk, 2 * B.n + 2)
                    pe.wait_ge(act_tq, B.n + 1)
                    turn(B, 2, 1, pe_tk)
                if T:
                    pe.wait_ge(act_sq, 2 * T.n + 1)
                    project(T, T.t, 3, 1, pe_k)
                if B:
                    pe.wait_ge(act_tk, B.n + 1)
                    if C:
                        pe.wait_ge(dve_sub, C.n + 1)
                    for a in range(2):
                        nc.tensor.matmul(ps_s[:, a, :], ident_b[:],
                                         spread(mask[:, min(B.t, 1), :], 1, [P, HEADS // 2, KEYS]),
                                         start=True, stop=False, skip_group_check=True)
                        for p in range(a * 4, a * 4 + 4):
                            for w in range(WINS):
                                col = B.t * P + w * WIN
                                last = nc.tensor.matmul(
                                    ps_heads[w * WIN:(w + 1) * WIN, 2 * p:2 * p + 2, :],
                                    qT[:, p, w * WIN:(w + 1) * WIN], kT[:, p, :, col:col + KEYS],
                                    start=False, stop=True, skip_group_check=True)
                    last.then_inc(pe_s, 1)
                if D:
                    values(D, E)
                if A:
                    if B:
                        pe.wait_ge(act_tk, B.n + 1)
                    else:
                        pe.wait_ge(act_sq, 2 * A.n + 2)
                    project(A, A.t + 1, 4, 2, pe_v)
            pe.wait_ge(cleared, 2 * run + 2)
            with pe.Fori(first, first + DEPTH) as layer:
                pe.wait_ge(w_in, layer * 32 + 32)
                attention_layer(pe, layer, step)
                pe.wait_ge(w2_in, layer * 48 + 48)

                def mean(b):
                    pe.wait_ge(f_copy, layer * BATCH + b + 1)
                    nc.tensor.matmul(ps_s[:, 0, :], mean_w[:], shifted[:], start=True, stop=True).then_inc(f_mean, 1)

                def variance(b):
                    pe.wait_ge(f_sq_s, layer * BATCH + b + 1)
                    if b:
                        pe.wait_ge(f_std, layer * BATCH + b)
                    nc.tensor.matmul(ps_s[:, 1, :], mean_w[:], sq, start=True, stop=True).then_inc(f_var, 1)

                def up(b, i):
                    n = (layer * BATCH + b) * FFB + i
                    if i == 0:
                        pe.wait_ge(f_ln, layer * BATCH + b + 1)
                    if b or i == 2:
                        pe.wait_ge(f_hid_s, n - 1)
                    for part in range(2):
                        last = nc.tensor.matmul(ring[:, (b * FFB + i) % 2, part, :], w_1[:, part * FFB + i, :], xn[b],
                                                start=True, stop=True)
                    last.then_inc(f_h, 1)

                def down(b):
                    pe.wait_ge(f_hid_s, (layer * BATCH + b) * FFB + FFB)
                    if b >= 2:
                        pe.wait_ge(f_add, layer * BATCH + b - 1)
                    for i in range(FFB):
                        last = nc.tensor.matmul(ps_o[:, b % 2, :], w_2[:, i, :], hid[i], start=i == 0,
                                                stop=i == FFB - 1)
                    last.then_inc(f_out, 1)

                C, D, E = tiles(layer, BATCH, TAIL)[3:]
                mean(0)
                output(E)
                variance(0)
                values(D, E)
                mean(1)
                output(D)
                variance(1)
                values(C, D)
                mean(2)
                output(C)
                variance(2)
                for i in range(FFB):
                    up(0, i)
                mean(3)
                up(1, 0)
                variance(3)
                down(0)
                for b in range(1, BATCH):
                    for i in range(1, FFB):
                        up(b, i)
                    if b + 1 < BATCH:
                        up(b + 1, 0)
                    down(b)

        @block.scalar
        def _(act):
            def values_out(D, E):
                act.wait_ge(pe_pv, D.n + 1)
                if E:
                    act.wait_ge(pe_y, E.n + 1)
                nc.scalar.activation(attT[:], ps_pairs, ACT.Copy).then_inc(act_o, 1)

            def copy_and_square(T, A, which, done):
                projected = ring[:, half(T.t, 1 + 2 * which), :, :].rearrange("p a b -> p (a b)")
                act.wait_ge(done, T.n + 1)
                if A:
                    act.wait_ge(dve_turn, 2 * A.n + which + 1)
                nc.scalar.activation(raw[:, which, :], projected, ACT.Copy).then_inc(act_raw, 1)
                if A:
                    act.wait_ge(dve_ss, 2 * A.n + which + 1)
                nc.scalar.activation(squares[:, which, :], projected, ACT.Square).then_inc(act_sq, 1)

            def step(T, A, B, C, D, E):
                if B:
                    act.wait_ge(pe_tq, B.n + 1)
                    if C:
                        act.wait_ge(pe_s, C.n + 1)
                    nc.scalar.activation(qT[:].rearrange("p a b -> p (a b)"),
                                         ring[:, half(B.t + 2, 0), :, :].rearrange("p a b -> p (a b)"),
                                         ACT.Copy).then_inc(act_tq, 1)
                if T:
                    copy_and_square(T, A, 0, pe_q)
                if B:
                    act.wait_ge(pe_tk, B.n + 1)
                    turned_k = ring[:, half(B.t + 2, 2), :, :].rearrange("p a (b q) -> p (a b) q", q=P)
                    for h in range(2):
                        last = nc.scalar.activation(
                            kT[h * DH:(h + 1) * DH, :, h, HALO + B.t * P:HALO + (B.t + 1) * P],
                            turned_k[h * DH:(h + 1) * DH], ACT.Copy)
                    last.then_inc(act_tk, 1)
                if T:
                    copy_and_square(T, A, 1, pe_k)
                if D:
                    values_out(D, E)
                if B:
                    act.wait_ge(dve_sub, B.n + 1)
                    nc.scalar.activation(probs[:], probs[:], ACT.Exp).then_inc(act_exp, 1)
                if A:
                    act.wait_ge(pe_v, A.n + 1)
                    nc.scalar.activation(v[:, A.t, :], ring[:, half(A.t + 1, 4), :, :].rearrange("p a b -> p (a b)"),
                                         ACT.Copy).then_inc(act_v, 1)

            act.wait_ge(cleared, 2 * run + 2)
            with act.Fori(first, first + DEPTH) as layer:
                attention_layer(act, layer, step)
                act.wait_ge(w2_in, layer * 48 + 48)

                def square(b):
                    act.wait_ge(f_cen_s, layer * BATCH + b + 1)
                    if b:
                        act.wait_ge(f_var, layer * BATCH + b)
                    nc.scalar.activation(sq, xn[b], ACT.Square).then_inc(f_sq_s, 1)

                def deviation(b):
                    act.wait_ge(f_var, layer * BATCH + b + 1)
                    nc.scalar.activation(std[b], ps_s[:, 1, :], ACT.Sqrt, bias=eps[:, 0:1]).then_inc(f_std, 1)

                def gelu(b, i):
                    n = (layer * BATCH + b) * FFB + i
                    act.wait_ge(f_h, n + 1)
                    if b or i == 2:
                        act.wait_ge(f_hid_s, n - 1)
                    nc.scalar.activation(gate[(b * FFB + i) % 2], ring[:, (b * FFB + i) % 2, 1, :], ACT.Gelu,
                                         bias=vec[:, 2 + FFB + i:3 + FFB + i]).then_inc(f_gelu, 1)

                for b in range(BATCH):
                    square(b)
                    deviation(b)
                    if b < 2:
                        values_out(*tiles(layer, BATCH, TAIL + b)[4:])
                    if b == 2:
                        for i in range(FFB):
                            gelu(0, i)
                for b in range(1, BATCH):
                    for i in range(FFB):
                        gelu(b, i)

        @block.vector
        def _(dve):
            nc.vector.memset(shifted[:], 0.0)
            nc.vector.memset(kT[:], 0.0).then_inc(cleared, 1)
            dve.wait_ge(cleared, 2 * run + 2)

            def shifted_copy(col, t):
                nc.vector.tensor_copy(shifted[0:64, t * P:(t + 1) * P], ZT[0:64, bass.ds(col, P)])
                if t == 0:
                    nc.vector.tensor_copy(shifted[64:128, 1:P], ZT[64:128, bass.ds(col, P - 1)]).then_inc(shift_ready, 1)
                else:
                    nc.vector.tensor_copy(shifted[64:128, t * P:(t + 1) * P],
                                          ZT[64:128, bass.ds(col - 1, P)]).then_inc(shift_ready, 1)

            def rotate(T, A, which):
                dve.wait_ge(act_raw, 2 * T.n + which + 1)
                if A:
                    dve.wait_ge(pool_add, 2 * A.n + which + 1)
                src = raw[:, which, :].rearrange("p (h d) -> p h d", d=DH)
                cos = spread(rot_l[:, which, 0, T.t, :], 1, [P, HEADS, DH])
                nc.vector.tensor_tensor(turned[:, which, 0, :].rearrange("p (h d) -> p h d", d=DH),
                                        src, cos, ALU.mult)
                swapped = raw[:, which, :].rearrange("p (h two d) -> p h two d", two=2,
                                                     d=HALF)[:, :, ::-1, :]
                sin = spread(rot_l[:, which, 1, T.t, :].rearrange("p (two d) -> p two d", two=2),
                             1, [P, HEADS, 2, HALF])
                nc.vector.tensor_tensor(turned[:, which, 1, :].rearrange("p (h two d) -> p h two d", two=2, d=HALF),
                                        swapped, sin, ALU.mult).then_inc(dve_turn, 1)
                dve.wait_ge(act_sq, 2 * T.n + which + 1)
                if A:
                    dve.wait_ge(pool_inv, A.n + 1)
                nc.vector.reduce_sum(sumsq[:, which, :], squares[:, which, :]
                                     .rearrange("p (h d) -> p h d", d=DH), AXX).then_inc(dve_ss, 1)

            def transpose_probs(C):
                dve.wait_ge(pool_p, C.n + 1)
                for w in range(WINS):
                    q = slice(w * WIN, (w + 1) * WIN)
                    last = nc.vector.transpose(pT[q, C.t % 2, :, q], probs_n[q, :, WIN:KEYS])
                    if w:
                        last = nc.vector.transpose(pT[(w - 1) * WIN:w * WIN, C.t % 2, :, q], probs_n[q, :, 0:WIN])
                    elif C.t:
                        nc.vector.transpose(pT_prev[P - WIN:P, C.t % 2, :, :], probs_n[q, :, 0:WIN])
                last.then_inc(dve_pT, 1)

            def add_output(E):
                dve.wait_ge(pe_y, E.n + 1)
                nc.vector.tensor_tensor(ZT[:, bass.ds(E.col, P)], ps_pairs[:, 0, :], ZT[:, bass.ds(E.col, P)],
                                        ALU.add).then_inc(dve_y, 1)

            def step(T, A, B, C, D, E):
                if T:
                    rotate(T, A, 0)
                if E:
                    add_output(E)
                if T:
                    rotate(T, A, 1)
                if B:
                    dve.wait_ge(pe_s, B.n + 1)
                    nc.vector.reduce_max(row_max[:], ps_heads, AXX).then_inc(dve_max, 1)
                if T:
                    dve.wait_ge(dve_ss, 2 * T.n + 2)
                    nc.vector.tensor_scalar(halved[:], sumsq[:], 1e-24, -0.5, ALU.max, ALU.mult)
                    nc.vector.tensor_scalar_max(sumsq[:], sumsq[:], 1e-24).then_inc(dve_floor, 1)
                if B:
                    if C:
                        dve.wait_ge(pool_p, C.n + 1)
                    dve.wait_ge(dve_max, B.n + 1)
                    nc.vector.tensor_tensor(probs[:], ps_heads, spread(row_max[:], 2, [P, HEADS, KEYS]),
                                            ALU.subtract).then_inc(dve_sub, 1)
                if T:
                    dve.wait_ge(dve_floor, T.n + 1)
                    nc.vector.tensor_scalar(bits[:], sumsq[:].bitcast(I32), 1, None,
                                            ALU.logical_shift_right).then_inc(dve_shift, 1)
                    shifted_copy(T.col + P, (T.t + 1) % TILES)
                    dve.wait_ge(dve_shift, T.n + 1)
                    nc.vector.tensor_scalar(bits[:], bits[:], -1.0, float(ROOT_BITS),
                                            ALU.mult, ALU.add).then_inc(dve_guess, 1)
                if C:
                    transpose_probs(C)
                if B:
                    dve.wait_ge(act_exp, B.n + 1)
                    nc.vector.reduce_sum(row_sum[:], probs[:], AXX).then_inc(dve_sum, 1)
                    dve.wait_ge(dve_sum, B.n + 1)
                    nc.vector.reciprocal(row_inv[:], row_sum[:]).then_inc(dve_inv, 1)

            with dve.Fori(first, first + DEPTH) as layer:
                def shift(b):
                    if b:
                        dve.wait_ge(f_cen_s, layer * BATCH + b)
                    nc.vector.tensor_copy(shifted[0:64, :], ZT[0:64, b * SEQ:(b + 1) * SEQ])
                    nc.vector.tensor_copy(shifted[64:128, 1:SEQ],
                                          ZT[64:128, b * SEQ:(b + 1) * SEQ - 1]).then_inc(f_copy, 1)

                def center(b):
                    dve.wait_ge(f_mean, layer * BATCH + b + 1)
                    nc.vector.tensor_tensor(xn[b], shifted[:], ps_s[:, 0, :], ALU.subtract).then_inc(f_cen_s, 1)

                def normalise(b):
                    dve.wait_ge(f_std, layer * BATCH + b + 1)
                    nc.vector.reciprocal(std[b], std[b]).then_inc(f_rstd_s, 1)
                    dve.wait_ge(f_rstd_s, layer * BATCH + b + 1)
                    nc.vector.tensor_tensor(xn[b], xn[b], std[b], ALU.mult).then_inc(f_nrm, 1)
                    dve.wait_ge(f_nrm, layer * BATCH + b + 1)
                    nc.vector.tensor_scalar(xn[b], xn[b], vec[:, 0:1], vec[:, 1:2],
                                            ALU.mult, ALU.add).then_inc(f_ln, 1)

                def hidden(b, i):
                    n = (layer * BATCH + b) * FFB + i
                    dve.wait_ge(f_gelu, n + 1)
                    if b and i == 0:
                        dve.wait_ge(f_out, layer * BATCH + b)
                    nc.vector.scalar_tensor_tensor(hid[i], ring[:, (b * FFB + i) % 2, 0, :], vec[:, 2 + i:3 + i],
                                                   gate[(b * FFB + i) % 2], ALU.add, ALU.mult).then_inc(f_hid_s, 1)

                def add_rows(b):
                    dve.wait_ge(f_out, layer * BATCH + b + 1)
                    cols = ZT[:, b * SEQ:(b + 1) * SEQ]
                    nc.vector.scalar_tensor_tensor(cols, ps_o[:, b % 2, :], vec[:, VEC - 1:VEC], cols,
                                                   ALU.add, ALU.add).then_inc(f_add, 1)

                shifted_copy(0, 0)
                dve.wait_ge(rot_ready, layer + 1)
                attention_layer(dve, layer, step)
                C, D, E = tiles(layer, BATCH, TAIL)[3:]
                dve.wait_ge(w2_in, layer * 48 + 48)
                dve.wait_ge(pool_add, 2 * (layer * PER + PER))
                shift(0)
                center(0)
                shift(1)
                add_output(E)
                transpose_probs(C)
                center(1)
                shift(2)
                add_output(D)
                normalise(0)
                center(2)
                normalise(1)
                add_output(C)
                dve.wait_ge(dve_y, layer * PER + PER)
                shift(3)
                hidden(0, 0)
                center(3)
                hidden(0, 1)
                hidden(0, 2)
                normalise(2)
                hidden(1, 0)
                hidden(1, 1)
                add_rows(0)
                hidden(1, 2)
                normalise(3)
                add_rows(1)
                for b in range(2, BATCH):
                    for i in range(FFB):
                        hidden(b, i)
                    add_rows(b)
                dve.wait_ge(f_add, layer * BATCH + BATCH)

        @block.gpsimd
        def _(pool):
            nc.gpsimd.memset(pT_prev[:], 0.0)
            nc.gpsimd.memset(c_1_5[:], 1.5)
            nc.gpsimd.memset(pT[:], 0.0).then_inc(cleared, 1)
            pool.wait_ge(cleared, 2 * run + 2)
            pool.wait_ge(tab_in, 32 * run + 32)

            def add(T, B, which, turned_out):
                pool.wait_ge(dve_turn, 2 * T.n + which + 1)
                if B:
                    pool.wait_ge(turned_out, B.n + 1)
                nc.gpsimd.tensor_tensor(qk[:, T.t % 2, which, :], turned[:, which, 0, :], turned[:, which, 1, :],
                                        ALU.add).then_inc(pool_add, 1)

            def step(T, A, B, C, D, E):
                if T:
                    add(T, B, 0, pe_tq)
                    add(T, B, 1, pe_tk)
                if T:
                    pool.wait_ge(dve_guess, T.n + 1)
                    steps = 4 * NEWTONS
                    y = bits[:].bitcast(F32)
                    for k in range(NEWTONS):
                        at = T.n * (steps - 1) + 4 * k
                        if k:
                            pool.wait_ge(pool_newton, at)
                        nc.gpsimd.tensor_tensor(newton[:], y, y, ALU.mult).then_inc(pool_newton, 1)
                        pool.wait_ge(pool_newton, at + 1)
                        nc.gpsimd.tensor_tensor(newton[:], newton[:], halved[:], ALU.mult).then_inc(pool_newton, 1)
                        pool.wait_ge(pool_newton, at + 2)
                        nc.gpsimd.tensor_tensor(newton[:], newton[:], c_1_5[:], ALU.add).then_inc(pool_newton, 1)
                        pool.wait_ge(pool_newton, at + 3)
                        nc.gpsimd.tensor_tensor(inv_norm[:], newton[:], y, ALU.mult).then_inc(
                            pool_newton if k < NEWTONS - 1 else pool_inv, 1)
                        y = inv_norm[:]
                    pool.wait_ge(pool_inv, T.n + 1)
                    pool.wait_ge(pool_add, 2 * T.n + 2)
                    for which in range(2):
                        heads = qk[:, T.t % 2, which, :].rearrange("p (h d) -> p h d", d=DH)
                        nc.gpsimd.tensor_tensor(heads, heads, spread(inv_norm[:, which, :], 2, [P, HEADS, DH]),
                                                ALU.mult).then_inc(pool_qk, 1)
                if B:
                    pool.wait_ge(dve_inv, B.n + 1)
                    if C:
                        pool.wait_ge(dve_pT, C.n + 1)
                    nc.gpsimd.tensor_tensor(probs_n[:], probs[:], spread(row_inv[:], 2, [P, HEADS, KEYS]),
                                            ALU.mult).then_inc(pool_p, 1)

            with pool.Fori(first, first + DEPTH) as layer:
                pool.wait_ge(shift_ready, Tile(layer, 0, 0).s + 1)
                for which in range(2):
                    scale = qk_scale[:, which, bass.ds(layer - first, 1), :].rearrange("p a d -> p (a d)")
                    nc.gpsimd.tensor_tensor(rot_l[:, which, 0, :, :], rot[:, which, 0, :, :],
                                            spread(scale, 1, [P, TILES, DH]), ALU.mult)
                    for d in range(2):
                        here = slice(d * HALF, (d + 1) * HALF)
                        there = slice((1 - d) * HALF, (2 - d) * HALF)
                        last = nc.gpsimd.tensor_tensor(rot_l[:, which, 1, :, here], rot[:, which, 1, :, here],
                                                       spread(scale[:, there], 1, [P, TILES, HALF]), ALU.mult)
                last.then_inc(rot_ready, 1)
                attention_layer(pool, layer, step)


def rotary_tables():
    half = np.arange(0, DH, 2, dtype=np.float32)
    inv_freq = (1.0 / np.power(np.float32(10000.0), half / DH)).astype(np.float32)
    t = np.arange(SEQ, dtype=np.float32)
    freqs = (t[:, None] * inv_freq[None, :]).astype(np.float32).astype(np.float64)
    base = ((half + 0.4 * DH) / (1.4 * DH)).astype(np.float64)
    scale = base[None, :] ** ((t[:, None] - SEQ // 2) / (WIN // 2)).astype(np.float64)
    both = lambda a, b: np.concatenate([a, b], -1)
    cos, sin = np.cos(freqs), np.sin(freqs)
    rows = []
    for s in (8.0 * scale, 1.0 / scale):
        rows.append([both(cos * s, cos * s), both(-sin * s, sin * s)])
    rows = np.array(rows).astype(np.float32)
    rows = rows.reshape(2, 2, TILES, P, DH).transpose(3, 0, 1, 2, 4)
    return np.ascontiguousarray(rows.reshape(P, -1))


def window_mask():
    row = np.arange(P)
    i, key = row % WIN, np.arange(KEYS)
    ok = np.where(key[None, :] < WIN, key[None, :] >= i[:, None], key[None, :] - WIN <= i[:, None])
    first = ok & ~((row[:, None] < WIN) & (key[None, :] < WIN))
    return np.where(np.stack([first, ok], 1), 0.0, MASKED).astype(np.float32).reshape(P, 2 * KEYS)


def layer_weights(i, depth=DEPTH):
    A = lambda n: np.asarray(i[f"L1_ffn_{n}"])[:depth]
    out = {"w_qkv": A("Wqkv"), "w_o": A("Wo").reshape(depth, PAIRS, P, DIM).transpose(0, 2, 1, 3)}
    w1 = np.zeros((depth, P, 2, FFB * P), np.float32)
    w1[:, :, 0, :FF], w1[:, :, 1, :FF] = A("W1")[:, :, :FF], A("W1")[:, :, FF:]
    w2 = np.zeros((depth, FFB * P, DIM), np.float32)
    w2[:, :FF] = A("W2")
    b1 = np.zeros((depth, 2, FFB * P), np.float32)
    b1[:, 0, :FF], b1[:, 1, :FF] = A("b1")[:, :FF], A("b1")[:, FF:]
    cols = [A("ln_g")[:, :, None], A("ln_b")[:, :, None], b1.reshape(depth, 2 * FFB, P).transpose(0, 2, 1),
            A("b2")[:, :, None]]
    out.update(w_1=w1, w_2=w2.reshape(depth, FFB, P, DIM).transpose(0, 2, 1, 3), vec=np.concatenate(cols, -1))
    scales = np.stack([A("q_scale"), A("k_scale")]).reshape(1, -1)
    out["qk_scale"] = np.broadcast_to(scales, (P, scales.shape[1]))
    return {k: np.ascontiguousarray(v.reshape(v.shape[:2] + (-1,)) if v.ndim > 2 else v) for k, v in out.items()}


H0, D0 = 16, 8
GROUPS = DIM // D0
TOK = SEQ // H0
QUADS = 4
J0 = H0 // QUADS
KB = SEQ // P
FF0 = 512
BLK = FF0 // P


def layer_norm(nc, run, sem, src, dst, consts):
    tag, base = f"n{run}", run * BATCH
    mean_w, eps = consts["mean_w"], consts["eps"]
    with ExitStack() as ctx:
        std = ctx.enter_context(nc.sbuf_tensor(f"{tag}_std", [P, BATCH, SEQ], F32))
        sq = ctx.enter_context(nc.sbuf_tensor(f"{tag}_sq", [P, BATCH, SEQ], F32))
        ps = ctx.enter_context(nc.psum_tensor(f"{tag}_ps", [P, 2, BATCH, SEQ], F32))
        mean_s, cen_s, sq_s, var_s, std_s, inv_s, out_s = [
            sem(n) for n in ("mean", "cen", "sq", "var", "std", "inv", "out")]
        block = ctx.enter_context(nc.Block())
        cols = [slice(b * SEQ, (b + 1) * SEQ) for b in range(BATCH)]

        @block.tensor
        def _(pe):
            for b in range(BATCH):
                nc.tensor.matmul(ps[:, 0, b, :], mean_w[:], src[:, cols[b]], start=True, stop=True).then_inc(mean_s, 1)
            for b in range(BATCH):
                pe.wait_ge(sq_s, base + b + 1)
                nc.tensor.matmul(ps[:, 1, b, :], mean_w[:], sq[:, b, :], start=True, stop=True).then_inc(var_s, 1)

        @block.scalar
        def _(act):
            for b in range(BATCH):
                act.wait_ge(cen_s, base + b + 1)
                nc.scalar.activation(sq[:, b, :], dst[:, cols[b]], ACT.Square).then_inc(sq_s, 1)
            for b in range(BATCH):
                act.wait_ge(var_s, base + b + 1)
                nc.scalar.activation(std[:, b, :], ps[:, 1, b, :], ACT.Sqrt, bias=eps[:, 0:1]).then_inc(std_s, 1)

        @block.vector
        def _(dve):
            for b in range(BATCH):
                dve.wait_ge(mean_s, base + b + 1)
                nc.vector.tensor_tensor(dst[:, cols[b]], src[:, cols[b]], ps[:, 0, b, :], ALU.subtract).then_inc(cen_s, 1)
            for b in range(BATCH):
                dve.wait_ge(std_s, base + b + 1)
                nc.vector.reciprocal(std[:, b, :], std[:, b, :]).then_inc(inv_s, 1)
                dve.wait_ge(inv_s, base + b + 1)
                nc.vector.tensor_tensor(dst[:, cols[b]], dst[:, cols[b]], std[:, b, :], ALU.mult).then_inc(out_s, 1)
            dve.wait_ge(out_s, base + BATCH)


def sign_ffn(nc, run, sem, XT, xn, dram):
    tag = f"f{run}"
    with ExitStack() as ctx:
        def sb(name, shape, dt=F32):
            return ctx.enter_context(nc.sbuf_tensor(f"{tag}_{name}", shape, dt))

        k0, k1, k2 = sb("k0", [P, 2, FF0], U8), sb("k1", [P, BLK, FF0], U8), sb("k2", [P, BLK, DIM], U8)
        w0, w1, w2 = sb("w0", [P, FF0]), sb("w1", [P, BLK, FF0]), sb("w2", [P, BLK, DIM])
        s_in, s_use = sb("s_in", [P, 3]), sb("s_use", [P, 3])
        h0, h1 = sb("h0", [P, 2, BLK, SEQ]), sb("h1", [P, 2, BLK, SEQ])
        ps = ctx.enter_context(nc.psum_tensor(f"{tag}_ps", [P, 8, SEQ], F32))
        loaded, diff, ready = sem("loaded"), sem("diff"), sem("ready")
        pe_0, pe_1, pe_2, act_0, act_1, dve_x = [sem(n) for n in ("pe_0", "pe_1", "pe_2", "act_0", "act_1", "dve_x")]
        block = ctx.enter_context(nc.Block())

        @block.sync
        def _(sp):
            for dst, src in ((k0, "k0"), (k1, "k1"), (k2, "k2")):
                sp.dma_start(dst[:].rearrange("p a b -> p (a b)"), dram[src]).then_inc(loaded, 16)
            sp.dma_start(s_in[:], dram["s"]).then_inc(loaded, 16)

        @block.tensor
        def _(pe):
            pe.wait_ge(ready, 5 * run + 5)
            for c in range(BATCH):
                n = run * BATCH + c
                for m in range(BLK):
                    if c:
                        pe.wait_ge(act_0, BLK * (n - 1) + m + 1)
                    nc.tensor.matmul(ps[:, m, :], w0[:, m * P:(m + 1) * P], xn[:, c * SEQ:(c + 1) * SEQ],
                                     start=True, stop=True).then_inc(pe_0, 1)
                pe.wait_ge(act_0, BLK * (n + 1))
                for m in range(BLK):
                    if BLK * c + m >= 2:
                        pe.wait_ge(act_1, BLK * n + m - 1)
                    for k in range(BLK):
                        last = nc.tensor.matmul(ps[:, 4 + m % 2, :], w1[:, k, m * P:(m + 1) * P], h0[:, c % 2, k, :],
                                                start=k == 0, stop=k == BLK - 1)
                    last.then_inc(pe_1, 1)
                pe.wait_ge(act_1, BLK * (n + 1))
                if c >= 2:
                    pe.wait_ge(dve_x, n - 1)
                for k in range(BLK):
                    last = nc.tensor.matmul(ps[:, 6 + c % 2, :], w2[:, k, :], h1[:, c % 2, k, :],
                                            start=k == 0, stop=k == BLK - 1)
                last.then_inc(pe_2, 1)

        @block.scalar
        def _(act):
            act.wait_ge(ready, 5 * run + 5)
            for c in range(BATCH):
                n = run * BATCH + c
                for m in range(BLK):
                    act.wait_ge(pe_0, BLK * n + m + 1)
                    nc.scalar.activation(h0[:, c % 2, m, :], ps[:, m, :], ACT.Relu, scale=s_use[:, 0:1]).then_inc(act_0, 1)
                for m in range(BLK):
                    act.wait_ge(pe_1, BLK * n + m + 1)
                    nc.scalar.activation(h1[:, c % 2, m, :], ps[:, 4 + m % 2, :], ACT.Relu,
                                         scale=s_use[:, 1:2]).then_inc(act_1, 1)

        @block.vector
        def _(dve):
            dve.wait_ge(loaded, 64 * run + 64)
            nc.vector.tensor_tensor(w0[:], k0[:, 0, :], k0[:, 1, :], ALU.subtract).then_inc(diff, 1)
            nc.vector.tensor_scalar(w1[:], k1[:], 2.0, -1.0, ALU.mult, ALU.add).then_inc(ready, 1)
            nc.vector.tensor_scalar(w2[:], k2[:], 2.0, -1.0, ALU.mult, ALU.add).then_inc(ready, 1)
            nc.vector.tensor_scalar(s_use[:, 0:2], s_in[:, 0:2], 2.0, None, ALU.mult).then_inc(ready, 1)
            nc.vector.tensor_scalar(s_use[:, 2:3], s_in[:, 2:3], 0.5, None, ALU.mult).then_inc(ready, 1)
            dve.wait_ge(diff, run + 1)
            nc.vector.tensor_scalar(w0[:], w0[:], 2.0, None, ALU.mult).then_inc(ready, 1)
            dve.wait_ge(ready, 5 * run + 5)
            for c in range(BATCH):
                n = run * BATCH + c
                cols = XT[:, c * SEQ:(c + 1) * SEQ]
                dve.wait_ge(pe_2, n + 1)
                nc.vector.scalar_tensor_tensor(cols, ps[:, 6 + c % 2, :], s_use[:, 2:3], cols,
                                               ALU.mult, ALU.add).then_inc(dve_x, 1)
            dve.wait_ge(dve_x, run * BATCH + BATCH)


def mixed_attention(nc, tag, XT, xn, consts, dram):
    ident, one = consts["ident"], consts["one"]
    UNITS = J0 * GROUPS
    LAG = 2
    with ExitStack() as ctx:
        def sb(name, shape, dt=F32):
            return ctx.enter_context(nc.sbuf_tensor(f"{tag}_{name}", shape, dt))

        def sem(name):
            return ctx.enter_context(nc.semaphore(f"{tag}_{name}"))

        w_in = sb("w_in", [P, 4, DIM])
        cs = sb("cs", [P, 2, D0 // 2])
        w_v = sb("w_v", [P, KB, QUADS, D0])
        b_v = sb("b_v", [P, KB, D0])
        w_o = sb("w_o", [P, J0, DIM])
        b_o = sb("b_o", [P, 1])
        sel = sb("sel", [P, P])
        prod = sb("prod", [P, 4, 4 * GROUPS, D0 // 2])
        w_r = sb("w_r", [P, 4, GROUPS, 32])
        b_r = sb("b_r", [P, 2, GROUPS])
        QT = sb("QT", [P, J0 * BATCH, GROUPS, TOK])
        KT = sb("KT", [P, J0 * BATCH, GROUPS, TOK])
        V = sb("V", [P, BATCH, H0, KB, D0 + 1])
        q_diag = sb("q_diag", [P, 2, GROUPS, QUADS, TOK])
        v_now = sb("v_now", [P, 2, QUADS, KB, D0 + 1])
        neg_max = sb("neg_max", [P, 4])
        probs = sb("probs", [P, 3, SEQ])
        pT = sb("pT", [P, KB, QUADS, GROUPS, TOK])
        oT = sb("oT", [P, SEQ])
        inv = sb("inv", [P, SEQ])
        ps = ctx.enter_context(nc.psum_tensor(f"{tag}_ps", [P, 8, SEQ], F32))
        loaded, cleared = sem("loaded"), sem("cleared")
        products, rotated, scaled = sem("products"), sem("rotated"), sem("scaled")
        pe_b, dve_b, pe_p, act_p, pe_v, dve_v = [sem(n) for n in ("pe_b", "dve_b", "pe_p", "act_p", "pe_v", "dve_v")]
        pool_in, pool_q, pe_s, dve_m, act_e, pe_t, dve_t = [sem(n) for n in ("pool_in", "pool_q", "pe_s", "dve_m", "act_e", "pe_t", "dve_t")]
        pe_o, act_o, pe_n, dve_r, dve_n, pe_y, dve_y = [
            sem(n) for n in ("pe_o", "act_o", "pe_n", "dve_r", "dve_n", "pe_y", "dve_y")]
        block = ctx.enter_context(nc.Block())
        S_BANKS, T_BANKS, O_BANK, N_BANK, Y_BANK = (0, 1, 2), (3, 4), 5, 6, 7
        V_BANKS = BATCH * H0 * KB * D0 // SEQ

        @block.sync
        def _(sp):
            for dst, name in ((w_in, "w_in"), (cs, "cs"), (w_o, "a_w_o")):
                sp.dma_start(dst[:].rearrange("p a b -> p (a b)"), dram[name]).then_inc(loaded, 16)
            sp.dma_start(w_v[:].rearrange("p a b c -> p (a b c)"), dram["w_v"]).then_inc(loaded, 16)
            sp.dma_start(b_v[:].rearrange("p a b -> p (a b)"), dram["b_v"]).then_inc(loaded, 16)
            sp.dma_start(b_o[:], dram["b_o"]).then_inc(loaded, 16)
            sp.dma_start(sel[:], dram["sel"]).then_inc(loaded, 16)

        xh = xn[:, 0:TOKENS].rearrange("p (bj r t) -> p bj r t", r=QUADS, t=TOK)

        @block.tensor
        def _(pe):
            pe.wait_ge(loaded, 7 * 16)
            pe.wait_ge(scaled, 1)
            pe.wait_ge(cleared, 2)
            for which in range(2):
                for g in range(GROUPS):
                    for r in range(QUADS):
                        col = which * GROUPS + g
                        last = nc.tensor.matmul(ps[32 * r:32 * r + 32, 6, col:col + 1], w_r[0:1, 2 + which, g, :],
                                                one[0:1, 0:1], start=True, stop=True, skip_group_check=True)
            last.then_inc(pe_b, 1)
            n = 0
            for which in range(2):
                for g in range(GROUPS):
                    if n >= 4:
                        pe.wait_ge(act_p, n - 3)
                    for r in range(QUADS):
                        last = nc.tensor.matmul(ps[32 * r:32 * r + 32, n % 4, :], w_r[:, which, g, :], xh[:, :, r, :],
                                                start=True, stop=True)
                    last.then_inc(pe_p, 1)
                    n += 1
            pe.wait_ge(act_p, 2 * GROUPS)
            for bh in range(BATCH * H0):
                for q in range(QUADS):
                    last = nc.tensor.matmul(
                        ps[32 * q:32 * q + 32, 0:V_BANKS, :].rearrange("p a (h d) -> p (a h) d", d=KB * D0)[:, bh, :],
                        xn[:, bh * TOK:(bh + 1) * TOK], w_v[:, :, q, :], start=True, stop=True,
                        skip_group_check=True)
            last.then_inc(pe_v, 1)
            pe.wait_ge(dve_v, 2)

            with pe.Fori(0, BATCH) as b:
                def finish(j):
                    n = b * J0 + j
                    pe.wait_ge(act_o, n + 1)
                    nc.tensor.matmul(ps[:, N_BANK, :], sel[:], oT[:], start=True, stop=True).then_inc(pe_n, 1)
                    pe.wait_ge(dve_n, n + 1)
                    nc.tensor.matmul(ps[:, Y_BANK, :], w_o[:, j, :], oT[:], start=j == 0,
                                     stop=j == J0 - 1).then_inc(pe_y, 1)

                for u in range(UNITS + LAG):
                    if u < UNITS:
                        j, g, n = u // GROUPS, u % GROUPS, b * UNITS + u
                        if g == 0:
                            pe.wait_ge(pool_in, b * J0 + j + 1)
                        if u >= 3:
                            pe.wait_ge(act_e, n - 2)
                        nc.tensor.matmul(ps[:, S_BANKS[u % 3], :],
                                         q_diag[:, j % 2, g, :, :].rearrange("p r t -> p (r t)"),
                                         KT[:, bass.ds(b * J0 + j, 1), :, :].rearrange("p a g t -> p (a g t)"),
                                         start=True, stop=True).then_inc(pe_s, 1)
                    if u >= LAG:
                        v_, j, g, n = u - LAG, (u - LAG) // GROUPS, (u - LAG) % GROUPS, b * UNITS + u - LAG
                        pe.wait_ge(act_e, n + 1)
                        if v_ >= 2:
                            pe.wait_ge(dve_t, n - 1)
                        for a in range(KB):
                            last = nc.tensor.transpose(ps[:, T_BANKS[v_ % 2], a * P:(a + 1) * P],
                                                       probs[:, v_ % 3, a * P:(a + 1) * P], ident[:])
                        last.then_inc(pe_t, 1)
                        if g == GROUPS - 1:
                            pe.wait_ge(dve_t, n + 1)
                            if j:
                                pe.wait_ge(act_o, b * J0 + j)
                            for a in range(KB):
                                for r in range(QUADS):
                                    last = nc.tensor.matmul(
                                        ps[32 * r:32 * r + D0 + 1, O_BANK, :], v_now[:, j % 2, r, a, :],
                                        pT[:, a, r, :, :].rearrange("p g t -> p (g t)"),
                                        start=a == 0, stop=a == KB - 1)
                            last.then_inc(pe_o, 1)
                        if g == 3 and j:
                            finish(j - 1)
                finish(J0 - 1)

        @block.scalar
        def _(act):
            act.wait_ge(dve_b, 1)
            for n in range(2 * GROUPS):
                act.wait_ge(pe_p, n + 1)
                which, g = n // GROUPS, n % GROUPS
                nc.scalar.activation((QT, KT)[which][:, :, g, :], ps[:, n % 4, :].rearrange("p (a t) -> p a t", t=TOK),
                                     ACT.Identity, bias=b_r[:, which, g:g + 1]).then_inc(act_p, 1)
            with act.Fori(0, BATCH) as b:
                for u in range(UNITS + 6):
                    if u < UNITS:
                        n = b * UNITS + u
                        act.wait_ge(dve_m, n + 1)
                        if u >= 3:
                            act.wait_ge(pe_t, n - 2)
                        nc.scalar.activation(probs[:, u % 3, :], ps[:, S_BANKS[u % 3], :], ACT.Exp,
                                             bias=neg_max[:, u % 4:u % 4 + 1]).then_inc(act_e, 1)
                    v_ = u - 4
                    if v_ >= 0 and v_ % GROUPS == GROUPS - 1:
                        j = v_ // GROUPS
                        if j < J0:
                            act.wait_ge(pe_o, b * J0 + j + 1)
                            if j:
                                act.wait_ge(pe_y, b * J0 + j)
                            nc.scalar.activation(oT[:], ps[:, O_BANK, :], ACT.Copy).then_inc(act_o, 1)

        @block.vector
        def _(dve):
            dve.wait_ge(loaded, 7 * 16)
            nc.vector.memset(w_r[:], 0.0)
            nc.vector.memset(ps[:, O_BANK, :], 0.0)
            nc.vector.memset(V[:].rearrange("p b h a d -> p (b h a) d")[:, :, D0:D0 + 1], 1.0).then_inc(cleared, 1)
            w = w_in[:].rearrange("p s (g c two) -> p (s g) c two", two=2, c=D0 // 2)
            re, im = w[:, :, :, 0], w[:, :, :, 1]
            shape = [P, 4 * GROUPS, D0 // 2]
            c, s = spread(cs[:, 0, :], 1, shape), spread(cs[:, 1, :], 1, shape)
            for i, (x, y) in enumerate(((re, c), (im, s), (re, s), (im, c))):
                nc.vector.tensor_tensor(prod[:, i, :, :], x, y, ALU.mult).then_inc(products, 1)
            dve.wait_ge(products, 4)
            dve.wait_ge(cleared, 2)
            out = w_r[:].rearrange("p s g (c two) -> p (s g) c two", two=2)[:, :, 0:D0 // 2, :]
            nc.vector.tensor_tensor(out[:, :, :, 0], prod[:, 0, :, :], prod[:, 1, :, :], ALU.subtract)
            nc.vector.tensor_tensor(out[:, :, :, 1], prod[:, 2, :, :], prod[:, 3, :, :], ALU.add).then_inc(rotated, 1)
            dve.wait_ge(rotated, 1)
            qs = w_r[:, 0:4:2, :, :]
            nc.vector.tensor_scalar(qs, qs, 1.0 / float(np.sqrt(D0)), None, ALU.mult).then_inc(scaled, 1)
            dve.wait_ge(pe_b, 1)
            nc.vector.tensor_copy(b_r[:].rearrange("p a g -> p (a g)"), ps[:, 6, 0:2 * GROUPS]).then_inc(dve_b, 1)
            dve.wait_ge(pe_v, 1)
            for b in range(0, BATCH, 2):
                nc.vector.tensor_tensor(
                    V[:, b:b + 2, :, :, 0:D0].rearrange("p b h a d -> p (b h) a d"),
                    ps[:, b:b + 2, :].rearrange("p b (h a d) -> p (b h) a d", a=KB, d=D0),
                    spread(b_v[:], 1, [P, 2 * H0, KB, D0]), ALU.add).then_inc(dve_v, 1)
            with dve.Fori(0, BATCH) as b:
                def normalise(j):
                    n = b * J0 + j
                    dve.wait_ge(pe_n, n + 1)
                    nc.vector.reciprocal(inv[:], ps[:, N_BANK, :]).then_inc(dve_r, 1)
                    dve.wait_ge(dve_r, n + 1)
                    nc.vector.tensor_tensor(oT[:], oT[:], inv[:], ALU.mult).then_inc(dve_n, 1)

                for u in range(UNITS + LAG):
                    if u < UNITS:
                        n = b * UNITS + u
                        dve.wait_ge(pe_s, n + 1)
                        if u >= 4:
                            dve.wait_ge(act_e, n - 3)
                        nc.vector.tensor_reduce(neg_max[:, u % 4:u % 4 + 1], ps[:, S_BANKS[u % 3], :], AXX, ALU.max,
                                                negate=True).then_inc(dve_m, 1)
                    if u >= LAG:
                        v_, g, j = u - LAG, (u - LAG) % GROUPS, (u - LAG) // GROUPS
                        dve.wait_ge(pe_t, b * UNITS + v_ + 1)
                        if g == 0 and j:
                            dve.wait_ge(pe_o, b * J0 + j)
                        nc.vector.tensor_copy(pT[:, :, :, g, :],
                                              ps[:, T_BANKS[v_ % 2], :].rearrange("p (a r t) -> p a r t", r=QUADS, t=TOK)
                                              ).then_inc(dve_t, 1)
                        if g == 3 and j:
                            normalise(j - 1)
                normalise(J0 - 1)
                dve.wait_ge(pe_y, b * J0 + J0)
                cols = XT[:, bass.ds(b * SEQ, SEQ)].rearrange("p (t g) -> p g t", g=GROUPS)
                nc.vector.scalar_tensor_tensor(cols, ps[:, Y_BANK, :].rearrange("p (g t) -> p g t", t=TOK), b_o[:, 0:1],
                                               cols, ALU.add, ALU.add).then_inc(dve_y, 1)
            dve.wait_ge(dve_y, BATCH)

        @block.gpsimd
        def _(pool):
            nc.gpsimd.memset(q_diag[:].rearrange("p a g r t -> p (a g r t)"), 0.0).then_inc(cleared, 1)
            pool.wait_ge(cleared, 2)
            pool.wait_ge(act_p, 2 * GROUPS)
            pool.wait_ge(dve_v, 2)

            def feed(b, j):
                if j >= 2 or not isinstance(b, int):
                    pool.wait_ge(pe_o, b * J0 + j - 1)
                for r in range(QUADS):
                    nc.gpsimd.tensor_copy(q_diag[32 * r:32 * r + 32, j % 2, :, r, :],
                                          QT[32 * r:32 * r + 32, bass.ds(b * J0 + j, 1), :, :]
                                          .rearrange("p a g t -> p (a g) t")).then_inc(pool_q, 1)
                    pool.wait_ge(pool_q, (b * J0 + j) * QUADS + r + 1)
                nc.gpsimd.tensor_copy(
                    v_now[:, j % 2, :, :, :].rearrange("p r a d -> p (r a) d"),
                    V[:, bass.ds(b, 1), j * QUADS:(j + 1) * QUADS, :, :].rearrange("p b r a d -> p (b r a) d")
                ).then_inc(pool_in, 1)

            for j in range(J0):
                feed(0, j)
            with pool.Fori(1, BATCH) as b:
                for j in range(J0):
                    feed(b, j)


def mixed_weights(i):
    A = lambda n: np.asarray(i[f"L0_attn_{n}"])
    rows = lambda v: np.broadcast_to(v.reshape(1, -1), (P, v.size))
    w_o = np.zeros((QUADS, 32, J0, DIM), np.float32)
    w_o[:, :D0] = A("wo").T.reshape(J0, QUADS, D0, DIM).transpose(1, 2, 0, 3)
    sel = np.zeros((P, P), np.float32)
    sel[32 * (np.arange(P) // 32) + D0, np.arange(P)] = 1.0
    b_v = np.repeat(A("bv").reshape(KB, QUADS, D0).transpose(1, 0, 2), TOK, axis=0)
    out = {
        "w_in": np.concatenate([A("wq").T, A("wk").T, rows(A("bq")), rows(A("bk"))], 1),
        "cs": np.concatenate([rows(A("rot_cos")[-1]), rows(A("rot_sin")[-1])], 1),
        "w_v": A("wv").T, "b_v": b_v.reshape(P, -1), "a_w_o": w_o.reshape(P, -1), "b_o": A("bo")[:, None], "sel": sel,
    }
    return {k: np.ascontiguousarray(v) for k, v in out.items()}


def sign_weights(i):
    A = lambda n: np.asarray(i[f"L0_ffn_{n}"])
    tall = lambda k: k.reshape(-1, P, k.shape[1]).transpose(1, 0, 2).reshape(P, -1)
    scales = np.stack([A("s0"), A("s1"), A("s2")]).reshape(1, 3)
    out = {"k0": tall(A("k0")), "k1": tall(A("k1")), "k2": tall(A("k2")), "s": np.broadcast_to(scales, (P, 3))}
    return {k: np.ascontiguousarray(v) for k, v in out.items()}


CH, HD = 64, 8
DD = DIM // HD
HQ = 4
NT = TOKENS // P
CHUNKS = SEQ // CH
LEVELS = (2, 4, 8, 16, 32)


def delta_memory(nc, tag, XT, xn, consts, dram):
    ident = consts["ident"]
    NL = len(LEVELS)
    with ExitStack() as ctx:
        def sb(name, shape, dt=F32):
            return ctx.enter_context(nc.sbuf_tensor(f"{tag}_{name}", shape, dt))

        def sem(name):
            return ctx.enter_context(nc.semaphore(f"{tag}_{name}"))

        w_vb = sb("w_vb", [P, DIM + HD])
        w_read = sb("w_read", [P, DIM])
        rate = sb("rate", [P, HD])
        table = sb("table", [P, 4, P])
        levels = sb("levels", [P, 2 + NL, P])
        small = sb("small", [P, 2 + HQ + HQ * DD])
        rateP = sb("rateP", [P, 2])
        beta, nbeta = sb("beta", [P, NT, HD]), sb("nbeta", [P, NT, HD])
        dec_raw = sb("dec_raw", [P, 2, HD])
        dec = sb("dec", [P, 2, HD])
        bdec = sb("bdec", [P, NT, HD])
        total = sb("total", [P, 2])
        L = sb("L", [P, 2, HD, P])
        sums, rinv = sb("sums", [P, NT * HD]), sb("rinv", [P, NT * HD])
        rkT = sb("rkT", [P, 2, BATCH, SEQ + 1])
        wk_dw = sb("wk_dw", [P, NT, HD, 32])
        Vt = sb("Vt", [P, NT, HD, DD])
        U = Vt[:].rearrange("p t h d -> p t (h d)")
        attnT = sb("attnT", [P, NT, HD, P])
        wks = sb("wks", [P, 2, P])
        rws = sb("rws", [P, HD, 32])
        wrk_bd = sb("wrk_bd", [P, 2, 2, HQ, P])
        wk_bd, rk_bd = wrk_bd[:, 0], wrk_bd[:, 1]
        nbL = sb("nbL", [P, 2, HQ, P])
        N_, N_T = nbL, sb("N_T", [P, 2, HQ, P])
        T_, T_T = sb("T_", [P, 2, HQ, P]), sb("T_T", [P, 2, HQ, P])
        M_T, W_ = sb("M_T", [P, 2, HQ, P]), sb("W_", [P, 2, HQ, P])
        S = M_T[:, 0].rearrange("p h q -> p (h q)").rearrange("p (k d) -> p k d", d=HQ * DD)
        S_new = M_T[:, 1].rearrange("p h q -> p (h q)").rearrange("p (k d) -> p k d", d=HQ * DD)
        O = wrk_bd[:].rearrange("p a q h t -> p (a q h t)").rearrange("p (t d) -> p t d", d=DIM)
        OT = [buf[:, i].rearrange("p h q -> p (h q)") for buf in (T_, T_T) for i in range(2)]
        flat = attnT[:].rearrange("p t h q -> p (t h q)")
        xtok = flat[:, 0:2048]
        sqs = flat[:, 2048:4096]
        rk_pad = flat[:, 4096:8192].rearrange("p (t h d) -> p t h d", h=HD, d=32)
        Rw = sb("Rw", [P, NT, HD, 32])
        WT = Rw[:].rearrange("p t h d -> p t (h d)").rearrange("p t (q i) -> p t q i", q=2)

        ps = ctx.enter_context(nc.psum_tensor(f"{tag}_ps", [P, 8, 512], F32))
        mk = lambda names: [sem(n) for n in names.split()]
        loaded, cleared, done = mk("loaded cleared done")
        pe_a, act_a, dve_a = mk("pe_a act_a dve_a")
        act_s, pool_bd, pool_nb, dve_N, pe_nt, act_nt = mk("act_s pool_bd pool_nb dve_N pe_nt act_nt")
        pe_g, pe_at, dve_at, pool_t, pool_m, pool_nb2 = mk("pe_g pe_at dve_at pool_t pool_m pool_nb2")
        pe_w, act_w, pe_d, dve_t, pe_u, act_u = mk("pe_w act_w pe_d dve_t pe_u act_u")
        pe_ws, dve_vn, pe_su, dve_s, dve_o, dve_tmp = mk("pe_ws dve_vn pe_su dve_s dve_o dve_tmp")
        pe_av, dve_av, pe_ot, act_ot, pe_y, dve_y = mk("pe_av dve_av pe_ot act_ot pe_y dve_y")
        block = ctx.enter_context(nc.Block())
        row = lambda i: table[:, i, :]

        @block.sync
        def _(sp):
            for dst, name in ((w_vb, "w_vb"), (w_read, "w_read"), (rate, "rate"), (small, "small"), (rateP, "rateP")):
                sp.dma_start(dst[:], dram[name]).then_inc(loaded, 16)
            sp.dma_start(table[:].rearrange("p a b -> p (a b)"), dram["table"]).then_inc(loaded, 16)
            sp.dma_start(levels[:].rearrange("p a b -> p (a b)"), dram["levels"]).then_inc(loaded, 16)

        heads4 = lambda ap: ap.rearrange("p h q -> p (h q)")

        @block.tensor
        def _(pe):
            for t in range(NT):
                last = nc.tensor.transpose(ps[:, t // 4, (t % 4) * P:(t % 4 + 1) * P], xn[:, t * P:(t + 1) * P], ident[:])
            last.then_inc(pe_a, 1)
            pe.wait_ge(loaded, 7 * 16)
            for t in range(NT):
                last = nc.tensor.matmul(ps[:, 7, t * HD:(t + 1) * HD], xn[:, t * P:(t + 1) * P], w_vb[:, DIM:],
                                        start=True, stop=True, skip_group_check=True)
            last.then_inc(pe_a, 1)
            pe.wait_ge(act_a, 2)
            for t in range(NT):
                last = nc.tensor.matmul(ps[:, t // 4, (t % 4) * P:(t % 4 + 1) * P], xn[:, t * P:(t + 1) * P], w_vb[:, 0:DIM],
                                        start=True, stop=True, skip_group_check=True)
            last.then_inc(pe_a, 1)
            pe.wait_ge(dve_a, 2)
            pe.wait_ge(dve_tmp, 6)
            for q in range(2):
                for t in range(NT):
                    last = nc.tensor.transpose(ps[:, q * 4 + t // 4, (t % 4) * P:(t % 4 + 1) * P],
                                               rk_pad[:, t, q * HQ:(q + 1) * HQ, :].rearrange("p h d -> p (h d)"), ident[:])
            last.then_inc(pe_a, 1)
            pe.wait_ge(act_a, 6)
            for t in range(NT):
                for q in range(2):
                    last = nc.tensor.transpose(ps[:, t // 2, (t % 2) * 256 + q * P:(t % 2) * 256 + (q + 1) * P],
                                               rkT[:, q, t // TILES, (t % TILES) * P:(t % TILES + 1) * P], ident[:])
            last.then_inc(pe_a, 1)
            pe.wait_ge(dve_a, 4)

            with pe.Fori(0, NT) as n:
                for q in range(2):
                    pe.wait_ge(act_s, n + 1)
                    pe.wait_ge(pool_bd, n * 4 + 2 * q + 2)
                    nc.tensor.matmul(ps[:, 4 * q, :], wks[:, q, :], heads4(wk_bd[:, q]), start=True, stop=True).then_inc(pe_g, 1)
                    nc.tensor.matmul(ps[:, 4 * q + 1, :], wks[:, q, :], heads4(rk_bd[:, q]), start=True,
                                     stop=True).then_inc(pe_at, 1)
                for q in range(2):
                    pe.wait_ge(dve_N, n * 2 + q + 1)
                    for h in range(HQ):
                        last = nc.tensor.transpose(ps[:, 4 * q + 2, h * P:(h + 1) * P], N_[:, q, h, :], ident[:])
                    last.then_inc(pe_nt, 1)
                for l in range(NL):
                    at = lambda q: (n * NL + l) * 2 + q + 1
                    for q in range(2):
                        pe.wait_ge(pool_m, at(q))
                        pe.wait_ge(pool_t, n * 2 + q + 1)
                        if l:
                            pe.wait_ge(dve_t, at(q) - 2)
                        for h in range(HQ):
                            last = nc.tensor.matmul(ps[:, 4 * q + 2, h * P:(h + 1) * P], M_T[:, q, h, :], T_[:, q, h, :],
                                                    start=True, stop=True, skip_group_check=True)
                        last.then_inc(pe_w, 1)
                    for q in range(2):
                        pe.wait_ge(act_w, at(q))
                        if l == 0:
                            pe.wait_ge(dve_at, n * 2 + q + 1)
                        for h in range(HQ):
                            cols = slice(h * P, (h + 1) * P)
                            if l < NL - 1:
                                nc.tensor.matmul(ps[:, 4 * q, cols], T_T[:, q, h, :], W_[:, q, h, :],
                                                 start=True, stop=True, skip_group_check=True)
                            last = nc.tensor.matmul(ps[:, 4 * q + 1, cols], W_[:, q, h, :], T_T[:, q, h, :],
                                                    start=True, stop=True, skip_group_check=True)
                        last.then_inc(pe_d, 1)
                for q in range(2):
                    pe.wait_ge(dve_t, (n * NL + NL - 1) * 2 + q + 1)
                    for h in range(HQ):
                        nc.tensor.matmul(ps[:, 4 * q + 3, h * DD:(h + 1) * DD], T_T[:, q, h, :],
                                         Vt[:, bass.ds(n, 1), q * HQ + h, :].rearrange("p a d -> p (a d)"),
                                         start=True, stop=True, skip_group_check=True)
                    for h in range(HQ):
                        last = nc.tensor.matmul(ps[32 * h:32 * h + 32, 4 * q + 3, P:2 * P], rws[:, q * HQ + h, :],
                                                T_T[:, q, h, :], start=True, stop=True, skip_group_check=True)
                    last.then_inc(pe_u, 1)

            pe.wait_ge(act_u, 4 * NT + 1)
            for c in range(CHUNKS):
                r = slice(CH * (c % 2), CH * (c % 2) + CH)
                if c:
                    pe.wait_ge(dve_s, c)
                    for b in range(BATCH):
                        for q in range(2):
                            k = 2 * b + q
                            cols = slice(k * HQ * DD, (k + 1) * HQ * DD)
                            nc.tensor.matmul(ps[r, c % 2, cols], WT[:, b * TILES + c // 2, q, r], S[:, k, :],
                                             start=True, stop=True, skip_group_check=True)
                            last = nc.tensor.matmul(ps[r, 2 + c % 2, cols], rkT[:, q, b, 1 + c * CH:1 + (c + 1) * CH],
                                                    S[:, k, :], start=True, stop=True, skip_group_check=True)
                    last.then_inc(pe_ws, 1)
                    pe.wait_ge(dve_vn, c)
                if c < CHUNKS - 1:
                    for b in range(BATCH):
                        for q in range(2):
                            k = 2 * b + q
                            last = nc.tensor.matmul(ps[:, 4, k * HQ * DD:(k + 1) * HQ * DD],
                                                    wk_dw[r, b * TILES + c // 2, q * HQ:(q + 1) * HQ, :].rearrange("p h d -> p (h d)"),
                                                    U[r, b * TILES + c // 2, q * HQ * DD:(q + 1) * HQ * DD],
                                                    start=True, stop=True, skip_group_check=True)
                    last.then_inc(pe_su, 1)
            pe.wait_ge(dve_o, CHUNKS - 1)
            for g in range(BATCH):
                for t in range(g * 4, g * 4 + 4):
                    for h in range(HD):
                        last = nc.tensor.matmul(ps[:, g, (t % 4) * P + h * DD:(t % 4) * P + (h + 1) * DD], attnT[:, t, h, :],
                                                U[:, t, h * DD:(h + 1) * DD], start=True, stop=True, skip_group_check=True)
                last.then_inc(pe_av, 1)
            for g in range(BATCH):
                pe.wait_ge(dve_av, g + 1)
                for t in range(g * 4, g * 4 + 4):
                    last = nc.tensor.transpose(ps[:, 4 + g % 2, (t % 4) * P:(t % 4 + 1) * P], O[:, t, :], ident[:])
                last.then_inc(pe_ot, 1)
                pe.wait_ge(act_ot, g + 1)
                if g >= 2:
                    pe.wait_ge(dve_y, g - 1)
                nc.tensor.matmul(ps[:, 6 + g % 2, :], w_read[:], OT[g],
                                 start=True, stop=True).then_inc(pe_y, 1)

        @block.scalar
        def _(act):
            act.wait_ge(loaded, 7 * 16)
            act.wait_ge(pe_a, 1)
            nc.scalar.activation(sqs, ps[:, 0:4, :].rearrange("p a b -> p (a b)"), ACT.Square).then_inc(act_a, 1)
            nc.scalar.activation(xtok, ps[:, 0:4, :].rearrange("p a b -> p (a b)"), ACT.Copy).then_inc(act_a, 1)
            act.wait_ge(dve_a, 1)
            nc.scalar.activation(sums[:], sums[:], ACT.Sqrt).then_inc(act_a, 1)
            act.wait_ge(pe_a, 2)
            nc.scalar.activation(beta[:].rearrange("p t h -> p (t h)"), ps[:, 7, 0:NT * HD], ACT.Sigmoid).then_inc(act_a, 1)
            nc.scalar.activation(rate[:], rate[:], ACT.Sigmoid).then_inc(done, 1)
            nc.scalar.activation(rateP[:], rateP[:], ACT.Sigmoid).then_inc(done, 1)
            act.wait_ge(done, 2)
            nc.scalar.activation(rate[:], rate[:], ACT.Ln).then_inc(done, 1)
            nc.scalar.activation(rateP[:], rateP[:], ACT.Ln).then_inc(done, 1)
            act.wait_ge(done, 4)
            for k in range(2):
                for h in range(HD):
                    nc.scalar.activation(L[:, k, h, :], row(k), ACT.Exp, scale=rate[:, h:h + 1]).then_inc(done, 1)
            nc.scalar.activation(total[:], rateP[:], ACT.Exp, scale=float(CH)).then_inc(act_a, 1)
            act.wait_ge(dve_a, 3)
            nc.scalar.activation(dec[:].rearrange("p a h -> p (a h)"), dec_raw[:].rearrange("p a h -> p (a h)"),
                                 ACT.Exp).then_inc(done, 1)
            act.wait_ge(pe_a, 4)
            act.wait_ge(cleared, 2)
            for q in range(2):
                last = nc.scalar.activation(rkT[:, q, :, 1:SEQ + 1], ps[:, 4 * q:4 * q + 4, :], ACT.Copy)
            last.then_inc(act_a, 1)
            act.wait_ge(dve_a, 4)
            nc.scalar.activation(wks[:], wks[:], ACT.Copy).then_inc(act_u, 1)
            with act.Fori(0, BATCH) as b:
                for t in range(TILES):
                    n = b * TILES + t
                    act.wait_ge(act_u, n * 4 + 1)
                    nc.scalar.activation(wks[:], rkT[:, :, bass.ds(b, 1), t * P:(t + 1) * P]
                                         .rearrange("p q a t -> p (q a) t"), ACT.Copy)
                    nc.scalar.activation(rws[:].rearrange("p h d -> p (h d)"), Rw[:, bass.ds(n, 1), :, :]
                                         .rearrange("p a h d -> p (a h d)"), ACT.Copy).then_inc(act_s, 1)
                    for q in range(2):
                        act.wait_ge(pe_nt, n * 2 + q + 1)
                        nc.scalar.activation(heads4(N_T[:, q]), ps[:, 4 * q + 2, :], ACT.Copy).then_inc(act_nt, 1)
                    for l in range(NL):
                        for q in range(2):
                            act.wait_ge(pe_w, (n * NL + l) * 2 + q + 1)
                            nc.scalar.activation(heads4(W_[:, q]), ps[:, 4 * q + 2, :], ACT.Copy).then_inc(act_w, 1)
                    for q in range(2):
                        act.wait_ge(pe_u, n * 2 + q + 1)
                        nc.scalar.activation(U[:, bass.ds(n, 1), q * 64:(q + 1) * 64].rearrange("p a d -> p (a d)"),
                                             ps[:, 4 * q + 3, 0:64], ACT.Copy).then_inc(act_u, 1)
                        nc.scalar.activation(WT[:, bass.ds(n, 1), q, :].rearrange("p a d -> p (a d)"),
                                             ps[:, 4 * q + 3, P:2 * P], ACT.Copy).then_inc(act_u, 1)
            for g in range(BATCH):
                act.wait_ge(pe_ot, g + 1)
                nc.scalar.activation(OT[g], ps[:, 4 + g % 2, :],
                                     ACT.Copy).then_inc(act_ot, 1)

        @block.vector
        def _(dve):
            nc.vector.memset(rkT[:].rearrange("p q b t -> p (q b) t")[:, :, 0:1], 0.0)
            nc.vector.memset(rk_pad, 0.0).then_inc(cleared, 1)
            dve.wait_ge(act_a, 1)
            nc.vector.reduce_sum(sums[:], sqs.rearrange("p (g d) -> p g d", d=DD), AXX).then_inc(dve_a, 1)
            dve.wait_ge(act_a, 3)
            nc.vector.tensor_scalar_max(sums[:], sums[:], 1e-12).then_inc(dve_tmp, 1)
            dve.wait_ge(dve_tmp, 1)
            nc.vector.reciprocal(rinv[:], sums[:]).then_inc(dve_tmp, 1)
            dve.wait_ge(dve_tmp, 2)
            dve.wait_ge(cleared, 2)
            nc.vector.tensor_tensor(rk_pad[:, :, :, 0:DD].rearrange("p t h d -> p (t h) d"),
                                    xtok.rearrange("p (g d) -> p g d", d=DD),
                                    spread(rinv[:], 2, [P, NT * HD, DD]), ALU.mult).then_inc(dve_a, 1)
            dve.wait_ge(done, 4)
            for k in range(2):
                last = nc.vector.tensor_scalar(dec_raw[:, k, :], rate[:], small[:, k:k + 1], None, ALU.mult)
            last.then_inc(dve_a, 1)
            dve.wait_ge(done, 4 + 2 * HD)
            for k in range(2):
                nc.vector.tensor_tensor(L[:, k, :, :], L[:, k, :, :], spread(row(2 + k), 1, [P, HD, P]),
                                        ALU.mult).then_inc(dve_tmp, 1)
            dve.wait_ge(act_a, 4)
            nc.vector.tensor_scalar(nbeta[:], beta[:], -1.0, None, ALU.mult).then_inc(dve_tmp, 1)
            dve.wait_ge(pe_a, 3)
            nc.vector.tensor_tensor(Vt[:].rearrange("p t h d -> p (t h) d"),
                                    ps[:, 0:4, :].rearrange("p a (g d) -> p (a g) d", d=DD),
                                    spread(beta[:].rearrange("p t h -> p (t h)"), 2, [P, NT * HD, DD]),
                                    ALU.mult).then_inc(dve_tmp, 1)
            dve.wait_ge(done, 5 + 2 * HD)
            nc.vector.tensor_tensor(bdec[:], beta[:], spread(dec[:, 0, :], 1, [P, NT, HD]), ALU.mult).then_inc(dve_tmp, 1)
            dve.wait_ge(dve_tmp, 7)
            dve.wait_ge(pe_a, 5)
            wk = ps[:, :, :].rearrange("p a (t h d) -> p (a t) h d", h=HD, d=32)
            for t in range(NT):
                nc.vector.tensor_tensor(wk_dw[:, t], wk[:, t], spread(dec[:, 1, :], 2, [P, HD, 32]), ALU.mult)
                last = nc.vector.tensor_tensor(Rw[:, t], wk[:, t], spread(bdec[:, t, :], 2, [P, HD, 32]), ALU.mult)
            last.then_inc(dve_a, 1)
            with dve.Fori(0, NT) as n:
                for q in range(2):
                    dve.wait_ge(pe_g, n * 2 + q + 1)
                    dve.wait_ge(pool_nb, n * 2 + q + 1)
                    nc.vector.tensor_tensor(heads4(N_[:, q]), ps[:, 4 * q, :], heads4(nbL[:, q]), ALU.mult).then_inc(dve_N, 1)
                for q in range(2):
                    dve.wait_ge(pe_at, n * 2 + q + 1)
                    nc.vector.tensor_tensor(attnT[:, bass.ds(n, 1), q * HQ:(q + 1) * HQ, :].rearrange("p a h t -> p (a h t)"),
                                            ps[:, 4 * q + 1, :], heads4(L[:, 1, q * HQ:(q + 1) * HQ, :]),
                                            ALU.mult).then_inc(dve_at, 1)
                for l in range(NL):
                    for q in range(2):
                        dve.wait_ge(pe_d, (n * NL + l) * 2 + q + 1)
                        if l < NL - 1:
                            nc.vector.tensor_tensor(heads4(T_[:, q]), heads4(T_[:, q]), ps[:, 4 * q, :], ALU.add)
                        nc.vector.tensor_tensor(heads4(T_T[:, q]), heads4(T_T[:, q]), ps[:, 4 * q + 1, :],
                                                ALU.add).then_inc(dve_t, 1)
            dve.wait_ge(act_u, 4 * NT + 1)
            tiles = lambda ap, c: ap.rearrange("p (b t) d -> p b t d", t=TILES)[CH * (c % 2):CH * (c % 2) + CH, :, c // 2, :]
            blocks = spread(small[:, 2 + HQ:], 1, [P, 2 * BATCH, HQ * DD])
            for c in range(CHUNKS):
                r = slice(CH * (c % 2), CH * (c % 2) + CH)
                if c:
                    dve.wait_ge(pe_ws, c)
                    nc.vector.tensor_tensor(tiles(U, c), tiles(U, c), ps[r, c % 2, :].rearrange("p (b d) -> p b d", b=BATCH),
                                            ALU.subtract).then_inc(dve_vn, 1)
                    for b in range(BATCH):
                        last = nc.vector.tensor_tensor(
                            O[r, b * TILES + c // 2, :].rearrange("p (h d) -> p h d", d=DD),
                            ps[r, 2 + c % 2, b * P:(b + 1) * P].rearrange("p (h d) -> p h d", d=DD),
                            spread(dec[r, 0, :], 2, [CH, HD, DD]), ALU.mult)
                    last.then_inc(dve_o, 1)
                else:
                    last = nc.vector.memset(tiles(O, c), 0.0)
                if c < CHUNKS - 1:
                    dve.wait_ge(pe_su, c + 1)
                    if c:
                        nc.vector.tensor_tensor(S_new, ps[:, 4, :].rearrange("p (k d) -> p k d", d=HQ * DD), blocks,
                                                ALU.mult).then_inc(dve_tmp, 1)
                        dve.wait_ge(dve_tmp, 7 + c)
                        for q in range(2):
                            last = nc.vector.scalar_tensor_tensor(S[:, q::2, :], S[:, q::2, :], total[:, q:q + 1],
                                                                  S_new[:, q::2, :], ALU.mult, ALU.add)
                        last.then_inc(dve_s, 1)
                    else:
                        nc.vector.tensor_tensor(S, ps[:, 4, :].rearrange("p (k d) -> p k d", d=HQ * DD), blocks,
                                                ALU.mult).then_inc(dve_s, 1)
            for g in range(BATCH):
                dve.wait_ge(pe_av, g + 1)
                dve.wait_ge(dve_o, CHUNKS - 1)
                og = O[:, g * 4:g * 4 + 4, :].rearrange("p t d -> p (t d)")
                nc.vector.tensor_tensor(og, og, ps[:, g, :], ALU.add).then_inc(dve_av, 1)
            for g in range(BATCH):
                dve.wait_ge(pe_y, g + 1)
                cols = slice(g * SEQ, (g + 1) * SEQ)
                nc.vector.tensor_tensor(XT[:, cols], XT[:, cols], ps[:, 6 + g % 2, :], ALU.add).then_inc(dve_y, 1)
                dve.wait_ge(dve_y, g + 1)
                nc.vector.tensor_tensor(XT[:, cols], XT[:, cols], xn[:, cols], ALU.add).then_inc(dve_tmp, 1)
            dve.wait_ge(dve_tmp, 7 + CHUNKS - 2 + BATCH)

        @block.gpsimd
        def _(pool):
            nc.gpsimd.memset(wks[:], 0.0).then_inc(cleared, 1)
            pool.wait_ge(dve_a, 4)
            half_mask = small[:, 2:2 + HQ]
            with pool.Fori(0, BATCH) as b:
                for t in range(TILES):
                    n = b * TILES + t
                    for q in range(2):
                        pool.wait_ge(act_u, n * 4 + 1)
                        nc.gpsimd.tensor_tensor(nbL[:, q], L[:, 0, q * HQ:(q + 1) * HQ, :],
                                                spread(nbeta[:, bass.ds(n, 1), q * HQ:(q + 1) * HQ]
                                                       .rearrange("p a h -> p (a h)"), 2, [P, HQ, P]), ALU.mult).then_inc(pool_nb, 1)
                        for bd, off in ((wk_bd, 0), (rk_bd, 1)):
                            src = rkT[:, q, bass.ds(b, 1), t * P + off:(t + 1) * P + off].rearrange("p a t -> p (a t)")
                            nc.gpsimd.tensor_tensor(bd[:, q], spread(src, 1, [P, HQ, P]), spread(half_mask, 2, [P, HQ, P]),
                                                    ALU.mult).then_inc(pool_bd, 1)
                    for q in range(2):
                        pool.wait_ge(dve_N, n * 2 + q + 1)
                        nc.gpsimd.tensor_tensor(T_[:, q], N_[:, q], spread(levels[:, 0, :], 1, [P, HQ, P]), ALU.mult).then_inc(pool_nb2, 1)
                        pool.wait_ge(act_nt, n * 2 + q + 1)
                        nc.gpsimd.tensor_tensor(T_T[:, q], N_T[:, q], spread(levels[:, 1, :], 1, [P, HQ, P]), ALU.mult).then_inc(pool_nb2, 1)
                        pool.wait_ge(pool_nb2, (n * 2 + q) * 3 + 2)
                        nc.gpsimd.tensor_tensor(T_[:, q], T_[:, q], spread(ident[:], 1, [P, HQ, P]), ALU.add).then_inc(pool_nb2, 1)
                        nc.gpsimd.tensor_tensor(T_T[:, q], T_T[:, q], spread(ident[:], 1, [P, HQ, P]), ALU.add).then_inc(pool_t, 1)
                    for l in range(NL):
                        for q in range(2):
                            if l:
                                pool.wait_ge(pe_w, (n * NL + l - 1) * 2 + q + 1)
                            nc.gpsimd.tensor_tensor(M_T[:, q], N_T[:, q], spread(levels[:, 2 + l, :], 1, [P, HQ, P]),
                                                    ALU.mult).then_inc(pool_m, 1)


def delta_weights(i):
    A = lambda n: np.asarray(i[f"L1_attn_{n}"])
    p = np.arange(P)
    pos, chunk = p % CH, p // CH
    same = chunk[:, None] == chunk[None, :]
    d = (pos[:, None] - pos[None, :]).astype(np.float32)
    low, strict = same & (d >= 0), same & (d > 0)
    table = [np.where(strict, d, 0), np.where(low, d, 0).T, strict, low.T]

    def level(s):
        return same & (pos[:, None] // (2 * s) == pos[None, :] // (2 * s)) \
            & (pos[:, None] // s % 2 == 1) & (pos[None, :] // s % 2 == 0)
    levels = [level(1), level(1).T] + [level(s).T for s in LEVELS]
    head = p // 32
    small = [pos[:, None] + 1, CH - 1 - pos[:, None], head[:, None] == np.arange(HQ)[None, :],
             head[:, None] == (np.arange(HQ * DD) // DD)[None, :]]
    f = lambda parts: np.concatenate([np.asarray(x, np.float32) for x in parts], 1)
    decay = A("decay")
    out = {
        "w_vb": np.concatenate([A("W_write").T, A("W_beta").T], 1), "w_read": A("W_read").T,
        "rate": np.broadcast_to(decay[None], (P, HD)), "rateP": decay.reshape(2, HQ).T[head],
        "table": f(table), "levels": f(levels), "small": f(small),
    }
    return {k: np.ascontiguousarray(v) for k, v in out.items()}


def half_sum(nc, run, added, XT, ZT):
    with nc.Block() as block:
        @block.vector
        def _(dve):
            nc.vector.scalar_tensor_tensor(XT[:], ZT[:, 0:TOKENS], 0.5, XT[:], ALU.mult, ALU.add).then_inc(added, 1)
            dve.wait_ge(added, run + 1)


def build(nc, dram, out):
    with ExitStack() as ctx:
        def sb(name, shape, dt=F32):
            return ctx.enter_context(nc.sbuf_tensor(name, shape, dt))

        XT, ZT = sb("XT", [P, TOKENS]), sb("ZT", [P, TOKENS + P])
        ident, ident_b, mean_w = sb("ident", [P, P]), sb("ident_b", [P, P], BF16), sb("mean_w", [P, P])
        mask_in, mask = sb("mask_in", [P, 2, KEYS]), sb("mask", [P, 2, KEYS], BF16)
        eps, one = sb("eps", [P, 1]), sb("one", [P, 1])
        loaded, ready, stored, added = [
            ctx.enter_context(nc.semaphore(n)) for n in ("loaded", "ready", "stored", "added")]
        norm_sems, sign_sems, window_sems = [Semaphores(nc, ctx, s) for s in ("norm", "sign", "window")]

        with nc.Block() as block:
            @block.sync
            def _(sp):
                sp.dma_start(XT[:], dram["x"]).then_inc(loaded, 16)
                sp.dma_start(ident[:], dram["ident"]).then_inc(loaded, 16)
                sp.dma_start(mask_in[:].rearrange("p a k -> p (a k)"), dram["mask"]).then_inc(loaded, 16)

            @block.vector
            def _(dve):
                nc.vector.memset(mean_w[:], 1.0 / DIM).then_inc(ready, 1)
                nc.vector.memset(eps[:], EPS).then_inc(ready, 1)
                nc.vector.memset(one[:], 1.0).then_inc(ready, 1)
                nc.vector.memset(ZT[:, TOKENS:], 0.0).then_inc(ready, 1)
                dve.wait_ge(loaded, 3 * 16)
                nc.vector.tensor_copy(ident_b[:], ident[:]).then_inc(ready, 1)
                nc.vector.tensor_copy(mask[:], mask_in[:]).then_inc(ready, 1)
                dve.wait_ge(ready, 6)

        consts = dict(ident=ident, ident_b=ident_b, mean_w=mean_w, mask=mask, eps=eps, one=one)
        layer_norm(nc, 0, norm_sems, XT, ZT, consts)
        sign_ffn(nc, 0, sign_sems, XT, ZT, dram)
        layer_norm(nc, 1, norm_sems, XT, ZT, consts)
        mixed_attention(nc, "a0", XT, ZT, consts, dram)
        layer_norm(nc, 2, norm_sems, XT, ZT, consts)
        sign_ffn(nc, 1, sign_sems, XT, ZT, dram)
        layer_norm(nc, 3, norm_sems, XT, ZT, consts)
        windowed_layers(nc, 0, window_sems, ZT, consts, dram)
        half_sum(nc, 0, added, XT, ZT)
        layer_norm(nc, 4, norm_sems, XT, ZT, consts)
        delta_memory(nc, "a1", XT, ZT, consts, dram)
        layer_norm(nc, 5, norm_sems, XT, ZT, consts)
        windowed_layers(nc, 1, window_sems, ZT, consts, dram)
        half_sum(nc, 1, added, XT, ZT)

        with nc.Block() as block:
            @block.sync
            def _(sp):
                sp.dma_start(out, XT[:]).then_inc(stored, 16)
                sp.wait_ge(stored, 16)


def kernel(**inputs):
    import concourse.bacc as bacc
    from concourse.bass_utils import run_bass_kernel_spmd as run

    arrays = {"x": np.ascontiguousarray(np.asarray(inputs["L0_attn_x"]).reshape(TOKENS, DIM).T),
              "ident": np.eye(P, dtype=np.float32), "mask": window_mask(), "rot": rotary_tables()}
    for part in (sign_weights, mixed_weights, delta_weights, layer_weights):
        arrays.update(part(inputs))
    nc = bacc.Bacc("TRN2", target_bir_lowering=False, num_devices=1)
    dram = {name: nc.dram_tensor(f"in_{name}", a.shape, mybir.dt.from_np(a.dtype), kind="ExternalInput").ap()
            for name, a in arrays.items()}
    out = nc.dram_tensor("out", (DIM, TOKENS), F32, kind="ExternalOutput").ap()
    build(nc, dram, out)
    result = run(nc, [{f"in_{name}": a for name, a in arrays.items()}], core_ids=[0]).results[0]["out"]
    return np.ascontiguousarray(result.T).reshape(BATCH, SEQ, DIM)
```

```python
from contextlib import ExitStack

import numpy as np
import concourse.bass as bass
from concourse import mybir

P = 128
F32 = mybir.dt.float32
BF16 = mybir.dt.bfloat16
U8 = mybir.dt.uint8
I32 = mybir.dt.int32
ALU = mybir.AluOpType
ACT = mybir.ActivationFunctionType
AXX = mybir.AxisListType.X

BATCH, SEQ, DIM = 4, 512, 128
TOKENS = BATCH * SEQ
TILES = SEQ // P
PER = BATCH * TILES
EPS = 1e-5
DEPTH, HEADS, DH, WIN = 6, 16, 64, 32
INNER = HEADS * DH
PAIRS = HEADS // 2
HALF = DH // 2
WINS = P // WIN
KEYS = 2 * WIN
HALO = WIN
FF = int(DIM * 4 * 2 / 3)
FFB = -(-FF // P)
VEC = 3 + 2 * FFB
MASKED = -3.0e38
SPLIT = 12
ROOT_BITS, NEWTONS = 0x5F3759DF, 3


class Tile:

    def __init__(self, layer, g, i):
        self.n = layer * PER + g * TILES + i
        self.s = layer * (PER + 1) + g * TILES + i
        self.t = i % TILES
        self.col = g * SEQ + i * P


LAGS = 5


def tiles(layer, g, j):
    inside = lambda i: not isinstance(g, int) or 0 <= g * TILES + i < PER
    return [Tile(layer, g, j - k) if inside(j - k) else None for k in range(LAGS + 1)]


def attention_layer(eng, layer, step):
    for j in range(LAGS):
        step(*tiles(layer, 0, j))
    head = LAGS - TILES
    with eng.Fori(1, BATCH - 1) as g:
        for j in range(head, head + TILES):
            step(*tiles(layer, g, j))
    for j in range(head, TILES + 1):
        step(*tiles(layer, BATCH - 1, j))


def last_tiles(layer):
    return tiles(layer, BATCH, 2)[5], tiles(layer, BATCH, 2)[4], tiles(layer, BATCH, 2)[3]


def spread(ap, axis, shape):
    return ap.unsqueeze(axis).broadcast_to(shape)


class Semaphores:

    def __init__(self, nc, ctx, stage):
        self.nc, self.ctx, self.stage, self.held = nc, ctx, stage, {}

    def __call__(self, name):
        if name not in self.held:
            self.held[name] = self.ctx.enter_context(self.nc.semaphore(f"{self.stage}_{name}"))
        return self.held[name]


def windowed_layers(nc, run, sem, ZT, consts, dram):
    first = run * DEPTH
    tag = f"w{run}"
    ident, ident_b, mean_w, mask = consts["ident"], consts["ident_b"], consts["mean_w"], consts["mask"]
    eps = consts["eps"]
    ctx = ExitStack()
    with ctx:
        def sb(name, shape, dt=F32):
            return ctx.enter_context(nc.sbuf_tensor(f"{tag}_{name}", shape, dt))

        def ps(name, shape):
            return ctx.enter_context(nc.psum_tensor(f"{tag}_{name}", shape, F32))

        w_qkv = sb("w_qkv", [P, 3 * INNER])
        w_o = sb("w_o", [P, PAIRS, DIM])
        w_1 = sb("w_1", [P, 2 * FFB, P])
        w_2 = sb("w_2", [P, FFB, DIM])
        vec = sb("vec", [P, VEC])
        qk_scale = sb("qk_scale", [P, 2, DEPTH, DH])
        rot = sb("rot", [P, 2, 2, TILES, DH])
        rot_l = sb("rot_l", [P, 2, 2, TILES, DH])
        shifted = sb("shifted", [P, SEQ])
        raw = sb("raw", [P, 2, INNER])
        squares = sb("squares", [P, 2, INNER])
        turned = sb("turned", [P, 2, 2, INNER])
        sumsq = sb("sumsq", [P, 2, HEADS])
        bits = sb("bits", [P, 2, HEADS], I32)
        newton = sb("newton", [P, 2, HEADS])
        halved = sb("halved", [P, 2, HEADS])
        c_1_5 = sb("c_1_5", [P, 2, HEADS])
        inv_norm = sb("inv_norm", [P, 2, HEADS])
        qk = sb("qk", [P, 2, 2, INNER])
        qT = sb("qT", [P, PAIRS, P])
        kT = sb("kT", [P, PAIRS, 2, HALO + SEQ])
        v = sb("v", [P, TILES, INNER])
        probs = sb("probs", [P, HEADS, KEYS])
        probs_n = sb("probs_n", [P, HEADS, KEYS])
        neg_max = sb("neg_max", [P, HEADS])
        row_sum = sb("row_sum", [P, HEADS])
        row_inv = sb("row_inv", [P, HEADS])
        pT = sb("pT", [P, 2, HEADS, P])
        pT_prev = sb("pT_prev", [P, 2, HEADS, WIN])
        attT = sb("attT", [P, PAIRS, P])

        w_in, w2_in, tab_in, cleared = sem("w_in"), sem("w2_in"), sem("tab_in"), sem("cleared")
        shift_ready, rot_ready = sem("shift_ready"), sem("rot_ready")
        pe_q, pe_k, pe_v, pe_tq, pe_tk = sem("pe_q"), sem("pe_k"), sem("pe_v"), sem("pe_tq"), sem("pe_tk")
        pe_s, pe_pv, pe_y = sem("pe_s"), sem("pe_pv"), sem("pe_y")
        act_raw, act_sq, act_v, act_tq, act_tk = sem("act_raw"), sem("act_sq"), sem("act_v"), sem("act_tq"), sem("act_tk")
        act_exp, act_o = sem("act_exp"), sem("act_o")
        dve_ss, dve_floor, dve_turn = sem("dve_ss"), sem("dve_floor"), sem("dve_turn")
        dve_shift, dve_guess, pool_newton = sem("dve_shift"), sem("dve_guess"), sem("pool_newton")
        dve_max, dve_sub, dve_sum, dve_inv = sem("dve_max"), sem("dve_sub"), sem("dve_sum"), sem("dve_inv")
        dve_pT, dve_y = sem("dve_pT"), sem("dve_y")
        pool_add, pool_inv, pool_qk, pool_p = sem("pool_add"), sem("pool_inv"), sem("pool_qk"), sem("pool_p")
        f_copy, f_mean, f_cen_s, f_sq_s, f_var = sem("f_copy"), sem("f_mean"), sem("f_cen"), sem("f_sq"), sem("f_var")
        f_std, f_rstd_s, f_nrm, f_ln = sem("f_std"), sem("f_rstd"), sem("f_nrm"), sem("f_ln")
        f_h, f_gelu, f_hid_s, f_out, f_add = sem("f_h"), sem("f_gelu"), sem("f_hid"), sem("f_out"), sem("f_add")

        ring = ps("ring", [P, 2, 2, 512])
        ps_s = ps("ps_s", [P, 2, 512])
        ps_o = ps("ps_o", [P, 2, 512])
        ps_heads = ps_s[:, :, :].rearrange("p a (h k) -> p (a h) k", k=KEYS)
        ps_pairs = ps_o[:, :, :].rearrange("p a (h q) -> p (a h) q", q=P)

        xn = [turned[:, b // 2, 0, b % 2 * SEQ:(b % 2 + 1) * SEQ] for b in range(BATCH)]
        std = [turned[:, b // 2, 1, b % 2 * SEQ:(b % 2 + 1) * SEQ] for b in range(BATCH)]
        sq = squares[:, 1, SEQ:2 * SEQ]
        gate = [raw[:, 0, 0:SEQ], raw[:, 0, SEQ:2 * SEQ]]
        hid = [squares[:, 0, 0:SEQ], squares[:, 0, SEQ:2 * SEQ], squares[:, 1, 0:SEQ]]

        def half(t, use):
            return (5 * t + use) % 2

        def statistics(b, which):
            return ring[:, 0, which, :] if b < BATCH - 1 else ps_s[:, which, :]

        def hidden_half(b, i):
            return (b * FFB + i + 1) % 2

        block = ctx.enter_context(nc.Block())

        @block.sync
        def _(sp):
            def load_attention(layer):
                sp.dma_start(w_qkv[:], dram["w_qkv"][layer]).then_inc(w_in, 16)
                sp.dma_start(w_o[:].rearrange("p a b -> p (a b)"), dram["w_o"][layer]).then_inc(w_in, 16)

            def load_feed_forward(layer):
                sp.dma_start(w_1[:].rearrange("p a b -> p (a b)"), dram["w_1"][layer]).then_inc(w2_in, 16)
                sp.dma_start(w_2[:].rearrange("p a b -> p (a b)"), dram["w_2"][layer]).then_inc(w2_in, 16)
                sp.dma_start(vec[:], dram["vec"][layer]).then_inc(w2_in, 16)

            sp.dma_start(rot[:].rearrange("p a b t d -> p (a b t d)"), dram["rot"]).then_inc(tab_in, 16)
            sp.dma_start(qk_scale[:].rearrange("p a l d -> p (a l d)"), dram["qk_scale"]).then_inc(tab_in, 16)
            load_attention(0)
            load_feed_forward(0)
            with sp.Fori(1, DEPTH) as layer:
                sp.wait_ge(pe_y, (first + layer) * PER)
                load_attention(layer)
                sp.wait_ge(f_add, (first + layer) * BATCH)
                load_feed_forward(layer)

        @block.tensor
        def _(pe):
            def project(T, at, use, which, done):
                for c in range(2):
                    last = nc.tensor.matmul(ring[:, half(at, use), c, :], shifted[:, T.t * P:(T.t + 1) * P],
                                            w_qkv[:, which * INNER + c * 512:which * INNER + (c + 1) * 512],
                                            start=True, stop=True)
                last.then_inc(done, 1)

            def turn(B, use, which, done):
                at = half(B.t + 2, use)
                for p in range(PAIRS):
                    last = nc.tensor.transpose(ring[:, at, p // 4, (p % 4) * P:(p % 4 + 1) * P],
                                               qk[:, B.t % 2, which, p * P:(p + 1) * P], ident[:])
                last.then_inc(done, 1)

            def values(D, E):
                pe.wait_ge(dve_pT, D.n + 1)
                pe.wait_ge(act_v, D.n + 1)
                if E:
                    pe.wait_ge(dve_y, E.n + 1)
                for p in range(PAIRS):
                    for h in (2 * p, 2 * p + 1):
                        r = DH * (h % 2)
                        last = nc.tensor.matmul(ps_pairs[r:r + DH, p, :], v[:, D.t, h * DH:(h + 1) * DH],
                                                pT[:, D.t % 2, h, :], start=True, stop=D.t == 0)
                    for h in (2 * p, 2 * p + 1) if D.t else ():
                        r = DH * (h % 2)
                        last = nc.tensor.matmul(ps_pairs[r:r + DH, p, 0:WIN],
                                                v[:, D.t - 1, h * DH:(h + 1) * DH],
                                                pT_prev[:, D.t % 2, h, :], start=False, stop=True)
                last.then_inc(pe_pv, 1)

            def output(E):
                pe.wait_ge(act_o, E.n + 1)
                for p in range(PAIRS):
                    last = nc.tensor.matmul(ps_pairs[:, 0, :], w_o[:, p, :], attT[:, p, :],
                                            start=p == 0, stop=p == PAIRS - 1)
                last.then_inc(pe_y, 1)

            def step(T, A, B, C, D, E, between=None):
                if B:
                    pe.wait_ge(pool_qk, 2 * B.n + 1)
                    if A:
                        pe.wait_ge(act_sq, 2 * A.n + 2)
                    else:
                        pe.wait_ge(act_v, B.n)
                    turn(B, 0, 0, pe_tq)
                if T:
                    pe.wait_ge(shift_ready, T.s + run + 1)
                    if B:
                        pe.wait_ge(act_v, B.n + 1)
                    project(T, T.t, 1, 0, pe_q)
                if E:
                    output(E)
                if B:
                    pe.wait_ge(pool_qk, 2 * B.n + 2)
                    pe.wait_ge(act_tq, B.n + 1)
                    turn(B, 2, 1, pe_tk)
                if between:
                    between()
                if T:
                    pe.wait_ge(act_sq, 2 * T.n + 1)
                    project(T, T.t, 3, 1, pe_k)
                if B:
                    pe.wait_ge(act_tk, B.n + 1)
                    if C:
                        pe.wait_ge(act_exp, C.n + 1)
                    for a in range(2):
                        nc.tensor.matmul(ps_s[:, a, :], ident_b[:],
                                         spread(mask[:, min(B.t, 1), :], 1, [P, HEADS // 2, KEYS]),
                                         start=True, stop=False, skip_group_check=True)
                        for p in range(a * 4, a * 4 + 4):
                            for w in range(WINS):
                                col = B.t * P + w * WIN
                                last = nc.tensor.matmul(
                                    ps_heads[w * WIN:(w + 1) * WIN, 2 * p:2 * p + 2, :],
                                    qT[:, p, w * WIN:(w + 1) * WIN], kT[:, p, :, col:col + KEYS],
                                    start=False, stop=True, skip_group_check=True)
                    last.then_inc(pe_s, 1)
                if D:
                    values(D, E)
                if A:
                    if B:
                        pe.wait_ge(act_tk, B.n + 1)
                    else:
                        pe.wait_ge(act_sq, 2 * A.n + 2)
                    project(A, A.t + 1, 4, 2, pe_v)
            pe.wait_ge(cleared, 2 * run + 2)
            with pe.Fori(first, first + DEPTH) as layer:
                pe.wait_ge(w_in, layer * 32 + 32)
                attention_layer(pe, layer, step)
                pe.wait_ge(w2_in, layer * 48 + 48)

                def mean(b):
                    pe.wait_ge(f_copy, layer * BATCH + b + 1)
                    nc.tensor.matmul(statistics(b, 0), mean_w[:], shifted[:], start=True, stop=True).then_inc(f_mean, 1)

                def variance(b):
                    pe.wait_ge(f_sq_s, layer * BATCH + b + 1)
                    if b:
                        pe.wait_ge(f_std, layer * BATCH + b)
                    nc.tensor.matmul(statistics(b, 1), mean_w[:], sq, start=True, stop=True).then_inc(f_var, 1)

                def up(b, i):
                    n = (layer * BATCH + b) * FFB + i
                    if i == 0:
                        pe.wait_ge(f_ln, layer * BATCH + b + 1)
                    if b or i == 2:
                        pe.wait_ge(f_hid_s, n - 1)
                    elif i == 1:
                        pe.wait_ge(f_std, layer * BATCH + 3)
                    for part in range(2):
                        last = nc.tensor.matmul(ring[:, hidden_half(b, i), part, :], w_1[:, part * FFB + i, :], xn[b],
                                                start=True, stop=True)
                    last.then_inc(f_h, 1)

                def down(b):
                    pe.wait_ge(f_hid_s, (layer * BATCH + b) * FFB + FFB)
                    if b >= 2:
                        pe.wait_ge(f_add, layer * BATCH + b - 1)
                    for i in range(FFB):
                        last = nc.tensor.matmul(ps_o[:, b % 2, :], w_2[:, i, :], hid[i], start=i == 0,
                                                stop=i == FFB - 1)
                    last.then_inc(f_out, 1)

                thirteen, fourteen, fifteen = last_tiles(layer)
                step(*tiles(layer, BATCH, 1), between=lambda: mean(0))
                variance(0)
                mean(1)
                output(thirteen)
                values(fourteen, thirteen)
                variance(1)
                mean(2)
                output(fourteen)
                variance(2)
                up(0, 0)
                values(fifteen, fourteen)
                up(0, 1)
                output(fifteen)
                up(0, 2)
                mean(3)
                up(1, 0)
                variance(3)
                down(0)
                for b in range(1, BATCH):
                    for i in range(1, FFB):
                        up(b, i)
                    if b + 1 < BATCH:
                        up(b + 1, 0)
                    down(b)

        @block.scalar
        def _(act):
            def values_out(D, E):
                act.wait_ge(pe_pv, D.n + 1)
                if E:
                    act.wait_ge(pe_y, E.n + 1)
                nc.scalar.activation(attT[:], ps_pairs, ACT.Copy).then_inc(act_o, 1)

            def copy_and_square(T, A, which, done):
                projected = ring[:, half(T.t, 1 + 2 * which), :, :].rearrange("p a b -> p (a b)")
                act.wait_ge(done, T.n + 1)
                if A:
                    act.wait_ge(dve_turn, 2 * A.n + which + 1)
                nc.scalar.activation(raw[:, which, :], projected, ACT.Copy).then_inc(act_raw, 1)
                if A:
                    act.wait_ge(dve_ss, 2 * A.n + which + 1)
                nc.scalar.activation(squares[:, which, :], projected, ACT.Square).then_inc(act_sq, 1)

            def step(T, A, B, C, D, E, between=None):
                if B:
                    act.wait_ge(pe_tq, B.n + 1)
                    if C:
                        act.wait_ge(pe_s, C.n + 1)
                    nc.scalar.activation(qT[:].rearrange("p a b -> p (a b)"),
                                         ring[:, half(B.t + 2, 0), :, :].rearrange("p a b -> p (a b)"),
                                         ACT.Copy).then_inc(act_tq, 1)
                if T:
                    copy_and_square(T, A, 0, pe_q)
                if B:
                    act.wait_ge(pe_tk, B.n + 1)
                    turned_k = ring[:, half(B.t + 2, 2), :, :].rearrange("p a (b q) -> p (a b) q", q=P)
                    for h in range(2):
                        last = nc.scalar.activation(
                            kT[h * DH:(h + 1) * DH, :, h, HALO + B.t * P:HALO + (B.t + 1) * P],
                            turned_k[h * DH:(h + 1) * DH], ACT.Copy)
                    last.then_inc(act_tk, 1)
                if between:
                    between()
                if T:
                    copy_and_square(T, A, 1, pe_k)
                if D:
                    values_out(D, E)
                if A:
                    act.wait_ge(pe_v, A.n + 1)
                    nc.scalar.activation(v[:, A.t, :], ring[:, half(A.t + 1, 4), :, :].rearrange("p a b -> p (a b)"),
                                         ACT.Copy).then_inc(act_v, 1)
                if B:
                    act.wait_ge(dve_sub, B.n + 1)
                    nc.scalar.activation(probs[:, 0:SPLIT], probs[:, 0:SPLIT], ACT.Exp)
                    if C:
                        act.wait_ge(pool_p, C.n + 1)
                    for h in range(SPLIT, HEADS):
                        last = nc.scalar.activation(probs[:, h, :], ps_heads[:, h, :], ACT.Exp, bias=neg_max[:, h:h + 1],
                                                    accum_out=row_sum[:, h:h + 1])
                    last.then_inc(act_exp, 1)

            act.wait_ge(cleared, 2 * run + 2)
            with act.Fori(first, first + DEPTH) as layer:
                attention_layer(act, layer, step)
                act.wait_ge(w2_in, layer * 48 + 48)

                def square(b):
                    act.wait_ge(f_cen_s, layer * BATCH + b + 1)
                    if b:
                        act.wait_ge(f_var, layer * BATCH + b)
                    nc.scalar.activation(sq, xn[b], ACT.Square).then_inc(f_sq_s, 1)

                def deviation(b):
                    act.wait_ge(f_var, layer * BATCH + b + 1)
                    nc.scalar.activation(std[b], statistics(b, 1), ACT.Sqrt, bias=eps[:, 0:1]).then_inc(f_std, 1)

                def gelu(b, i):
                    n = (layer * BATCH + b) * FFB + i
                    act.wait_ge(f_h, n + 1)
                    if b or i == 2:
                        act.wait_ge(f_hid_s, n - 1)
                    nc.scalar.activation(gate[(b * FFB + i) % 2], ring[:, hidden_half(b, i), 1, :], ACT.Gelu,
                                         bias=vec[:, 2 + FFB + i:3 + FFB + i]).then_inc(f_gelu, 1)

                thirteen, fourteen, fifteen = last_tiles(layer)
                step(*tiles(layer, BATCH, 1), between=lambda: square(0))
                deviation(0)
                square(1)
                values_out(fourteen, thirteen)
                deviation(1)
                square(2)
                deviation(2)
                gelu(0, 0)
                values_out(fifteen, fourteen)
                gelu(0, 1)
                gelu(0, 2)
                square(3)
                deviation(3)
                for b in range(1, BATCH):
                    for i in range(FFB):
                        gelu(b, i)

        @block.vector
        def _(dve):
            nc.vector.memset(shifted[:], 0.0)
            nc.vector.memset(kT[:], 0.0).then_inc(cleared, 1)
            dve.wait_ge(cleared, 2 * run + 2)

            def shifted_copy(col, t):
                nc.vector.tensor_copy(shifted[0:64, t * P:(t + 1) * P], ZT[0:64, bass.ds(col, P)])
                if t == 0:
                    nc.vector.tensor_copy(shifted[64:128, 1:P], ZT[64:128, bass.ds(col, P - 1)]).then_inc(shift_ready, 1)
                else:
                    nc.vector.tensor_copy(shifted[64:128, t * P:(t + 1) * P],
                                          ZT[64:128, bass.ds(col - 1, P)]).then_inc(shift_ready, 1)

            def rotate(T, A, which):
                dve.wait_ge(act_raw, 2 * T.n + which + 1)
                if A:
                    dve.wait_ge(pool_add, 2 * A.n + which + 1)
                src = raw[:, which, :].rearrange("p (h d) -> p h d", d=DH)
                cos = spread(rot_l[:, which, 0, T.t, :], 1, [P, HEADS, DH])
                nc.vector.tensor_tensor(turned[:, which, 0, :].rearrange("p (h d) -> p h d", d=DH),
                                        src, cos, ALU.mult)
                swapped = raw[:, which, :].rearrange("p (h two d) -> p h two d", two=2,
                                                     d=HALF)[:, :, ::-1, :]
                sin = spread(rot_l[:, which, 1, T.t, :].rearrange("p (two d) -> p two d", two=2),
                             1, [P, HEADS, 2, HALF])
                nc.vector.tensor_tensor(turned[:, which, 1, :].rearrange("p (h two d) -> p h two d", two=2, d=HALF),
                                        swapped, sin, ALU.mult).then_inc(dve_turn, 1)
                dve.wait_ge(act_sq, 2 * T.n + which + 1)
                if A:
                    dve.wait_ge(pool_inv, A.n + 1)
                nc.vector.reduce_sum(sumsq[:, which, :], squares[:, which, :]
                                     .rearrange("p (h d) -> p h d", d=DH), AXX).then_inc(dve_ss, 1)

            def transpose_probs(C):
                dve.wait_ge(pool_p, C.n + 1)
                for w in range(WINS):
                    q = slice(w * WIN, (w + 1) * WIN)
                    last = nc.vector.transpose(pT[q, C.t % 2, :, q], probs_n[q, :, WIN:KEYS])
                    if w:
                        last = nc.vector.transpose(pT[(w - 1) * WIN:w * WIN, C.t % 2, :, q], probs_n[q, :, 0:WIN])
                    elif C.t:
                        nc.vector.transpose(pT_prev[P - WIN:P, C.t % 2, :, :], probs_n[q, :, 0:WIN])
                last.then_inc(dve_pT, 1)

            def add_output(E):
                dve.wait_ge(pe_y, E.n + 1)
                nc.vector.tensor_tensor(ZT[:, bass.ds(E.col, P)], ps_pairs[:, 0, :], ZT[:, bass.ds(E.col, P)],
                                        ALU.add).then_inc(dve_y, 1)

            def step(T, A, B, C, D, E, between=None):
                if T:
                    shifted_copy(T.col + P, (T.t + 1) % TILES)
                    rotate(T, A, 0)
                if E:
                    add_output(E)
                if between:
                    between()
                if T:
                    rotate(T, A, 1)
                if B:
                    dve.wait_ge(pe_s, B.n + 1)
                    if C:
                        dve.wait_ge(act_exp, C.n + 1)
                    nc.vector.tensor_reduce(neg_max[:], ps_heads, AXX, ALU.max, negate=True).then_inc(dve_max, 1)
                if T:
                    dve.wait_ge(dve_ss, 2 * T.n + 2)
                    nc.vector.tensor_scalar(halved[:], sumsq[:], 1e-24, -0.5, ALU.max, ALU.mult)
                    nc.vector.tensor_scalar_max(sumsq[:], sumsq[:], 1e-24).then_inc(dve_floor, 1)
                if B:
                    if C:
                        dve.wait_ge(pool_p, C.n + 1)
                    dve.wait_ge(dve_max, B.n + 1)
                    nc.vector.tensor_tensor(probs[:, 0:SPLIT], ps_heads[:, 0:SPLIT],
                                            spread(neg_max[:, 0:SPLIT], 2, [P, SPLIT, KEYS]),
                                            ALU.add).then_inc(dve_sub, 1)
                if T:
                    dve.wait_ge(dve_floor, T.n + 1)
                    nc.vector.tensor_scalar(bits[:], sumsq[:].bitcast(I32), 1, None,
                                            ALU.logical_shift_right).then_inc(dve_shift, 1)
                    dve.wait_ge(dve_shift, T.n + 1)
                    nc.vector.tensor_scalar(bits[:], bits[:], -1.0, float(ROOT_BITS),
                                            ALU.mult, ALU.add).then_inc(dve_guess, 1)
                if C:
                    transpose_probs(C)
                if B:
                    dve.wait_ge(act_exp, B.n + 1)
                    nc.vector.reduce_sum(row_sum[:, 0:SPLIT], probs[:, 0:SPLIT], AXX).then_inc(dve_sum, 1)
                    dve.wait_ge(dve_sum, B.n + 1)
                    nc.vector.reciprocal(row_inv[:], row_sum[:]).then_inc(dve_inv, 1)

            shifted_copy(0, 0)
            with dve.Fori(first, first + DEPTH) as layer:
                def shift(b):
                    if b:
                        dve.wait_ge(f_cen_s, layer * BATCH + b)
                    nc.vector.tensor_copy(shifted[0:64, :], ZT[0:64, b * SEQ:(b + 1) * SEQ])
                    nc.vector.tensor_copy(shifted[64:128, 1:SEQ],
                                          ZT[64:128, b * SEQ:(b + 1) * SEQ - 1]).then_inc(f_copy, 1)

                def center(b):
                    dve.wait_ge(f_mean, layer * BATCH + b + 1)
                    nc.vector.tensor_tensor(xn[b], shifted[:], statistics(b, 0), ALU.subtract).then_inc(f_cen_s, 1)

                def normalise(b):
                    dve.wait_ge(f_std, layer * BATCH + b + 1)
                    nc.vector.reciprocal(std[b], std[b]).then_inc(f_rstd_s, 1)
                    dve.wait_ge(f_rstd_s, layer * BATCH + b + 1)
                    nc.vector.tensor_tensor(xn[b], xn[b], std[b], ALU.mult).then_inc(f_nrm, 1)
                    dve.wait_ge(f_nrm, layer * BATCH + b + 1)
                    nc.vector.tensor_scalar(xn[b], xn[b], vec[:, 0:1], vec[:, 1:2],
                                            ALU.mult, ALU.add).then_inc(f_ln, 1)

                def hidden(b, i):
                    n = (layer * BATCH + b) * FFB + i
                    dve.wait_ge(f_gelu, n + 1)
                    if b and i == 0:
                        dve.wait_ge(f_out, layer * BATCH + b)
                    nc.vector.scalar_tensor_tensor(hid[i], ring[:, hidden_half(b, i), 0, :], vec[:, 2 + i:3 + i],
                                                   gate[(b * FFB + i) % 2], ALU.add, ALU.mult).then_inc(f_hid_s, 1)

                def add_rows(b):
                    dve.wait_ge(f_out, layer * BATCH + b + 1)
                    cols = ZT[:, b * SEQ:(b + 1) * SEQ]
                    nc.vector.scalar_tensor_tensor(cols, ps_o[:, b % 2, :], vec[:, VEC - 1:VEC], cols,
                                                   ALU.add, ALU.add).then_inc(f_add, 1)

                dve.wait_ge(rot_ready, layer + 1)
                attention_layer(dve, layer, step)
                thirteen, fourteen, fifteen = last_tiles(layer)
                dve.wait_ge(w2_in, layer * 48 + 48)
                dve.wait_ge(pool_add, 2 * (layer * PER + PER))
                dve.wait_ge(act_v, layer * PER + PER)
                shift(0)

                def front():
                    center(0)
                    shift(1)

                step(*tiles(layer, BATCH, 1), between=front)
                add_output(thirteen)
                center(1)
                shift(2)
                normalise(0)
                center(2)
                transpose_probs(fifteen)
                add_output(fourteen)
                hidden(0, 0)
                normalise(1)
                hidden(0, 1)
                add_output(fifteen)
                dve.wait_ge(dve_y, layer * PER + PER)
                shift(3)
                hidden(0, 2)
                center(3)
                normalise(2)
                hidden(1, 0)
                hidden(1, 1)
                add_rows(0)
                dve.wait_ge(f_add, layer * BATCH + 1)
                dve.wait_ge(f_cen_s, layer * BATCH + BATCH)
                shifted_copy(0, 0)
                hidden(1, 2)
                normalise(3)
                add_rows(1)
                for b in range(2, BATCH):
                    for i in range(FFB):
                        hidden(b, i)
                    add_rows(b)
                dve.wait_ge(f_add, layer * BATCH + BATCH)

        @block.gpsimd
        def _(pool):
            nc.gpsimd.memset(pT_prev[:], 0.0)
            nc.gpsimd.memset(c_1_5[:], 1.5)
            nc.gpsimd.memset(pT[:], 0.0).then_inc(cleared, 1)
            pool.wait_ge(cleared, 2 * run + 2)
            pool.wait_ge(tab_in, 32 * run + 32)

            def add(T, B, which, turned_out):
                pool.wait_ge(dve_turn, 2 * T.n + which + 1)
                if B:
                    pool.wait_ge(turned_out, B.n + 1)
                nc.gpsimd.tensor_tensor(qk[:, T.t % 2, which, :], turned[:, which, 0, :], turned[:, which, 1, :],
                                        ALU.add).then_inc(pool_add, 1)

            def step(T, A, B, C, D, E, between=None):
                if T:
                    add(T, B, 0, pe_tq)
                    add(T, B, 1, pe_tk)
                if T:
                    pool.wait_ge(dve_guess, T.n + 1)
                    steps = 4 * NEWTONS
                    y = bits[:].bitcast(F32)
                    for k in range(NEWTONS):
                        at = T.n * (steps - 1) + 4 * k
                        if k:
                            pool.wait_ge(pool_newton, at)
                        nc.gpsimd.tensor_tensor(newton[:], y, y, ALU.mult).then_inc(pool_newton, 1)
                        pool.wait_ge(pool_newton, at + 1)
                        nc.gpsimd.tensor_tensor(newton[:], newton[:], halved[:], ALU.mult).then_inc(pool_newton, 1)
                        pool.wait_ge(pool_newton, at + 2)
                        nc.gpsimd.tensor_tensor(newton[:], newton[:], c_1_5[:], ALU.add).then_inc(pool_newton, 1)
                        pool.wait_ge(pool_newton, at + 3)
                        nc.gpsimd.tensor_tensor(inv_norm[:], newton[:], y, ALU.mult).then_inc(
                            pool_newton if k < NEWTONS - 1 else pool_inv, 1)
                        y = inv_norm[:]
                    pool.wait_ge(pool_inv, T.n + 1)
                    pool.wait_ge(pool_add, 2 * T.n + 2)
                    for which in range(2):
                        heads = qk[:, T.t % 2, which, :].rearrange("p (h d) -> p h d", d=DH)
                        nc.gpsimd.tensor_tensor(heads, heads, spread(inv_norm[:, which, :], 2, [P, HEADS, DH]),
                                                ALU.mult).then_inc(pool_qk, 1)
                if B:
                    pool.wait_ge(dve_inv, B.n + 1)
                    if C:
                        pool.wait_ge(dve_pT, C.n + 1)
                    nc.gpsimd.tensor_tensor(probs_n[:], probs[:], spread(row_inv[:], 2, [P, HEADS, KEYS]),
                                            ALU.mult).then_inc(pool_p, 1)

            with pool.Fori(first, first + DEPTH) as layer:
                pool.wait_ge(shift_ready, Tile(layer, 0, 0).s + run + 1)
                for which in range(2):
                    scale = qk_scale[:, which, bass.ds(layer - first, 1), :].rearrange("p a d -> p (a d)")
                    nc.gpsimd.tensor_tensor(rot_l[:, which, 0, :, :], rot[:, which, 0, :, :],
                                            spread(scale, 1, [P, TILES, DH]), ALU.mult)
                    for d in range(2):
                        here = slice(d * HALF, (d + 1) * HALF)
                        there = slice((1 - d) * HALF, (2 - d) * HALF)
                        last = nc.gpsimd.tensor_tensor(rot_l[:, which, 1, :, here], rot[:, which, 1, :, here],
                                                       spread(scale[:, there], 1, [P, TILES, HALF]), ALU.mult)
                last.then_inc(rot_ready, 1)
                attention_layer(pool, layer, step)
                step(*tiles(layer, BATCH, 1))


def rotary_tables():
    half = np.arange(0, DH, 2, dtype=np.float32)
    inv_freq = (1.0 / np.power(np.float32(10000.0), half / DH)).astype(np.float32)
    t = np.arange(SEQ, dtype=np.float32)
    freqs = (t[:, None] * inv_freq[None, :]).astype(np.float32).astype(np.float64)
    base = ((half + 0.4 * DH) / (1.4 * DH)).astype(np.float64)
    scale = base[None, :] ** ((t[:, None] - SEQ // 2) / (WIN // 2)).astype(np.float64)
    both = lambda a, b: np.concatenate([a, b], -1)
    cos, sin = np.cos(freqs), np.sin(freqs)
    rows = []
    for s in (8.0 * scale, 1.0 / scale):
        rows.append([both(cos * s, cos * s), both(-sin * s, sin * s)])
    rows = np.array(rows).astype(np.float32)
    rows = rows.reshape(2, 2, TILES, P, DH).transpose(3, 0, 1, 2, 4)
    return np.ascontiguousarray(rows.reshape(P, -1))


def window_mask():
    row = np.arange(P)
    i, key = row % WIN, np.arange(KEYS)
    ok = np.where(key[None, :] < WIN, key[None, :] >= i[:, None], key[None, :] - WIN <= i[:, None])
    first = ok & ~((row[:, None] < WIN) & (key[None, :] < WIN))
    return np.where(np.stack([first, ok], 1), 0.0, MASKED).astype(np.float32).reshape(P, 2 * KEYS)


def layer_weights(i, depth=DEPTH):
    A = lambda n: np.asarray(i[f"L1_ffn_{n}"])[:depth]
    out = {"w_qkv": A("Wqkv"), "w_o": A("Wo").reshape(depth, PAIRS, P, DIM).transpose(0, 2, 1, 3)}
    w1 = np.zeros((depth, P, 2, FFB * P), np.float32)
    w1[:, :, 0, :FF], w1[:, :, 1, :FF] = A("W1")[:, :, :FF], A("W1")[:, :, FF:]
    w2 = np.zeros((depth, FFB * P, DIM), np.float32)
    w2[:, :FF] = A("W2")
    b1 = np.zeros((depth, 2, FFB * P), np.float32)
    b1[:, 0, :FF], b1[:, 1, :FF] = A("b1")[:, :FF], A("b1")[:, FF:]
    cols = [A("ln_g")[:, :, None], A("ln_b")[:, :, None], b1.reshape(depth, 2 * FFB, P).transpose(0, 2, 1),
            A("b2")[:, :, None]]
    out.update(w_1=w1, w_2=w2.reshape(depth, FFB, P, DIM).transpose(0, 2, 1, 3), vec=np.concatenate(cols, -1))
    scales = np.stack([A("q_scale"), A("k_scale")]).reshape(1, -1)
    out["qk_scale"] = np.broadcast_to(scales, (P, scales.shape[1]))
    return {k: np.ascontiguousarray(v.reshape(v.shape[:2] + (-1,)) if v.ndim > 2 else v) for k, v in out.items()}


H0, D0 = 16, 8
GROUPS = DIM // D0
TOK = SEQ // H0
QUADS = 4
J0 = H0 // QUADS
KB = SEQ // P
FF0 = 512
BLK = FF0 // P


def layer_norm(nc, run, sem, src, dst, consts):
    tag, base = f"n{run}", run * BATCH
    mean_w, eps = consts["mean_w"], consts["eps"]
    quad = P // BATCH
    with ExitStack() as ctx:
        std = ctx.enter_context(nc.sbuf_tensor(f"{tag}_std", [P, SEQ], F32))
        sel = ctx.enter_context(nc.sbuf_tensor(f"{tag}_sel", [P, BATCH, P], F32))
        sq = ctx.enter_context(nc.sbuf_tensor(f"{tag}_sq", [P, BATCH, SEQ], F32))
        ps = ctx.enter_context(nc.psum_tensor(f"{tag}_ps", [P, 5, SEQ], F32))
        mean_s, cen_s, sq_s, var_s, std_s, inv_s, sel_s, rep_s, out_s = [
            sem(n) for n in ("mean", "cen", "sq", "var", "std", "inv", "sel", "rep", "out")]
        block = ctx.enter_context(nc.Block())
        cols = [slice(b * SEQ, (b + 1) * SEQ) for b in range(BATCH)]

        @block.tensor
        def _(pe):
            for b in range(BATCH):
                nc.tensor.matmul(ps[:, b, :], mean_w[:], src[:, cols[b]], start=True, stop=True).then_inc(mean_s, 1)
            for b in range(BATCH):
                pe.wait_ge(sq_s, base + b + 1)
                last = nc.tensor.matmul(ps[b * quad:(b + 1) * quad, BATCH, :], mean_w[:, 0:quad], sq[:, b, :],
                                        start=True, stop=True)
            last.then_inc(var_s, 1)
            pe.wait_ge(sel_s, BATCH * (run + 1) + run + 1)
            pe.wait_ge(inv_s, run + 1)
            for b in range(BATCH):
                nc.tensor.matmul(ps[:, b, :], sel[:, b, :], std[:], start=True, stop=True).then_inc(rep_s, 1)

        @block.scalar
        def _(act):
            for b in range(BATCH):
                act.wait_ge(cen_s, base + b + 1)
                nc.scalar.activation(sq[:, b, :], dst[:, cols[b]], ACT.Square).then_inc(sq_s, 1)
            act.wait_ge(var_s, run + 1)
            nc.scalar.activation(std[:], ps[:, BATCH, :], ACT.Sqrt, bias=eps[:, 0:1]).then_inc(std_s, 1)

        @block.gpsimd
        def _(pool):
            nc.gpsimd.memset(sel[:], 0.0).then_inc(sel_s, 1)
            for b in range(BATCH):
                pool.wait_ge(sel_s, (BATCH + 1) * run + b + 1)
                nc.gpsimd.memset(sel[b * quad:b * quad + 1, b, :], 1.0).then_inc(sel_s, 1)

        @block.vector
        def _(dve):
            for b in range(BATCH):
                dve.wait_ge(mean_s, base + b + 1)
                nc.vector.tensor_tensor(dst[:, cols[b]], src[:, cols[b]], ps[:, b, :], ALU.subtract).then_inc(cen_s, 1)
            dve.wait_ge(std_s, run + 1)
            nc.vector.reciprocal(std[:], std[:]).then_inc(inv_s, 1)
            for b in range(BATCH):
                dve.wait_ge(rep_s, base + b + 1)
                nc.vector.tensor_tensor(dst[:, cols[b]], dst[:, cols[b]], ps[:, b, :], ALU.mult).then_inc(out_s, 1)
            dve.wait_ge(out_s, base + BATCH)


def sign_ffn(nc, run, sem, XT, xn, dram):
    tag = f"f{run}"
    with ExitStack() as ctx:
        def sb(name, shape, dt=F32):
            return ctx.enter_context(nc.sbuf_tensor(f"{tag}_{name}", shape, dt))

        k0, k1, k2 = sb("k0", [P, 2, FF0], U8), sb("k1", [P, BLK, FF0], U8), sb("k2", [P, BLK, DIM], U8)
        w0, w1, w2 = sb("w0", [P, FF0]), sb("w1", [P, BLK, FF0]), sb("w2", [P, BLK, DIM])
        s_in, s_use = sb("s_in", [P, 3]), sb("s_use", [P, 3])
        h0, h1 = sb("h0", [P, 2, BLK, SEQ]), sb("h1", [P, 2, BLK, SEQ])
        ps = ctx.enter_context(nc.psum_tensor(f"{tag}_ps", [P, 8, SEQ], F32))
        loaded, diff, ready = sem("loaded"), sem("diff"), sem("ready")
        pe_0, pe_1, pe_2, act_0, act_1, dve_x = [sem(n) for n in ("pe_0", "pe_1", "pe_2", "act_0", "act_1", "dve_x")]
        block = ctx.enter_context(nc.Block())

        @block.sync
        def _(sp):
            for dst, src in ((k0, "k0"), (k1, "k1"), (k2, "k2")):
                sp.dma_start(dst[:].rearrange("p a b -> p (a b)"), dram[src]).then_inc(loaded, 16)
            sp.dma_start(s_in[:], dram["s"]).then_inc(loaded, 16)

        @block.tensor
        def _(pe):
            pe.wait_ge(ready, 5 * run + 5)
            for c in range(BATCH):
                n = run * BATCH + c
                for m in range(BLK):
                    if c:
                        pe.wait_ge(act_0, BLK * (n - 1) + m + 1)
                    nc.tensor.matmul(ps[:, m, :], w0[:, m * P:(m + 1) * P], xn[:, c * SEQ:(c + 1) * SEQ],
                                     start=True, stop=True).then_inc(pe_0, 1)
                pe.wait_ge(act_0, BLK * (n + 1))
                for m in range(BLK):
                    if BLK * c + m >= 2:
                        pe.wait_ge(act_1, BLK * n + m - 1)
                    for k in range(BLK):
                        last = nc.tensor.matmul(ps[:, 4 + m % 2, :], w1[:, k, m * P:(m + 1) * P], h0[:, c % 2, k, :],
                                                start=k == 0, stop=k == BLK - 1)
                    last.then_inc(pe_1, 1)
                pe.wait_ge(act_1, BLK * (n + 1))
                if c >= 2:
                    pe.wait_ge(dve_x, n - 1)
                for k in range(BLK):
                    last = nc.tensor.matmul(ps[:, 6 + c % 2, :], w2[:, k, :], h1[:, c % 2, k, :],
                                            start=k == 0, stop=k == BLK - 1)
                last.then_inc(pe_2, 1)

        @block.scalar
        def _(act):
            act.wait_ge(ready, 5 * run + 5)
            for c in range(BATCH):
                n = run * BATCH + c
                for m in range(BLK):
                    act.wait_ge(pe_0, BLK * n + m + 1)
                    nc.scalar.activation(h0[:, c % 2, m, :], ps[:, m, :], ACT.Relu, scale=s_use[:, 0:1]).then_inc(act_0, 1)
                for m in range(BLK):
                    act.wait_ge(pe_1, BLK * n + m + 1)
                    nc.scalar.activation(h1[:, c % 2, m, :], ps[:, 4 + m % 2, :], ACT.Relu,
                                         scale=s_use[:, 1:2]).then_inc(act_1, 1)

        @block.vector
        def _(dve):
            dve.wait_ge(loaded, 64 * run + 64)
            nc.vector.tensor_tensor(w0[:], k0[:, 0, :], k0[:, 1, :], ALU.subtract).then_inc(diff, 1)
            nc.vector.tensor_scalar(w1[:], k1[:], 2.0, -1.0, ALU.mult, ALU.add).then_inc(ready, 1)
            nc.vector.tensor_scalar(w2[:], k2[:], 2.0, -1.0, ALU.mult, ALU.add).then_inc(ready, 1)
            nc.vector.tensor_scalar(s_use[:, 0:2], s_in[:, 0:2], 2.0, None, ALU.mult).then_inc(ready, 1)
            nc.vector.tensor_scalar(s_use[:, 2:3], s_in[:, 2:3], 0.5, None, ALU.mult).then_inc(ready, 1)
            dve.wait_ge(diff, run + 1)
            nc.vector.tensor_scalar(w0[:], w0[:], 2.0, None, ALU.mult).then_inc(ready, 1)
            dve.wait_ge(ready, 5 * run + 5)
            for c in range(BATCH):
                n = run * BATCH + c
                cols = XT[:, c * SEQ:(c + 1) * SEQ]
                dve.wait_ge(pe_2, n + 1)
                nc.vector.scalar_tensor_tensor(cols, ps[:, 6 + c % 2, :], s_use[:, 2:3], cols,
                                               ALU.mult, ALU.add).then_inc(dve_x, 1)
            dve.wait_ge(dve_x, run * BATCH + BATCH)


def mixed_attention(nc, tag, XT, xn, consts, dram):
    ident, one = consts["ident"], consts["one"]
    UNITS = J0 * GROUPS
    LAG = 2
    with ExitStack() as ctx:
        def sb(name, shape, dt=F32):
            return ctx.enter_context(nc.sbuf_tensor(f"{tag}_{name}", shape, dt))

        def sem(name):
            return ctx.enter_context(nc.semaphore(f"{tag}_{name}"))

        w_in = sb("w_in", [P, 4, DIM])
        cs = sb("cs", [P, 2, D0 // 2])
        w_v = sb("w_v", [P, KB, QUADS, D0])
        b_v = sb("b_v", [P, KB, D0])
        w_o = sb("w_o", [P, J0, DIM])
        b_o = sb("b_o", [P, 1])
        sel = sb("sel", [P, P])
        prod = sb("prod", [P, 4, 4 * GROUPS, D0 // 2])
        w_r = sb("w_r", [P, 4, GROUPS, 32])
        b_r = sb("b_r", [P, 2, GROUPS])
        QT = sb("QT", [P, J0 * BATCH, GROUPS, TOK])
        KT = sb("KT", [P, J0 * BATCH, GROUPS, TOK])
        V = sb("V", [P, BATCH, H0, KB, D0 + 1])
        q_diag = sb("q_diag", [P, 2, GROUPS, QUADS, TOK])
        v_now = sb("v_now", [P, 2, QUADS, KB, D0 + 1])
        neg_max = sb("neg_max", [P, 4])
        probs = sb("probs", [P, 3, SEQ])
        pT = sb("pT", [P, KB, QUADS, GROUPS, TOK])
        oT = sb("oT", [P, SEQ])
        inv = sb("inv", [P, SEQ])
        ps = ctx.enter_context(nc.psum_tensor(f"{tag}_ps", [P, 8, SEQ], F32))
        loaded, cleared = sem("loaded"), sem("cleared")
        products, rotated, scaled = sem("products"), sem("rotated"), sem("scaled")
        pe_b, dve_b, pe_p, act_p, pe_v, dve_v = [sem(n) for n in ("pe_b", "dve_b", "pe_p", "act_p", "pe_v", "dve_v")]
        pool_in, pool_q, pe_s, dve_m, act_e, pe_t, dve_t = [sem(n) for n in ("pool_in", "pool_q", "pe_s", "dve_m", "act_e", "pe_t", "dve_t")]
        pe_o, act_o, pe_n, dve_r, dve_n, pe_y, dve_y = [
            sem(n) for n in ("pe_o", "act_o", "pe_n", "dve_r", "dve_n", "pe_y", "dve_y")]
        block = ctx.enter_context(nc.Block())
        S_BANKS, T_BANKS, O_BANK, N_BANK, Y_BANK = (0, 1, 2), (3, 4), 5, 6, 7
        V_BANKS = BATCH * H0 * KB * D0 // SEQ

        @block.sync
        def _(sp):
            for dst, name in ((w_in, "w_in"), (cs, "cs"), (w_o, "a_w_o")):
                sp.dma_start(dst[:].rearrange("p a b -> p (a b)"), dram[name]).then_inc(loaded, 16)
            sp.dma_start(w_v[:].rearrange("p a b c -> p (a b c)"), dram["w_v"]).then_inc(loaded, 16)
            sp.dma_start(b_v[:].rearrange("p a b -> p (a b)"), dram["b_v"]).then_inc(loaded, 16)
            sp.dma_start(b_o[:], dram["b_o"]).then_inc(loaded, 16)
            sp.dma_start(sel[:], dram["sel"]).then_inc(loaded, 16)

        xh = xn[:, 0:TOKENS].rearrange("p (bj r t) -> p bj r t", r=QUADS, t=TOK)

        @block.tensor
        def _(pe):
            pe.wait_ge(loaded, 7 * 16)
            pe.wait_ge(scaled, 1)
            pe.wait_ge(cleared, 2)
            for which in range(2):
                for g in range(GROUPS):
                    for r in range(QUADS):
                        col = which * GROUPS + g
                        last = nc.tensor.matmul(ps[32 * r:32 * r + 32, 6, col:col + 1], w_r[0:1, 2 + which, g, :],
                                                one[0:1, 0:1], start=True, stop=True, skip_group_check=True)
            last.then_inc(pe_b, 1)
            n = 0
            for which in range(2):
                for g in range(GROUPS):
                    if n >= 4:
                        pe.wait_ge(act_p, n - 3)
                    for r in range(QUADS):
                        last = nc.tensor.matmul(ps[32 * r:32 * r + 32, n % 4, :], w_r[:, which, g, :], xh[:, :, r, :],
                                                start=True, stop=True)
                    last.then_inc(pe_p, 1)
                    n += 1
            pe.wait_ge(act_p, 2 * GROUPS)
            for bh in range(BATCH * H0):
                for q in range(QUADS):
                    last = nc.tensor.matmul(
                        ps[32 * q:32 * q + 32, 0:V_BANKS, :].rearrange("p a (h d) -> p (a h) d", d=KB * D0)[:, bh, :],
                        xn[:, bh * TOK:(bh + 1) * TOK], w_v[:, :, q, :], start=True, stop=True,
                        skip_group_check=True)
            last.then_inc(pe_v, 1)
            pe.wait_ge(dve_v, 2)

            with pe.Fori(0, BATCH) as b:
                def spread_sums(j):
                    pe.wait_ge(act_o, b * J0 + j + 1)
                    nc.tensor.matmul(ps[:, N_BANK, :], sel[:], oT[:], start=True, stop=True).then_inc(pe_n, 1)

                def project_out(j):
                    pe.wait_ge(dve_n, b * J0 + j + 1)
                    nc.tensor.matmul(ps[:, Y_BANK, :], w_o[:, j, :], oT[:], start=j == 0,
                                     stop=j == J0 - 1).then_inc(pe_y, 1)

                for u in range(UNITS + LAG):
                    if u < UNITS:
                        j, g, n = u // GROUPS, u % GROUPS, b * UNITS + u
                        if g == 0:
                            pe.wait_ge(pool_q, (b * J0 + j + 1) * QUADS)
                        if u >= 3:
                            pe.wait_ge(act_e, n - 2)
                        nc.tensor.matmul(ps[:, S_BANKS[u % 3], :],
                                         q_diag[:, j % 2, g, :, :].rearrange("p r t -> p (r t)"),
                                         KT[:, bass.ds(b * J0 + j, 1), :, :].rearrange("p a g t -> p (a g t)"),
                                         start=True, stop=True).then_inc(pe_s, 1)
                    if u >= LAG:
                        v_, j, g, n = u - LAG, (u - LAG) // GROUPS, (u - LAG) % GROUPS, b * UNITS + u - LAG
                        pe.wait_ge(act_e, n + 1)
                        if v_ >= 2:
                            pe.wait_ge(dve_t, n - 1)
                        for a in range(KB):
                            last = nc.tensor.transpose(ps[:, T_BANKS[v_ % 2], a * P:(a + 1) * P],
                                                       probs[:, v_ % 3, a * P:(a + 1) * P], ident[:])
                        last.then_inc(pe_t, 1)
                        if g == GROUPS - 1:
                            pe.wait_ge(dve_t, n + 1)
                            pe.wait_ge(pool_in, b * J0 + j + 1)
                            if j:
                                pe.wait_ge(act_o, b * J0 + j)
                            for a in range(KB):
                                for r in range(QUADS):
                                    last = nc.tensor.matmul(
                                        ps[32 * r:32 * r + D0 + 1, O_BANK, :], v_now[:, j % 2, r, a, :],
                                        pT[:, a, r, :, :].rearrange("p g t -> p (g t)"),
                                        start=a == 0, stop=a == KB - 1)
                            last.then_inc(pe_o, 1)
                        if g == 3 and j:
                            spread_sums(j - 1)
                        if g == 7 and j:
                            project_out(j - 1)
                spread_sums(J0 - 1)
                project_out(J0 - 1)

        @block.scalar
        def _(act):
            act.wait_ge(dve_b, 1)
            for n in range(2 * GROUPS):
                act.wait_ge(pe_p, n + 1)
                which, g = n // GROUPS, n % GROUPS
                nc.scalar.activation((QT, KT)[which][:, :, g, :], ps[:, n % 4, :].rearrange("p (a t) -> p a t", t=TOK),
                                     ACT.Identity, bias=b_r[:, which, g:g + 1]).then_inc(act_p, 1)
            with act.Fori(0, BATCH) as b:
                for u in range(UNITS + 6):
                    if u < UNITS:
                        n = b * UNITS + u
                        act.wait_ge(dve_m, n + 1)
                        if u >= 3:
                            act.wait_ge(pe_t, n - 2)
                        nc.scalar.activation(probs[:, u % 3, :], ps[:, S_BANKS[u % 3], :], ACT.Exp,
                                             bias=neg_max[:, u % 4:u % 4 + 1]).then_inc(act_e, 1)
                    v_ = u - 4
                    if v_ >= 0 and v_ % GROUPS == GROUPS - 1:
                        j = v_ // GROUPS
                        if j < J0:
                            act.wait_ge(pe_o, b * J0 + j + 1)
                            if j:
                                act.wait_ge(pe_y, b * J0 + j)
                            nc.scalar.activation(oT[:], ps[:, O_BANK, :], ACT.Copy).then_inc(act_o, 1)

        @block.vector
        def _(dve):
            dve.wait_ge(loaded, 7 * 16)
            nc.vector.memset(w_r[:], 0.0)
            nc.vector.memset(ps[:, O_BANK, :], 0.0)
            nc.vector.memset(V[:].rearrange("p b h a d -> p (b h a) d")[:, :, D0:D0 + 1], 1.0).then_inc(cleared, 1)
            w = w_in[:].rearrange("p s (g c two) -> p (s g) c two", two=2, c=D0 // 2)
            re, im = w[:, :, :, 0], w[:, :, :, 1]
            shape = [P, 4 * GROUPS, D0 // 2]
            c, s = spread(cs[:, 0, :], 1, shape), spread(cs[:, 1, :], 1, shape)
            for i, (x, y) in enumerate(((re, c), (im, s), (re, s), (im, c))):
                nc.vector.tensor_tensor(prod[:, i, :, :], x, y, ALU.mult).then_inc(products, 1)
            dve.wait_ge(products, 4)
            dve.wait_ge(cleared, 2)
            out = w_r[:].rearrange("p s g (c two) -> p (s g) c two", two=2)[:, :, 0:D0 // 2, :]
            nc.vector.tensor_tensor(out[:, :, :, 0], prod[:, 0, :, :], prod[:, 1, :, :], ALU.subtract)
            nc.vector.tensor_tensor(out[:, :, :, 1], prod[:, 2, :, :], prod[:, 3, :, :], ALU.add).then_inc(rotated, 1)
            dve.wait_ge(rotated, 1)
            qs = w_r[:, 0:4:2, :, :]
            nc.vector.tensor_scalar(qs, qs, 1.0 / float(np.sqrt(D0)), None, ALU.mult).then_inc(scaled, 1)
            dve.wait_ge(pe_b, 1)
            nc.vector.tensor_copy(b_r[:].rearrange("p a g -> p (a g)"), ps[:, 6, 0:2 * GROUPS]).then_inc(dve_b, 1)
            dve.wait_ge(pe_v, 1)
            for b in range(0, BATCH, 2):
                nc.vector.tensor_tensor(
                    V[:, b:b + 2, :, :, 0:D0].rearrange("p b h a d -> p (b h) a d"),
                    ps[:, b:b + 2, :].rearrange("p b (h a d) -> p (b h) a d", a=KB, d=D0),
                    spread(b_v[:], 1, [P, 2 * H0, KB, D0]), ALU.add).then_inc(dve_v, 1)
            with dve.Fori(0, BATCH) as b:
                def normalise(j):
                    n = b * J0 + j
                    dve.wait_ge(pe_n, n + 1)
                    nc.vector.reciprocal(inv[:], ps[:, N_BANK, :]).then_inc(dve_r, 1)
                    dve.wait_ge(dve_r, n + 1)
                    nc.vector.tensor_tensor(oT[:], oT[:], inv[:], ALU.mult).then_inc(dve_n, 1)

                for u in range(UNITS + LAG):
                    if u < UNITS:
                        n = b * UNITS + u
                        dve.wait_ge(pe_s, n + 1)
                        if u >= 4:
                            dve.wait_ge(act_e, n - 3)
                        nc.vector.tensor_reduce(neg_max[:, u % 4:u % 4 + 1], ps[:, S_BANKS[u % 3], :], AXX, ALU.max,
                                                negate=True).then_inc(dve_m, 1)
                    if u >= LAG:
                        v_, g, j = u - LAG, (u - LAG) % GROUPS, (u - LAG) // GROUPS
                        dve.wait_ge(pe_t, b * UNITS + v_ + 1)
                        if g == 0 and j:
                            dve.wait_ge(pe_o, b * J0 + j)
                        nc.vector.tensor_copy(pT[:, :, :, g, :],
                                              ps[:, T_BANKS[v_ % 2], :].rearrange("p (a r t) -> p a r t", r=QUADS, t=TOK)
                                              ).then_inc(dve_t, 1)
                        if g == 3 and j:
                            normalise(j - 1)
                normalise(J0 - 1)
                dve.wait_ge(pe_y, b * J0 + J0)
                cols = XT[:, bass.ds(b * SEQ, SEQ)].rearrange("p (t g) -> p g t", g=GROUPS)
                nc.vector.scalar_tensor_tensor(cols, ps[:, Y_BANK, :].rearrange("p (g t) -> p g t", t=TOK), b_o[:, 0:1],
                                               cols, ALU.add, ALU.add).then_inc(dve_y, 1)
            dve.wait_ge(dve_y, BATCH)

        @block.gpsimd
        def _(pool):
            nc.gpsimd.memset(q_diag[:].rearrange("p a g r t -> p (a g r t)"), 0.0).then_inc(cleared, 1)
            pool.wait_ge(cleared, 2)
            pool.wait_ge(act_p, 2 * GROUPS)

            def feed(b, j):
                if j >= 2 or not isinstance(b, int):
                    pool.wait_ge(pe_o, b * J0 + j - 1)
                for r in range(QUADS):
                    nc.gpsimd.tensor_copy(q_diag[32 * r:32 * r + 32, j % 2, :, r, :],
                                          QT[32 * r:32 * r + 32, bass.ds(b * J0 + j, 1), :, :]
                                          .rearrange("p a g t -> p (a g) t")).then_inc(pool_q, 1)
                    pool.wait_ge(pool_q, (b * J0 + j) * QUADS + r + 1)
                pool.wait_ge(dve_v, 2)
                nc.gpsimd.tensor_copy(
                    v_now[:, j % 2, :, :, :].rearrange("p r a d -> p (r a) d"),
                    V[:, bass.ds(b, 1), j * QUADS:(j + 1) * QUADS, :, :].rearrange("p b r a d -> p (b r a) d")
                ).then_inc(pool_in, 1)

            for j in range(J0):
                feed(0, j)
            with pool.Fori(1, BATCH) as b:
                for j in range(J0):
                    feed(b, j)


def mixed_weights(i):
    A = lambda n: np.asarray(i[f"L0_attn_{n}"])
    rows = lambda v: np.broadcast_to(v.reshape(1, -1), (P, v.size))
    w_o = np.zeros((QUADS, 32, J0, DIM), np.float32)
    w_o[:, :D0] = A("wo").T.reshape(J0, QUADS, D0, DIM).transpose(1, 2, 0, 3)
    sel = np.zeros((P, P), np.float32)
    sel[32 * (np.arange(P) // 32) + D0, np.arange(P)] = 1.0
    b_v = np.repeat(A("bv").reshape(KB, QUADS, D0).transpose(1, 0, 2), TOK, axis=0)
    out = {
        "w_in": np.concatenate([A("wq").T, A("wk").T, rows(A("bq")), rows(A("bk"))], 1),
        "cs": np.concatenate([rows(A("rot_cos")[-1]), rows(A("rot_sin")[-1])], 1),
        "w_v": A("wv").T, "b_v": b_v.reshape(P, -1), "a_w_o": w_o.reshape(P, -1), "b_o": A("bo")[:, None], "sel": sel,
    }
    return {k: np.ascontiguousarray(v) for k, v in out.items()}


def sign_weights(i):
    A = lambda n: np.asarray(i[f"L0_ffn_{n}"])
    tall = lambda k: k.reshape(-1, P, k.shape[1]).transpose(1, 0, 2).reshape(P, -1)
    scales = np.stack([A("s0"), A("s1"), A("s2")]).reshape(1, 3)
    out = {"k0": tall(A("k0")), "k1": tall(A("k1")), "k2": tall(A("k2")), "s": np.broadcast_to(scales, (P, 3))}
    return {k: np.ascontiguousarray(v) for k, v in out.items()}


CH, HD = 64, 8
DD = DIM // HD
HQ = 4
NT = TOKENS // P
CHUNKS = SEQ // CH
LEVELS = (2, 4, 8, 16, 32)


def delta_memory(nc, tag, XT, xn, consts, dram):
    ident = consts["ident"]
    NL = len(LEVELS)
    with ExitStack() as ctx:
        def sb(name, shape, dt=F32):
            return ctx.enter_context(nc.sbuf_tensor(f"{tag}_{name}", shape, dt))

        def sem(name):
            return ctx.enter_context(nc.semaphore(f"{tag}_{name}"))

        w_vb = sb("w_vb", [P, DIM + HD])
        w_read = sb("w_read", [P, 2, DIM])
        rate = sb("rate", [P, HD])
        table = sb("table", [P, 4, P])
        levels = sb("levels", [P, 2 + NL, P])
        small = sb("small", [P, 2 + HQ + HQ * DD])
        rateP = sb("rateP", [P, 2])
        beta, nbeta = sb("beta", [P, NT, HD]), sb("nbeta", [P, NT, HD])
        dec_raw = sb("dec_raw", [P, 2, HD])
        dec = sb("dec", [P, 2, HD])
        bdec = sb("bdec", [P, NT, HD])
        total = sb("total", [P, 2])
        L = sb("L", [P, 2, HD, P])
        sums, rinv = sb("sums", [P, NT * HD]), sb("rinv", [P, NT * HD])
        rkT = sb("rkT", [P, 2, BATCH, SEQ + 1])
        wk_dw = sb("wk_dw", [P, NT, HD, 32])
        Vt = sb("Vt", [P, NT, HD, DD])
        U = Vt[:].rearrange("p t h d -> p t (h d)")
        attnT = sb("attnT", [P, NT, HD, P])
        wks = sb("wks", [P, 2, P])
        rws = sb("rws", [P, HD, 32])
        wrk_bd = sb("wrk_bd", [P, 2, 2, HQ, P])
        wk_bd, rk_bd = wrk_bd[:, 0], wrk_bd[:, 1]
        nbL = sb("nbL", [P, 2, HQ, P])
        N_, N_T = nbL, sb("N_T", [P, 2, HQ, P])
        T_, T_T = sb("T_", [P, 2, HQ, P]), sb("T_T", [P, 2, HQ, P])
        M_T, W_ = sb("M_T", [P, 2, HQ, P]), sb("W_", [P, 2, HQ, P])
        S = M_T[:, 0].rearrange("p h q -> p (h q)").rearrange("p (k d) -> p k d", d=HQ * DD)
        S_new = M_T[:, 1].rearrange("p h q -> p (h q)").rearrange("p (k d) -> p k d", d=HQ * DD)
        O = [buf[:].rearrange("p a h q -> p (a h q)").rearrange("p (t h d) -> p t h d", h=HD, d=32)
             for buf in (nbL, N_T, T_, T_T)]
        OT = [wrk_bd[:, i].rearrange("p q h t -> p (q h t)") for i in range(2)]
        flat = attnT[:].rearrange("p t h q -> p (t h q)")
        xtok = flat[:, 0:2048]
        sqs = flat[:, 2048:4096]
        rk_pad = flat[:, 4096:8192].rearrange("p (t h d) -> p t h d", h=HD, d=32)
        Rw = sb("Rw", [P, NT, HD, 32])
        WT = Rw[:].rearrange("p t h d -> p t (h d)").rearrange("p t (q i) -> p t q i", q=2)

        ps = ctx.enter_context(nc.psum_tensor(f"{tag}_ps", [P, 8, 512], F32))
        mk = lambda names: [sem(n) for n in names.split()]
        loaded, cleared, done = mk("loaded cleared done")
        pe_a, act_a, dve_a = mk("pe_a act_a dve_a")
        act_s, act_r, pool_bd, pool_nb, dve_N, pe_nt, act_nt = mk("act_s act_r pool_bd pool_nb dve_N pe_nt act_nt")
        pe_g, pe_at, dve_at, dve_t0, dve_m, dve_i = mk("pe_g pe_at dve_at dve_t0 dve_m dve_i")
        pe_w, act_w, pe_d, dve_t, pe_u, act_u = mk("pe_w act_w pe_d dve_t pe_u act_u")
        pe_ws, dve_vn, pe_su, dve_s, dve_o, dve_tmp = mk("pe_ws dve_vn pe_su dve_s dve_o dve_tmp")
        pe_av, act_ot, pe_y, dve_y = mk("pe_av act_ot pe_y dve_y")
        block = ctx.enter_context(nc.Block())
        row = lambda i: table[:, i, :]

        @block.sync
        def _(sp):
            sp.dma_start(w_read[:].rearrange("p a b -> p (a b)"), dram["w_read"]).then_inc(loaded, 16)
            for dst, name in ((w_vb, "w_vb"), (rate, "rate"), (small, "small"), (rateP, "rateP")):
                sp.dma_start(dst[:], dram[name]).then_inc(loaded, 16)
            sp.dma_start(table[:].rearrange("p a b -> p (a b)"), dram["table"]).then_inc(loaded, 16)
            sp.dma_start(levels[:].rearrange("p a b -> p (a b)"), dram["levels"]).then_inc(loaded, 16)

        heads4 = lambda ap: ap.rearrange("p h q -> p (h q)")

        @block.tensor
        def _(pe):
            for t in range(NT):
                last = nc.tensor.transpose(ps[:, t // 4, (t % 4) * P:(t % 4 + 1) * P], xn[:, t * P:(t + 1) * P], ident[:])
            last.then_inc(pe_a, 1)
            pe.wait_ge(loaded, 7 * 16)
            for t in range(NT):
                last = nc.tensor.matmul(ps[:, 7, t * HD:(t + 1) * HD], xn[:, t * P:(t + 1) * P], w_vb[:, DIM:],
                                        start=True, stop=True, skip_group_check=True)
            last.then_inc(pe_a, 1)
            pe.wait_ge(act_a, 2)
            for t in range(NT):
                last = nc.tensor.matmul(ps[:, t // 4, (t % 4) * P:(t % 4 + 1) * P], xn[:, t * P:(t + 1) * P], w_vb[:, 0:DIM],
                                        start=True, stop=True, skip_group_check=True)
            last.then_inc(pe_a, 1)
            pe.wait_ge(dve_a, 2)
            pe.wait_ge(dve_tmp, 6)
            for q in range(2):
                for t in range(NT):
                    last = nc.tensor.transpose(ps[:, q * 4 + t // 4, (t % 4) * P:(t % 4 + 1) * P],
                                               rk_pad[:, t, q * HQ:(q + 1) * HQ, :].rearrange("p h d -> p (h d)"), ident[:])
            last.then_inc(pe_a, 1)
            pe.wait_ge(act_a, 6)
            for t in range(NT):
                for q in range(2):
                    last = nc.tensor.transpose(ps[:, t // 2, (t % 2) * 256 + q * P:(t % 2) * 256 + (q + 1) * P],
                                               rkT[:, q, t // TILES, (t % TILES) * P:(t % TILES + 1) * P], ident[:])
            last.then_inc(pe_a, 1)
            pe.wait_ge(dve_a, 4)

            def wk_products(n):
                for q in range(2):
                    pe.wait_ge(act_s, n + 1)
                    pe.wait_ge(pool_bd, n * 4 + 2 * q + 1)
                    nc.tensor.matmul(ps[:, 4 * q, :], wks[:, q, :], heads4(wk_bd[:, q]), start=True, stop=True).then_inc(pe_g, 1)

            def transposes(n):
                for q in range(2):
                    pe.wait_ge(dve_N, n * 2 + q + 1)
                    for h in range(HQ):
                        last = nc.tensor.transpose(ps[:, 4 * q + 2, h * P:(h + 1) * P], N_[:, q, h, :], ident[:])
                    last.then_inc(pe_nt, 1)

            def rk_products(n):
                for q in range(2):
                    pe.wait_ge(pool_bd, n * 4 + 2 * q + 2)
                    nc.tensor.matmul(ps[:, 4 * q + 1, :], wks[:, q, :], heads4(rk_bd[:, q]), start=True,
                                     stop=True).then_inc(pe_at, 1)

            def solve(n, more):
                for l in range(NL):
                    at = lambda q: (n * NL + l) * 2 + q + 1
                    for q in range(2):
                        pe.wait_ge(dve_m, at(q))
                        pe.wait_ge(dve_t0, n * 2 + q + 1)
                        if l:
                            pe.wait_ge(dve_t, at(q) - 2)
                        for h in range(HQ):
                            last = nc.tensor.matmul(ps[:, 4 * q + 2, h * P:(h + 1) * P], M_T[:, q, h, :], T_[:, q, h, :],
                                                    start=True, stop=True, skip_group_check=True)
                        last.then_inc(pe_w, 1)
                    if more and l == NL - 1:
                        wk_products(n + 1)
                    for q in range(2):
                        pe.wait_ge(act_w, at(q))
                        if l == 0:
                            pe.wait_ge(dve_at, n * 2 + q + 1)
                        for h in range(HQ):
                            cols = slice(h * P, (h + 1) * P)
                            if l < NL - 1:
                                nc.tensor.matmul(ps[:, 4 * q, cols], T_T[:, q, h, :], W_[:, q, h, :],
                                                 start=True, stop=True, skip_group_check=True)
                            last = nc.tensor.matmul(ps[:, 4 * q + 1, cols], W_[:, q, h, :], T_T[:, q, h, :],
                                                    start=True, stop=True, skip_group_check=True)
                        last.then_inc(pe_d, 1)
                if more:
                    transposes(n + 1)
                pe.wait_ge(act_r, n + 1)
                for q in range(2):
                    pe.wait_ge(dve_t, (n * NL + NL - 1) * 2 + q + 1)
                    for h in range(HQ):
                        nc.tensor.matmul(ps[:, 4 * q + 3, h * DD:(h + 1) * DD], T_T[:, q, h, :],
                                         Vt[:, bass.ds(n, 1), q * HQ + h, :].rearrange("p a d -> p (a d)"),
                                         start=True, stop=True, skip_group_check=True)
                    for h in range(HQ):
                        last = nc.tensor.matmul(ps[32 * h:32 * h + 32, 4 * q + 3, P:2 * P], rws[:, q * HQ + h, :],
                                                T_T[:, q, h, :], start=True, stop=True, skip_group_check=True)
                    last.then_inc(pe_u, 1)
                if more:
                    rk_products(n + 1)

            wk_products(0)
            transposes(0)
            rk_products(0)
            with pe.Fori(0, NT - 1) as n:
                solve(n, True)
            solve(NT - 1, False)

            pe.wait_ge(act_u, 4 * NT)
            for c in range(CHUNKS):
                r = slice(CH * (c % 2), CH * (c % 2) + CH)
                if c:
                    pe.wait_ge(dve_s, c)
                    for b in range(BATCH):
                        for q in range(2):
                            k = 2 * b + q
                            cols = slice(k * HQ * DD, (k + 1) * HQ * DD)
                            nc.tensor.matmul(ps[r, c % 2, cols], WT[:, b * TILES + c // 2, q, r], S[:, k, :],
                                             start=True, stop=True, skip_group_check=True)
                            last = nc.tensor.matmul(ps[r, 2 + c % 2, cols], rkT[:, q, b, 1 + c * CH:1 + (c + 1) * CH],
                                                    S[:, k, :], start=True, stop=True, skip_group_check=True)
                    last.then_inc(pe_ws, 1)
                    pe.wait_ge(dve_vn, c)
                if c < CHUNKS - 1:
                    for b in range(BATCH):
                        for q in range(2):
                            k = 2 * b + q
                            last = nc.tensor.matmul(ps[:, 4, k * HQ * DD:(k + 1) * HQ * DD],
                                                    wk_dw[r, b * TILES + c // 2, q * HQ:(q + 1) * HQ, :].rearrange("p h d -> p (h d)"),
                                                    U[r, b * TILES + c // 2, q * HQ * DD:(q + 1) * HQ * DD],
                                                    start=True, stop=True, skip_group_check=True)
                    last.then_inc(pe_su, 1)
            pe.wait_ge(dve_o, CHUNKS - 1)
            def outputs(g):
                if g >= 2:
                    pe.wait_ge(act_ot, g - 1)
                for q in range(2):
                    for t in range(TILES):
                        bank, cols, n = 2 * (g % 2) + q, slice(t * P, (t + 1) * P), g * TILES + t
                        nc.tensor.matmul(ps[:, bank, cols], O[g][:, t, q * HQ:(q + 1) * HQ, :].rearrange("p h d -> p (h d)"),
                                         ident[:], start=True, stop=False, skip_group_check=True)
                        for h in range(HQ):
                            k = q * HQ + h
                            last = nc.tensor.matmul(ps[32 * h:32 * h + DD, bank, cols], U[:, n, k * DD:(k + 1) * DD],
                                                    attnT[:, n, k, :], start=False, stop=True, skip_group_check=True)
                last.then_inc(pe_av, 1)

            outputs(0)
            for g in range(BATCH):
                if g + 1 < BATCH:
                    outputs(g + 1)
                pe.wait_ge(act_ot, g + 1)
                if g >= 2:
                    pe.wait_ge(dve_y, g - 1)
                for q in range(2):
                    last = nc.tensor.matmul(ps[:, 6 + g % 2, :], w_read[:, q, :], OT[g % 2][:, q * SEQ:(q + 1) * SEQ],
                                            start=q == 0, stop=q == 1)
                last.then_inc(pe_y, 1)

        @block.scalar
        def _(act):
            act.wait_ge(loaded, 7 * 16)
            act.wait_ge(pe_a, 1)
            nc.scalar.activation(sqs, ps[:, 0:4, :].rearrange("p a b -> p (a b)"), ACT.Square).then_inc(act_a, 1)
            nc.scalar.activation(xtok, ps[:, 0:4, :].rearrange("p a b -> p (a b)"), ACT.Copy).then_inc(act_a, 1)
            act.wait_ge(dve_a, 1)
            nc.scalar.activation(sums[:], sums[:], ACT.Sqrt).then_inc(act_a, 1)
            act.wait_ge(pe_a, 2)
            nc.scalar.activation(beta[:].rearrange("p t h -> p (t h)"), ps[:, 7, 0:NT * HD], ACT.Sigmoid).then_inc(act_a, 1)
            nc.scalar.activation(rate[:], rate[:], ACT.Sigmoid).then_inc(done, 1)
            nc.scalar.activation(rateP[:], rateP[:], ACT.Sigmoid).then_inc(done, 1)
            act.wait_ge(done, 2)
            nc.scalar.activation(rate[:], rate[:], ACT.Ln).then_inc(done, 1)
            nc.scalar.activation(rateP[:], rateP[:], ACT.Ln).then_inc(done, 1)
            act.wait_ge(done, 4)
            for k in range(2):
                for h in range(HD):
                    nc.scalar.activation(L[:, k, h, :], row(k), ACT.Exp, scale=rate[:, h:h + 1]).then_inc(done, 1)
            nc.scalar.activation(total[:], rateP[:], ACT.Exp, scale=float(CH)).then_inc(act_a, 1)
            act.wait_ge(dve_a, 3)
            nc.scalar.activation(dec[:].rearrange("p a h -> p (a h)"), dec_raw[:].rearrange("p a h -> p (a h)"),
                                 ACT.Exp).then_inc(done, 1)
            act.wait_ge(pe_a, 4)
            act.wait_ge(cleared, 2)
            for q in range(2):
                last = nc.scalar.activation(rkT[:, q, :, 1:SEQ + 1], ps[:, 4 * q:4 * q + 4, :], ACT.Copy)
            last.then_inc(act_a, 1)
            def take_wk(b, t):
                n = b * TILES + t
                if t or not isinstance(b, int) or b:
                    act.wait_ge(pe_at, 2 * n)
                nc.scalar.activation(wks[:], rkT[:, :, bass.ds(b, 1), t * P:(t + 1) * P]
                                     .rearrange("p q a t -> p (q a) t"), ACT.Copy).then_inc(act_s, 1)

            def take_N_T(n):
                for q in range(2):
                    act.wait_ge(pe_nt, n * 2 + q + 1)
                    nc.scalar.activation(heads4(N_T[:, q]), ps[:, 4 * q + 2, :], ACT.Copy).then_inc(act_nt, 1)

            def take_right_sides(n):
                nc.scalar.activation(rws[:].rearrange("p h d -> p (h d)"), Rw[:, bass.ds(n, 1), :, :]
                                     .rearrange("p a h d -> p (a h d)"), ACT.Copy).then_inc(act_r, 1)

            def solve(b, t):
                n = b * TILES + t
                more = not isinstance(b, int) or n + 1 < NT
                for l in range(NL):
                    if more and l == NL - 1:
                        take_wk(*((b, t + 1) if t + 1 < TILES else (b + 1, 0)))
                    for q in range(2):
                        act.wait_ge(pe_w, (n * NL + l) * 2 + q + 1)
                        nc.scalar.activation(heads4(W_[:, q]), ps[:, 4 * q + 2, :], ACT.Copy).then_inc(act_w, 1)
                if more:
                    take_N_T(n + 1)
                for q in range(2):
                    act.wait_ge(pe_u, n * 2 + q + 1)
                    nc.scalar.activation(U[:, bass.ds(n, 1), q * 64:(q + 1) * 64].rearrange("p a d -> p (a d)"),
                                         ps[:, 4 * q + 3, 0:64], ACT.Copy).then_inc(act_u, 1)
                    nc.scalar.activation(WT[:, bass.ds(n, 1), q, :].rearrange("p a d -> p (a d)"),
                                         ps[:, 4 * q + 3, P:2 * P], ACT.Copy).then_inc(act_u, 1)
                if more:
                    take_right_sides(n + 1)

            act.wait_ge(dve_a, 4)
            take_wk(0, 0)
            take_N_T(0)
            take_right_sides(0)
            with act.Fori(0, BATCH - 1) as b:
                for t in range(TILES):
                    solve(b, t)
            for t in range(TILES):
                solve(BATCH - 1, t)
            for g in range(BATCH):
                act.wait_ge(pe_av, g + 1)
                if g >= 2:
                    act.wait_ge(pe_y, g - 1)
                nc.scalar.activation(OT[g % 2], ps[:, 2 * (g % 2):2 * (g % 2) + 2, :].rearrange("p a b -> p (a b)"),
                                     ACT.Copy).then_inc(act_ot, 1)

        @block.vector
        def _(dve):
            nc.vector.memset(rkT[:].rearrange("p q b t -> p (q b) t")[:, :, 0:1], 0.0)
            nc.vector.memset(rk_pad, 0.0).then_inc(cleared, 1)
            dve.wait_ge(act_a, 1)
            nc.vector.reduce_sum(sums[:], sqs.rearrange("p (g d) -> p g d", d=DD), AXX).then_inc(dve_a, 1)
            dve.wait_ge(act_a, 3)
            nc.vector.tensor_scalar_max(sums[:], sums[:], 1e-12).then_inc(dve_tmp, 1)
            dve.wait_ge(dve_tmp, 1)
            nc.vector.reciprocal(rinv[:], sums[:]).then_inc(dve_tmp, 1)
            dve.wait_ge(dve_tmp, 2)
            dve.wait_ge(cleared, 2)
            nc.vector.tensor_tensor(rk_pad[:, :, :, 0:DD].rearrange("p t h d -> p (t h) d"),
                                    xtok.rearrange("p (g d) -> p g d", d=DD),
                                    spread(rinv[:], 2, [P, NT * HD, DD]), ALU.mult).then_inc(dve_a, 1)
            dve.wait_ge(done, 4)
            for k in range(2):
                last = nc.vector.tensor_scalar(dec_raw[:, k, :], rate[:], small[:, k:k + 1], None, ALU.mult)
            last.then_inc(dve_a, 1)
            dve.wait_ge(done, 4 + 2 * HD)
            for k in range(2):
                nc.vector.tensor_tensor(L[:, k, :, :], L[:, k, :, :], spread(row(2 + k), 1, [P, HD, P]),
                                        ALU.mult).then_inc(dve_tmp, 1)
            dve.wait_ge(act_a, 4)
            nc.vector.tensor_scalar(nbeta[:], beta[:], -1.0, None, ALU.mult).then_inc(dve_tmp, 1)
            dve.wait_ge(pe_a, 3)
            nc.vector.tensor_tensor(Vt[:].rearrange("p t h d -> p (t h) d"),
                                    ps[:, 0:4, :].rearrange("p a (g d) -> p (a g) d", d=DD),
                                    spread(beta[:].rearrange("p t h -> p (t h)"), 2, [P, NT * HD, DD]),
                                    ALU.mult).then_inc(dve_tmp, 1)
            dve.wait_ge(done, 5 + 2 * HD)
            nc.vector.tensor_tensor(bdec[:], beta[:], spread(dec[:, 0, :], 1, [P, NT, HD]), ALU.mult).then_inc(dve_tmp, 1)
            dve.wait_ge(dve_tmp, 7)
            dve.wait_ge(pe_a, 5)
            wk = ps[:, :, :].rearrange("p a (t h d) -> p (a t) h d", h=HD, d=32)
            for t in range(NT):
                nc.vector.tensor_tensor(wk_dw[:, t], wk[:, t], spread(dec[:, 1, :], 2, [P, HD, 32]), ALU.mult)
                last = nc.vector.tensor_tensor(Rw[:, t], wk[:, t], spread(bdec[:, t, :], 2, [P, HD, 32]), ALU.mult)
            last.then_inc(dve_a, 1)
            def mask_level(n, l, q, again):
                if again:
                    dve.wait_ge(pe_w, (n * NL + l - 1) * 2 + q + 1)
                nc.vector.tensor_tensor(M_T[:, q], N_T[:, q], spread(levels[:, 2 + l, :], 1, [P, HQ, P]),
                                        ALU.mult).then_inc(dve_m, 1)

            def form_N(n):
                for q in range(2):
                    dve.wait_ge(pe_g, n * 2 + q + 1)
                    dve.wait_ge(pool_nb, n * 2 + q + 1)
                    nc.vector.tensor_tensor(heads4(N_[:, q]), ps[:, 4 * q, :], heads4(nbL[:, q]), ALU.mult).then_inc(dve_N, 1)

            def prepare(n, again):
                for q in range(2):
                    dve.wait_ge(dve_N, n * 2 + q + 1)
                    if again:
                        dve.wait_ge(pe_u, 2 * n + q - 1)
                    nc.vector.tensor_tensor(T_[:, q], N_[:, q], spread(levels[:, 0, :], 1, [P, HQ, P]),
                                            ALU.mult).then_inc(dve_i, 1)
                    dve.wait_ge(act_nt, n * 2 + q + 1)
                    nc.vector.tensor_tensor(T_T[:, q], N_T[:, q], spread(levels[:, 1, :], 1, [P, HQ, P]),
                                            ALU.mult).then_inc(dve_i, 1)
                    mask_level(n, 0, q, again)
                    dve.wait_ge(dve_i, (n * 2 + q) * 2 + 2)
                    nc.vector.tensor_tensor(T_[:, q], T_[:, q], spread(ident[:], 1, [P, HQ, P]), ALU.add)
                    nc.vector.tensor_tensor(T_T[:, q], T_T[:, q], spread(ident[:], 1, [P, HQ, P]),
                                            ALU.add).then_inc(dve_t0, 1)
                for q in range(2):
                    dve.wait_ge(pe_at, n * 2 + q + 1)
                    nc.vector.tensor_tensor(attnT[:, bass.ds(n, 1), q * HQ:(q + 1) * HQ, :].rearrange("p a h t -> p (a h t)"),
                                            ps[:, 4 * q + 1, :], heads4(L[:, 1, q * HQ:(q + 1) * HQ, :]),
                                            ALU.mult).then_inc(dve_at, 1)

            def solve(n, more):
                for l in range(NL):
                    for q in range(2) if l < NL - 1 else ():
                        mask_level(n, l + 1, q, True)
                    if more and l == NL - 1:
                        form_N(n + 1)
                    for q in range(2):
                        dve.wait_ge(pe_d, (n * NL + l) * 2 + q + 1)
                        if l < NL - 1:
                            nc.vector.tensor_tensor(heads4(T_[:, q]), heads4(T_[:, q]), ps[:, 4 * q, :], ALU.add)
                        nc.vector.tensor_tensor(heads4(T_T[:, q]), heads4(T_T[:, q]), ps[:, 4 * q + 1, :],
                                                ALU.add).then_inc(dve_t, 1)
                if more:
                    prepare(n + 1, True)

            form_N(0)
            prepare(0, False)
            with dve.Fori(0, NT - 1) as n:
                solve(n, True)
            solve(NT - 1, False)
            dve.wait_ge(act_u, 4 * NT)
            dve.wait_ge(cleared, 3)
            tiles = lambda ap, c: ap.rearrange("p (b t) d -> p b t d", t=TILES)[CH * (c % 2):CH * (c % 2) + CH, :, c // 2, :]
            blocks = spread(small[:, 2 + HQ:], 1, [P, 2 * BATCH, HQ * DD])
            for c in range(CHUNKS):
                r = slice(CH * (c % 2), CH * (c % 2) + CH)
                if c:
                    dve.wait_ge(pe_ws, c)
                    nc.vector.tensor_tensor(tiles(U, c), tiles(U, c), ps[r, c % 2, :].rearrange("p (b d) -> p b d", b=BATCH),
                                            ALU.subtract).then_inc(dve_vn, 1)
                    for b in range(BATCH):
                        last = nc.vector.tensor_tensor(
                            O[b][r, c // 2, :, 0:DD],
                            ps[r, 2 + c % 2, b * P:(b + 1) * P].rearrange("p (h d) -> p h d", d=DD),
                            spread(dec[r, 0, :], 2, [CH, HD, DD]), ALU.mult)
                    last.then_inc(dve_o, 1)
                if c < CHUNKS - 1:
                    dve.wait_ge(pe_su, c + 1)
                    if c:
                        nc.vector.tensor_tensor(S_new, ps[:, 4, :].rearrange("p (k d) -> p k d", d=HQ * DD), blocks,
                                                ALU.mult).then_inc(dve_tmp, 1)
                        dve.wait_ge(dve_tmp, 7 + c)
                        for q in range(2):
                            last = nc.vector.scalar_tensor_tensor(S[:, q::2, :], S[:, q::2, :], total[:, q:q + 1],
                                                                  S_new[:, q::2, :], ALU.mult, ALU.add)
                        last.then_inc(dve_s, 1)
                    else:
                        nc.vector.tensor_tensor(S, ps[:, 4, :].rearrange("p (k d) -> p k d", d=HQ * DD), blocks,
                                                ALU.mult).then_inc(dve_s, 1)
            for g in range(BATCH):
                dve.wait_ge(pe_y, g + 1)
                cols = slice(g * SEQ, (g + 1) * SEQ)
                nc.vector.tensor_tensor(XT[:, cols], XT[:, cols], ps[:, 6 + g % 2, :], ALU.add).then_inc(dve_y, 1)
                dve.wait_ge(dve_y, g + 1)
                nc.vector.tensor_tensor(XT[:, cols], XT[:, cols], xn[:, cols], ALU.add).then_inc(dve_tmp, 1)
            dve.wait_ge(dve_tmp, 7 + CHUNKS - 2 + BATCH)

        @block.gpsimd
        def _(pool):
            nc.gpsimd.memset(wks[:], 0.0).then_inc(cleared, 1)
            pool.wait_ge(dve_a, 4)
            half_mask = small[:, 2:2 + HQ]

            def build(b, t):
                n = b * TILES + t
                again = t or not isinstance(b, int)
                for q in range(2):
                    src = [rkT[:, q, bass.ds(b, 1), t * P + off:(t + 1) * P + off].rearrange("p a t -> p (a t)")
                           for off in range(2)]
                    if again:
                        pool.wait_ge(pe_g, 2 * n + q - 1)
                    nc.gpsimd.tensor_tensor(wk_bd[:, q], spread(src[0], 1, [P, HQ, P]), spread(half_mask, 2, [P, HQ, P]),
                                            ALU.mult).then_inc(pool_bd, 1)
                    if again:
                        pool.wait_ge(pe_at, 2 * n + q - 1)
                    nc.gpsimd.tensor_tensor(rk_bd[:, q], spread(src[1], 1, [P, HQ, P]), spread(half_mask, 2, [P, HQ, P]),
                                            ALU.mult).then_inc(pool_bd, 1)
                for q in range(2):
                    if again:
                        pool.wait_ge(dve_t0, 2 * n + q - 1)
                    nc.gpsimd.tensor_tensor(nbL[:, q], L[:, 0, q * HQ:(q + 1) * HQ, :],
                                            spread(nbeta[:, bass.ds(n, 1), q * HQ:(q + 1) * HQ]
                                                   .rearrange("p a h -> p (a h)"), 2, [P, HQ, P]),
                                            ALU.mult).then_inc(pool_nb, 1)

            for t in range(TILES):
                build(0, t)
            with pool.Fori(1, BATCH) as b:
                for t in range(TILES):
                    build(b, t)
            pool.wait_ge(act_u, 4 * NT)
            for part in O:
                last = nc.gpsimd.memset(part, 0.0)
            last.then_inc(cleared, 1)


def delta_weights(i):
    A = lambda n: np.asarray(i[f"L1_attn_{n}"])
    p = np.arange(P)
    pos, chunk = p % CH, p // CH
    same = chunk[:, None] == chunk[None, :]
    d = (pos[:, None] - pos[None, :]).astype(np.float32)
    low, strict = same & (d >= 0), same & (d > 0)
    table = [np.where(strict, d, 0), np.where(low, d, 0).T, strict, low.T]

    def level(s):
        return same & (pos[:, None] // (2 * s) == pos[None, :] // (2 * s)) \
            & (pos[:, None] // s % 2 == 1) & (pos[None, :] // s % 2 == 0)
    levels = [level(1), level(1).T] + [level(s).T for s in LEVELS]
    head = p // 32
    small = [pos[:, None] + 1, CH - 1 - pos[:, None], head[:, None] == np.arange(HQ)[None, :],
             head[:, None] == (np.arange(HQ * DD) // DD)[None, :]]
    f = lambda parts: np.concatenate([np.asarray(x, np.float32) for x in parts], 1)
    decay = A("decay")
    w_read = np.zeros((2, HQ, 32, DIM), np.float32)
    w_read[:, :, :DD] = A("W_read").T.reshape(2, HQ, DD, DIM)
    out = {
        "w_vb": np.concatenate([A("W_write").T, A("W_beta").T], 1), "w_read": w_read.transpose(1, 2, 0, 3).reshape(P, -1),
        "rate": np.broadcast_to(decay[None], (P, HD)), "rateP": decay.reshape(2, HQ).T[head],
        "table": f(table), "levels": f(levels), "small": f(small),
    }
    return {k: np.ascontiguousarray(v) for k, v in out.items()}


def half_sum(nc, run, added, XT, ZT):
    with nc.Block() as block:
        @block.vector
        def _(dve):
            nc.vector.scalar_tensor_tensor(XT[:], ZT[:, 0:TOKENS], 0.5, XT[:], ALU.mult, ALU.add).then_inc(added, 1)
            dve.wait_ge(added, run + 1)


def build(nc, dram, out):
    with ExitStack() as ctx:
        def sb(name, shape, dt=F32):
            return ctx.enter_context(nc.sbuf_tensor(name, shape, dt))

        XT, ZT = sb("XT", [P, TOKENS]), sb("ZT", [P, TOKENS + P])
        ident, ident_b, mean_w = sb("ident", [P, P]), sb("ident_b", [P, P], BF16), sb("mean_w", [P, P])
        mask_in, mask = sb("mask_in", [P, 2, KEYS]), sb("mask", [P, 2, KEYS], BF16)
        eps, one = sb("eps", [P, 1]), sb("one", [P, 1])
        loaded, ready, stored, added = [
            ctx.enter_context(nc.semaphore(n)) for n in ("loaded", "ready", "stored", "added")]
        norm_sems, sign_sems, window_sems = [Semaphores(nc, ctx, s) for s in ("norm", "sign", "window")]

        with nc.Block() as block:
            @block.sync
            def _(sp):
                sp.dma_start(XT[:], dram["x"]).then_inc(loaded, 16)
                sp.dma_start(ident[:], dram["ident"]).then_inc(loaded, 16)
                sp.dma_start(mask_in[:].rearrange("p a k -> p (a k)"), dram["mask"]).then_inc(loaded, 16)

            @block.vector
            def _(dve):
                nc.vector.memset(mean_w[:], 1.0 / DIM).then_inc(ready, 1)
                nc.vector.memset(eps[:], EPS).then_inc(ready, 1)
                nc.vector.memset(one[:], 1.0).then_inc(ready, 1)
                nc.vector.memset(ZT[:, TOKENS:], 0.0).then_inc(ready, 1)
                dve.wait_ge(loaded, 3 * 16)
                nc.vector.tensor_copy(ident_b[:], ident[:]).then_inc(ready, 1)
                nc.vector.tensor_copy(mask[:], mask_in[:]).then_inc(ready, 1)
                dve.wait_ge(ready, 6)

        consts = dict(ident=ident, ident_b=ident_b, mean_w=mean_w, mask=mask, eps=eps, one=one)
        layer_norm(nc, 0, norm_sems, XT, ZT, consts)
        sign_ffn(nc, 0, sign_sems, XT, ZT, dram)
        layer_norm(nc, 1, norm_sems, XT, ZT, consts)
        mixed_attention(nc, "a0", XT, ZT, consts, dram)
        layer_norm(nc, 2, norm_sems, XT, ZT, consts)
        sign_ffn(nc, 1, sign_sems, XT, ZT, dram)
        layer_norm(nc, 3, norm_sems, XT, ZT, consts)
        windowed_layers(nc, 0, window_sems, ZT, consts, dram)
        half_sum(nc, 0, added, XT, ZT)
        layer_norm(nc, 4, norm_sems, XT, ZT, consts)
        delta_memory(nc, "a1", XT, ZT, consts, dram)
        layer_norm(nc, 5, norm_sems, XT, ZT, consts)
        windowed_layers(nc, 1, window_sems, ZT, consts, dram)
        half_sum(nc, 1, added, XT, ZT)

        with nc.Block() as block:
            @block.sync
            def _(sp):
                sp.dma_start(out, XT[:]).then_inc(stored, 16)
                sp.wait_ge(stored, 16)


def kernel(**inputs):
    import concourse.bacc as bacc
    from concourse.bass_utils import run_bass_kernel_spmd as run

    arrays = {"x": np.ascontiguousarray(np.asarray(inputs["L0_attn_x"]).reshape(TOKENS, DIM).T),
              "ident": np.eye(P, dtype=np.float32), "mask": window_mask(), "rot": rotary_tables()}
    for part in (sign_weights, mixed_weights, delta_weights, layer_weights):
        arrays.update(part(inputs))
    nc = bacc.Bacc("TRN2", target_bir_lowering=False, num_devices=1)
    dram = {name: nc.dram_tensor(f"in_{name}", a.shape, mybir.dt.from_np(a.dtype), kind="ExternalInput").ap()
            for name, a in arrays.items()}
    out = nc.dram_tensor("out", (DIM, TOKENS), F32, kind="ExternalOutput").ap()
    build(nc, dram, out)
    result = run(nc, [{f"in_{name}": a for name, a in arrays.items()}], core_ids=[0]).results[0]["out"]
    return np.ascontiguousarray(result.T).reshape(BATCH, SEQ, DIM)
```
